# Optimizing a Trainium2 kernel written in Bass

```python
import numpy as np
import jax
import jax.numpy as jnp

def _softmax(x, axis=-1):
    return jax.nn.softmax(x, axis=axis)

def _gelu(x):
    return jax.nn.gelu(x, approximate=True)

def _silu(x):
    return jax.nn.silu(x)

def _sigmoid(x):
    return jax.nn.sigmoid(x)

def _layernorm(x, axis=-1, eps=1e-05):
    m = jnp.mean(x, axis=axis, keepdims=True)
    v = jnp.var(x, axis=axis, keepdims=True)
    return (x - m) / jnp.sqrt(v + eps)

def _scatter_add(tgt, idx, src, axis=0):
    return tgt.at[idx].add(src)

def _segment_sum(src, seg, n):
    return jax.ops.segment_sum(src, seg, n)
kernel_name = 'mk_seq_postln_d2_jaxref_r8_ac445e'

def setup_inputs(seed: int=0):
    np.random.seed(seed)
    _w = jnp.asarray

    def _L0_attn_setup():
        import jax, jax.numpy as jnp
        import numpy as np
        MIN_TIMESCALE = 1.0
        MAX_TIMESCALE = 10000.0

        def llama_rope(x):
            B, S, N, H = x.shape
            half = H // 2
            fraction = 2.0 * jnp.arange(0, half, dtype=jnp.float32) / H
            timescale = MIN_TIMESCALE * (MAX_TIMESCALE / MIN_TIMESCALE) ** fraction
            position = jnp.arange(S, dtype=jnp.float32)[None, :, None, None]
            sinusoid = position / timescale[None, None, None, :]
            sin, cos = (jnp.sin(sinusoid), jnp.cos(sinusoid))
            xr = x.astype(jnp.float32).reshape(B, S, N, half, 2)
            x1, x2 = (xr[..., 0], xr[..., 1])
            r1 = x1 * cos - x2 * sin
            r2 = x2 * cos + x1 * sin
            out = jnp.stack((r1, r2), axis=-1).reshape(B, S, N, H)
            return out.astype(x.dtype)
        key = jax.random.key(seed)
        kx, kq, kk, kv, ko = jax.random.split(key, 5)
        B, S, D, N, H = (4, 256, 256, 16, 128)
        x = jax.random.normal(kx, (B, S, D), dtype=jnp.float32)
        wq = jax.random.normal(kq, (D, N, H), dtype=jnp.float32) / np.sqrt(D)
        wk = jax.random.normal(kk, (D, N, H), dtype=jnp.float32) / np.sqrt(D)
        wv = jax.random.normal(kv, (D, N, H), dtype=jnp.float32) / np.sqrt(D)
        wo = jax.random.normal(ko, (N, H, D), dtype=jnp.float32) / np.sqrt(N * H)
        return {'x': x, 'wq': wq, 'wk': wk, 'wv': wv, 'wo': wo}
    _L0_attn_in = _L0_attn_setup()

    def _L0_ffn_setup():
        import jax, jax.numpy as jnp
        import numpy as np
        EPS = 1e-07
        CURVATURE = 1.0
        MAX_NORM_RATIO = 0.99
        B, L, N, K = (4, 256, 256, 256)

        def _ternary_init(key, n, k):
            rand = jax.random.normal(key, (n, k), dtype=jnp.float32)
            threshold = 0.5 * jnp.mean(jnp.abs(rand))
            return jnp.where(rand > threshold, 1.0, jnp.where(rand < -threshold, -1.0, 0.0)).astype(jnp.float32)
        key = jax.random.key(seed)
        kx, kw = jax.random.split(key)
        x = jax.random.normal(kx, (B, L, N), dtype=jnp.float32)
        weight = _ternary_init(kw, N, K)
        scale = jnp.full((K,), 1.0 / np.sqrt(N), dtype=jnp.float32)
        return {'x': x, 'weight': weight, 'scale': scale}
    _L0_ffn_in = _L0_ffn_setup()

    def _L1_attn_setup():
        import jax, jax.numpy as jnp
        import numpy as np
        HQ, HKV, HD, WIN = (16, 4, 128, 64)

        def _sliding_window_attention(q, k, v, win):
            B, H, S, hd = q.shape
            W = win
            nb = S // W
            qb = q.reshape(B, H, nb, W, hd)
            kpad = jnp.pad(k, ((0, 0), (0, 0), (W, 0), (0, 0)))
            vpad = jnp.pad(v, ((0, 0), (0, 0), (W, 0), (0, 0)))
            kb = jnp.concatenate([kpad[:, :, :S].reshape(B, H, nb, W, hd), k.reshape(B, H, nb, W, hd)], axis=3)
            vb = jnp.concatenate([vpad[:, :, :S].reshape(B, H, nb, W, hd), v.reshape(B, H, nb, W, hd)], axis=3)
            scores = jnp.einsum('bhnqd,bhnkd->bhnqk', qb, kb) / jnp.asarray(hd, qb.dtype)
            qi = jnp.arange(W)[:, None]
            ki = jnp.arange(2 * W)[None, :]
            band = (ki >= qi + 1) & (ki <= qi + W)
            blk = jnp.arange(nb)[:, None, None]
            valid = band[None] & ((blk > 0) | (ki[None] >= W))
            neg = jnp.finfo(scores.dtype).min
            scores = jnp.where(valid[None, None], scores, neg)
            probs = jax.nn.softmax(scores, axis=-1)
            out = jnp.einsum('bhnqk,bhnkd->bhnqd', probs, vb)
            return out.reshape(B, H, S, hd)
        key = jax.random.key(seed)
        k0, k1, k2, k3, k4 = jax.random.split(key, 5)
        B, S, D = (1, 1024, 256)
        std = 0.02
        hidden_states = jax.random.normal(k0, (B, S, D), jnp.float32)
        Wq = jax.random.normal(k1, (D, HQ * HD), jnp.float32) * std
        Wk = jax.random.normal(k2, (D, HKV * HD), jnp.float32) * std
        Wv = jax.random.normal(k3, (D, HKV * HD), jnp.float32) * std
        Wo = jax.random.normal(k4, (HQ * HD, D), jnp.float32) * std
        return {'hidden_states': hidden_states, 'Wq': Wq, 'Wk': Wk, 'Wv': Wv, 'Wo': Wo}
    _L1_attn_in = _L1_attn_setup()

    def _L1_ffn_setup():
        import jax, jax.numpy as jnp
        import numpy as np
        B, S, H = (1, 256, 256)
        E, K, I = (16, 4, 176)
        IS = 352
        CAP = 128
        key = jax.random.key(seed)
        ks = jax.random.split(key, 8)
        sc = 0.02
        return {'hidden_states': jax.random.normal(ks[0], (B, S, H), jnp.float32), 'gate_w': jax.random.normal(ks[1], (E, H), jnp.float32) * sc, 'w_gate': jax.random.normal(ks[2], (E, H, I), jnp.float32) * sc, 'w_up': jax.random.normal(ks[3], (E, H, I), jnp.float32) * sc, 'w_down': jax.random.normal(ks[4], (E, I, H), jnp.float32) * sc, 'sw_gate': jax.random.normal(ks[5], (H, IS), jnp.float32) * sc, 'sw_up': jax.random.normal(ks[6], (H, IS), jnp.float32) * sc, 'sw_down': jax.random.normal(ks[7], (IS, H), jnp.float32) * sc}
    _L1_ffn_in = _L1_ffn_setup()
    _d = {'L0_attn_x': _L0_attn_in['x'], 'L0_attn_wq': _L0_attn_in['wq'], 'L0_attn_wk': _L0_attn_in['wk'], 'L0_attn_wv': _L0_attn_in['wv'], 'L0_attn_wo': _L0_attn_in['wo'], 'L0_ffn_weight': _L0_ffn_in['weight'], 'L0_ffn_scale': _L0_ffn_in['scale'], 'L1_attn_Wq': _L1_attn_in['Wq'], 'L1_attn_Wk': _L1_attn_in['Wk'], 'L1_attn_Wv': _L1_attn_in['Wv'], 'L1_attn_Wo': _L1_attn_in['Wo'], 'L1_ffn_gate_w': _L1_ffn_in['gate_w'], 'L1_ffn_w_gate': _L1_ffn_in['w_gate'], 'L1_ffn_w_up': _L1_ffn_in['w_up'], 'L1_ffn_w_down': _L1_ffn_in['w_down'], 'L1_ffn_sw_gate': _L1_ffn_in['sw_gate'], 'L1_ffn_sw_up': _L1_ffn_in['sw_up'], 'L1_ffn_sw_down': _L1_ffn_in['sw_down']}
    _x0 = _d['L0_attn_x']
    _d['L0_attn_x'] = jax.random.normal(jax.random.fold_in(jax.random.key(seed), 1), (1, 2048, 256), dtype=_x0.dtype)
    del _x0
    return _d

def reference(L0_attn_x, L0_attn_wq, L0_attn_wk, L0_attn_wv, L0_attn_wo, L0_ffn_weight, L0_ffn_scale, L1_attn_Wq, L1_attn_Wk, L1_attn_Wv, L1_attn_Wo, L1_ffn_gate_w, L1_ffn_w_gate, L1_ffn_w_up, L1_ffn_w_down, L1_ffn_sw_gate, L1_ffn_sw_up, L1_ffn_sw_down):

    def _L0_attn_ref(x, wq, wk, wv, wo):
        import jax, jax.numpy as jnp
        import numpy as np
        MIN_TIMESCALE = 1.0
        MAX_TIMESCALE = 10000.0

        def llama_rope(x):
            B, S, N, H = x.shape
            half = H // 2
            fraction = 2.0 * jnp.arange(0, half, dtype=jnp.float32) / H
            timescale = MIN_TIMESCALE * (MAX_TIMESCALE / MIN_TIMESCALE) ** fraction
            position = jnp.arange(S, dtype=jnp.float32)[None, :, None, None]
            sinusoid = position / timescale[None, None, None, :]
            sin, cos = (jnp.sin(sinusoid), jnp.cos(sinusoid))
            xr = x.astype(jnp.float32).reshape(B, S, N, half, 2)
            x1, x2 = (xr[..., 0], xr[..., 1])
            r1 = x1 * cos - x2 * sin
            r2 = x2 * cos + x1 * sin
            out = jnp.stack((r1, r2), axis=-1).reshape(B, S, N, H)
            return out.astype(x.dtype)
        q = jnp.einsum('bsd,dnh->bsnh', x, wq)
        k = jnp.einsum('bsd,dnh->bsnh', x, wk)
        v = jnp.einsum('bsd,dnh->bsnh', x, wv)
        q = llama_rope(q)
        k = llama_rope(k)
        head_dim = q.shape[-1]
        q = q / jnp.sqrt(jnp.asarray(head_dim, q.dtype))
        S = q.shape[1]
        logits = jnp.einsum('bqnh,bknh->bnqk', q, k)
        causal = jnp.tril(jnp.ones((S, S), dtype=bool))
        logits = jnp.where(causal[None, None, :, :], logits, jnp.asarray(-1e+30, logits.dtype))
        probs = jax.nn.softmax(logits.astype(jnp.float32), axis=-1).astype(v.dtype)
        attn = jnp.einsum('bnqk,bknh->bqnh', probs, v)
        return jnp.einsum('bqnh,nhd->bqd', attn, wo)

    def _L0_ffn_ref(x, weight, scale):
        import jax, jax.numpy as jnp
        import numpy as np
        EPS = 1e-07
        CURVATURE = 1.0
        MAX_NORM_RATIO = 0.99
        B, L, N, K = (4, 256, 256, 256)

        def _ternary_init(key, n, k):
            rand = jax.random.normal(key, (n, k), dtype=jnp.float32)
            threshold = 0.5 * jnp.mean(jnp.abs(rand))
            return jnp.where(rand > threshold, 1.0, jnp.where(rand < -threshold, -1.0, 0.0)).astype(jnp.float32)
        sqrt_c = jnp.sqrt(jnp.float32(CURVATURE))
        out = jnp.einsum('bln,nk->blk', x, weight) * scale
        v_norm = jnp.maximum(jnp.linalg.norm(out, axis=-1, keepdims=True), EPS)
        scaled_norm = sqrt_c * v_norm
        out = out * (jnp.tanh(scaled_norm) / (scaled_norm + EPS))
        max_norm = MAX_NORM_RATIO / sqrt_c
        o_norm = jnp.maximum(jnp.linalg.norm(out, axis=-1, keepdims=True), EPS)
        out = out * jnp.minimum(max_norm / o_norm, 1.0)
        return out.astype(x.dtype)

    def _L1_attn_ref(hidden_states, Wq, Wk, Wv, Wo):
        import jax, jax.numpy as jnp
        import numpy as np
        HQ, HKV, HD, WIN = (16, 4, 128, 64)

        def _sliding_window_attention(q, k, v, win):
            B, H, S, hd = q.shape
            W = win
            nb = S // W
            qb = q.reshape(B, H, nb, W, hd)
            kpad = jnp.pad(k, ((0, 0), (0, 0), (W, 0), (0, 0)))
            vpad = jnp.pad(v, ((0, 0), (0, 0), (W, 0), (0, 0)))
            kb = jnp.concatenate([kpad[:, :, :S].reshape(B, H, nb, W, hd), k.reshape(B, H, nb, W, hd)], axis=3)
            vb = jnp.concatenate([vpad[:, :, :S].reshape(B, H, nb, W, hd), v.reshape(B, H, nb, W, hd)], axis=3)
            scores = jnp.einsum('bhnqd,bhnkd->bhnqk', qb, kb) / jnp.asarray(hd, qb.dtype)
            qi = jnp.arange(W)[:, None]
            ki = jnp.arange(2 * W)[None, :]
            band = (ki >= qi + 1) & (ki <= qi + W)
            blk = jnp.arange(nb)[:, None, None]
            valid = band[None] & ((blk > 0) | (ki[None] >= W))
            neg = jnp.finfo(scores.dtype).min
            scores = jnp.where(valid[None, None], scores, neg)
            probs = jax.nn.softmax(scores, axis=-1)
            out = jnp.einsum('bhnqk,bhnkd->bhnqd', probs, vb)
            return out.reshape(B, H, S, hd)
        B, S, D = hidden_states.shape
        q = (hidden_states @ Wq).reshape(B, S, HQ, HD).transpose(0, 2, 1, 3)
        k = (hidden_states @ Wk).reshape(B, S, HKV, HD).transpose(0, 2, 1, 3)
        v = (hidden_states @ Wv).reshape(B, S, HKV, HD).transpose(0, 2, 1, 3)
        rep = HQ // HKV
        k = jnp.repeat(k, rep, axis=1)
        v = jnp.repeat(v, rep, axis=1)
        attn = _sliding_window_attention(q, k, v, WIN)
        attn = attn.transpose(0, 2, 1, 3).reshape(B, S, HQ * HD)
        return attn @ Wo

    def _L1_ffn_ref(hidden_states, gate_w, w_gate, w_up, w_down, sw_gate, sw_up, sw_down):
        import jax, jax.numpy as jnp
        import numpy as np
        B, S, H = (1, 256, 256)
        E, K, I = (16, 4, 176)
        IS = 352
        CAP = 128
        b, s, h = hidden_states.shape
        x = hidden_states.reshape(-1, h)
        T = x.shape[0]
        scores = jax.nn.softmax(x @ gate_w.T, axis=-1)
        topk_w, topk_i = jax.lax.top_k(scores, K)
        topk_w = topk_w / (topk_w.sum(-1, keepdims=True) + 1e-20)
        flat_i = topk_i.reshape(-1)
        flat_w = topk_w.reshape(-1)
        order = jnp.argsort(flat_i)
        se = flat_i[order]
        counts = jax.ops.segment_sum(jnp.ones_like(flat_i), flat_i, num_segments=E)
        starts = jnp.cumsum(counts) - counts
        rank = jnp.arange(T * K) - starts[se]
        tok = order // K
        slot = jnp.where(rank < CAP, rank, CAP)
        buf = jnp.full((E, CAP + 1), T, dtype=jnp.int32).at[se, slot].set(tok)[:, :CAP]
        wbuf = jnp.zeros((E, CAP + 1), x.dtype).at[se, slot].set(flat_w[order])[:, :CAP]
        xpad = jnp.concatenate([x, jnp.zeros((1, h), x.dtype)], axis=0)
        xg = xpad[buf]
        gact = jax.nn.silu(jnp.einsum('ech,ehi->eci', xg, w_gate))
        mid = gact * jnp.einsum('ech,ehi->eci', xg, w_up)
        eout = jnp.einsum('eci,eih->ech', mid, w_down) * wbuf[..., None]
        y = jnp.zeros((T + 1, h), x.dtype).at[buf.reshape(-1)].add(eout.reshape(-1, h))[:T]
        shared = jax.nn.silu(x @ sw_gate) * (x @ sw_up) @ sw_down
        return (y + shared).reshape(b, s, h)
    x = L0_attn_x
    x = _layernorm(x + _L0_attn_ref(x, L0_attn_wq, L0_attn_wk, L0_attn_wv, L0_attn_wo), axis=-1)
    x = _layernorm(x + _L0_ffn_ref(x, L0_ffn_weight, L0_ffn_scale), axis=-1)
    x = _layernorm(x + _L1_attn_ref(x, L1_attn_Wq, L1_attn_Wk, L1_attn_Wv, L1_attn_Wo), axis=-1)
    x = _layernorm(x + _L1_ffn_ref(x, L1_ffn_gate_w, L1_ffn_w_gate, L1_ffn_w_up, L1_ffn_w_down, L1_ffn_sw_gate, L1_ffn_sw_up, L1_ffn_sw_down), axis=-1)
    return x

_drawn_inputs = setup_inputs


def setup_inputs(seed=0):
    import zlib

    import numpy as np

    out = dict(_drawn_inputs(seed))
    spreads = {'L0_ffn_scale': (0.0625, 0.6)}
    factors = {'L1_attn_Wq': 8.0,
     'L1_attn_Wk': 8.0,
     'L1_ffn_gate_w': 8.0,
     'L1_ffn_w_gate': 8.0,
     'L1_ffn_w_up': 8.0,
     'L1_ffn_w_down': 8.0,
     'L1_ffn_sw_gate': 2.892,
     'L1_ffn_sw_up': 2.865,
     'L1_ffn_sw_down': 2.858}
    for name, (base, spread) in spreads.items():
        noise = np.random.default_rng([zlib.crc32(name.encode()), seed]).standard_normal(out[name].shape)
        drawn = base * np.exp(spread * noise) if base else spread * noise
        out[name] = jnp.asarray(drawn.astype(out[name].dtype))
    for name, factor in factors.items():
        out[name] = (out[name] * factor).astype(out[name].dtype)
    return out
```

```python
from contextlib import ExitStack

import concourse.bass as bass
from concourse import mybir

F32 = mybir.dt.float32
F32R = mybir.dt.float32r
BF16 = mybir.dt.bfloat16
I32 = mybir.dt.int32
ALU = mybir.AluOpType
ACT = mybir.ActivationFunctionType
AX = mybir.AxisListType

P = 128
T = 2048
D = 256
TILES = T // P
KT = D // P
PAIRS = TILES // 2
BANK = 512
LN_EPS = 1e-5

H0 = 16
HD = 128
HALF = HD // 2
QKV = 3 * HD
SCALE0 = float(HD) ** -0.5

BALL_EPS = 1e-7
MAX_NORM = 0.99

HQ, HKV, WIN = 16, 4, 64
REP = HQ // HKV
SCALE1 = 1.0 / HD

E = 16
TOPK = 4
INNER = 176
INNER_S = 352
CAP = 128

MASKED = -1e30

_WIDTHS = [("ident", P), ("causal", 2 * 2 * P), ("window", 2 * 2 * P), ("cos", TILES * HALF),
           ("sin", TILES * HD), ("iota", P), ("before", P), ("lower", E * E), ("where", 2 * TILES)]
CONST = {}
_at = 0
for _name, _n in _WIDTHS:
    CONST[_name] = (_at, _at + _n)
    _at += _n
CONSTS = _at


def at(loop, per_turn, count):
    return loop * per_turn + count


def rows(ap):
    return ap.rearrange("(t p) d -> p t d", p=P)


def bc(ap, shape):
    return ap.to_broadcast(shape)


class Core:

    def __init__(self, nc, ctx):
        self.ctx = ctx
        self.Y = ctx.enter_context(nc.sbuf_tensor("Y", [P, TILES, D], F32))
        self.ident = ctx.enter_context(nc.sbuf_tensor("ident", [P, P], F32))
        self.S = ctx.enter_context(nc.psum_tensor("S", [P, 4, BANK], F32))
        self.TP = ctx.enter_context(nc.psum_tensor("TP", [P, 3, BANK], F32))
        self.PV = ctx.enter_context(nc.psum_tensor("PV", [P, BANK], F32))


def norm_stage(nc, core, name, xT_hi=None, xT_lo=None, xT=None, source=None, normalize=True, store=None):
    Y, ident, TP = core.Y, core.ident, core.TP
    turn = xT_hi is not None or xT is not None
    with ExitStack() as ctx:
        def sem(n):
            return core.ctx.enter_context(nc.semaphore(f"{name}_{n}"))

        loaded = [sem(f"loaded{c}") for c in range(4)] if source is not None else None
        if normalize:
            statistics, root_done, tile_ready = sem("statistics"), sem("root_done"), sem("tile_ready")
        if turn:
            turned, hi_done = sem("turned"), sem("hi_done")
        if xT_hi is not None:
            group_free = sem("group_free")
        if store is not None:
            stored = sem("stored")
        stats = ctx.enter_context(nc.sbuf_tensor(f"{name}_stats", [P, TILES, 6], F32))
        moments = ctx.enter_context(nc.sbuf_tensor(f"{name}_moments", [P, TILES, 2], F32))
        var_eps = ctx.enter_context(nc.sbuf_tensor(f"{name}_var_eps", [P, TILES], F32))
        std = ctx.enter_context(nc.sbuf_tensor(f"{name}_std", [P, TILES], F32))
        rstd = ctx.enter_context(nc.sbuf_tensor(f"{name}_rstd", [P, TILES], F32))
        block = ctx.enter_context(nc.Block())

        @block.sync
        def _(sp):
            if source is not None:
                for c in range(4):
                    sp.dma_start(Y[:, 4 * c:4 * c + 4, :], rows(source)[:, 4 * c:4 * c + 4, :]).then_inc(loaded[c], 16)
            if store is not None:
                for c in range(4):
                    sp.wait_ge(tile_ready, 4 * c + 4)
                    sp.dma_start(rows(store)[:, 4 * c:4 * c + 4, :], Y[:, 4 * c:4 * c + 4, :]).then_inc(stored, 16)
                sp.wait_ge(stored, 4 * 16)

        @block.vector
        def _(dve):
            if normalize:
                for t in range(TILES):
                    dve.bn_stats(stats[:, t, :], Y[:, t, :]).then_inc(statistics, 1)
                for t in range(TILES):
                    dve.wait_ge(statistics, t + 1)
                    dve.bn_aggr(moments[:, t, :], stats[:, t, :]).then_inc(statistics, 1)
                dve.wait_ge(statistics, 2 * TILES)
                dve.tensor_scalar(var_eps[:, :], moments[:, :, 1], LN_EPS, None, ALU.add).then_inc(statistics, 1)
                dve.wait_ge(root_done, 1)
                dve.reciprocal(rstd[:, :], std[:, :]).then_inc(statistics, 1)
                dve.wait_ge(statistics, 2 * TILES + 2)
                for t in range(TILES):
                    dve.tensor_scalar(Y[:, t, :], Y[:, t, :], moments[:, t, 0:1], rstd[:, t:t + 1],
                                      ALU.subtract, ALU.mult).then_inc(tile_ready, 1)
            if xT_hi is not None:
                for g in range(PAIRS):
                    dve.wait_ge(hi_done, g + 1)
                    cols = slice(2 * P * g, 2 * P * (g + 1))
                    dve.tensor_tensor(xT_lo[:, :, cols], TP[:, g % 3, :].rearrange("p (k c) -> p k c", k=KT),
                                      xT_hi[:, :, cols].bitcast(F32), ALU.subtract).then_inc(group_free, 1)

        @block.scalar
        def _(act):
            if normalize:
                act.wait_ge(statistics, 2 * TILES + 1)
                act.activation(std[:, :], var_eps[:, :], ACT.Sqrt).then_inc(root_done, 1)
            if turn:
                for g in range(PAIRS):
                    act.wait_ge(turned, g + 1)
                    cols = slice(2 * P * g, 2 * P * (g + 1))
                    to = xT_hi if xT_hi is not None else xT
                    act.activation(to[:, :, cols], TP[:, g % 3, :].rearrange("p (k c) -> p k c", k=KT),
                                   ACT.Copy).then_inc(hi_done, 1)

        @block.tensor
        def _(pe):
            if not turn:
                return
            for g in range(PAIRS):
                if source is not None and g % 2 == 0:
                    pe.wait_ge(loaded[g // 2], 16)
                if normalize:
                    pe.wait_ge(tile_ready, 2 * g + 2)
                if g >= 3:
                    pe.wait_ge(group_free if xT_hi is not None else hi_done, g - 2)
                for k in range(KT):
                    for j in range(2):
                        last = pe.transpose(TP[:, g % 3, (2 * k + j) * P:(2 * k + j + 1) * P],
                                            Y[:, 2 * g + j, k * P:(k + 1) * P], ident[:, :])
                last.then_inc(turned, 1)


def rotary_attention(nc, core, consts, wqkv, wo, xT_hi, xT_lo):
    Y, ident, S, TP, PV = core.Y, core.ident, core.S, core.TP, core.PV
    ROW_GROUPS = [(2 * (i // 2) + 2 + 3) // 4 for i in range(TILES)]
    TURN = PAIRS
    FREED = TURN + sum(ROW_GROUPS) + PAIRS
    number, n = {}, TURN
    for s in range(TILES + 3):
        if 1 <= s <= TILES:
            for g in range(ROW_GROUPS[s - 1]):
                number["row", s - 1, g] = n
                n += 1
        if s % 2 == 0 and s >= 4:
            number["out", (s - 4) // 2] = n
            n += 1
    assert n == FREED
    CHUNKS = sum(ROW_GROUPS)
    chunk_at = [sum(ROW_GROUPS[:i]) for i in range(TILES)]
    group_at = chunk_at

    def width(i):
        return 2 * P * (i // 2 + 1)

    def base(i):
        return 2 * (i % 2) if ROW_GROUPS[i] <= 2 else 0

    def row(i):
        return S[:, :, :].rearrange("p b c -> p (b c)")[:, base(i) * BANK:base(i) * BANK + width(i)]

    with ExitStack() as ctx:
        def sb(n, shape, dt=F32):
            return ctx.enter_context(nc.sbuf_tensor("l0_" + n, shape, dt))

        def sem(n):
            return core.ctx.enter_context(nc.semaphore("l0_" + n))

        zero = sb("zero", [P, 1])
        w_raw = sb("w_raw", [P, KT, QKV])
        w_hi, w_lo = sb("w_hi", [P, KT, QKV], F32R), sb("w_lo", [P, KT, QKV], F32R)
        wo_raw = sb("wo_raw", [P, D])
        wo_hi, wo_lo = sb("wo_hi", [P, D], F32R), sb("wo_lo", [P, D], F32R)
        cos, sin = sb("cos", [P, TILES, HALF]), sb("sin", [P, TILES, 2, HALF])
        mask32, mask = sb("mask32", [P, 4 * P]), sb("mask", [P, 2, 2 * P], BF16)
        ident16 = sb("ident16", [P, P], BF16)
        straight, crossed = sb("straight", [P, 2, 2, HD]), sb("crossed", [P, 2, 2, HD])
        rotated = sb("rotated", [P, 4, 2, HD])
        qk_hi, qk_lo = sb("qk_hi", [P, 2, T], F32R), sb("qk_lo", [P, 2, T], F32R)
        v_hi, v_lo = sb("v_hi", [P, TILES, HD], F32R), sb("v_lo", [P, TILES, HD], F32R)
        probs = sb("probs", [P, 2, T])
        pT_hi, pT_lo = sb("pT_hi", [P, TILES, 2 * P], F32R), sb("pT_lo", [P, TILES, 2 * P], F32R)
        a_hi, a_lo = sb("a_hi", [P, 2 * P], F32R), sb("a_lo", [P, 2 * P], F32R)
        part_max, neg_max = sb("part_max", [P, 2, 2]), sb("neg_max", [P, 2])
        row_sum, row_inv = sb("row_sum", [P, TILES]), sb("row_inv", [P, TILES])

        consts_in, consts_cast, w_in, wo_in, w_split, wo_split, w_hi_done, wo_hi_done = (sem(n) for n in (
            "consts_in", "consts_cast", "w_in", "wo_in", "w_split", "wo_split", "w_hi_done", "wo_hi_done"))
        zeroed = sem("zeroed")
        tile_projected, tile_multiplied, tile_rotated, qk_turned, v_hi_done, tile_free, qk_hi_done = (sem(n) for n in (
            "tile_projected", "tile_multiplied", "tile_rotated", "qk_turned", "v_hi_done", "tile_free", "qk_hi_done"))
        chunk_scored, part_max_done, neg_max_done, row_exped, row_turned, pT_hi_done, tp_free = (sem(n) for n in (
            "chunk_scored", "part_max_done", "neg_max_done", "row_exped", "row_turned", "pT_hi_done", "tp_free"))
        pair_mixed, a_hi_done, a_lo_done, pair_out, inv_done = (sem(n) for n in (
            "pair_mixed", "a_hi_done", "a_lo_done", "pair_out", "inv_done"))
        block = ctx.enter_context(nc.Block())

        @block.sync
        def _(sp):
            for n, to in (("causal", mask32[:, :]), ("cos", cos[:, :, :].rearrange("p t c -> p (t c)")),
                          ("sin", sin[:, :, :, :].rearrange("p t a c -> p (t a c)"))):
                sp.dma_start(to, consts[:, CONST[n][0]:CONST[n][1]]).then_inc(consts_in, 16)
            sp.dma_start(w_raw[:, :, :], wqkv[0, :, :, :]).then_inc(w_in, 16)
            sp.dma_start(wo_raw[:, :], wo[0, :, :]).then_inc(wo_in, 16)
            with sp.Fori(1, H0) as h:
                sp.wait_ge(w_split, at(h, 1, 0))
                sp.dma_start(w_raw[:, :, :], wqkv[h, :, :, :]).then_inc(w_in, 16)
                sp.wait_ge(wo_split, at(h, 1, 0))
                sp.dma_start(wo_raw[:, :], wo[h, :, :]).then_inc(wo_in, 16)

        @block.gpsimd
        def _(pool):
            pool.memset(zero[:, :], 0.0).then_inc(zeroed, 1)
            pool.wait_ge(zeroed, 1)
            with pool.Fori(0, H0) as h:
                pool.wait_ge(w_in, at(h, 16, 16))
                pool.tensor_tensor(w_hi[:, :, :], w_raw[:, :, :], zero[:, :].unsqueeze(2).to_broadcast([P, KT, QKV]), ALU.add).then_inc(w_hi_done, 1)
                pool.wait_ge(w_hi_done, at(h, 1, 1))
                pool.tensor_tensor(w_lo[:, :, :], w_raw[:, :, :], w_hi[:, :, :].bitcast(F32),
                                   ALU.subtract).then_inc(w_split, 1)
                for t in range(TILES):
                    pool.wait_ge(tile_multiplied, at(h, TILES, t + 1))
                    if t >= 4:
                        pool.wait_ge(qk_turned, at(h, TURN, t // 2 - 1))
                    other = crossed[:, t % 2, :, :].rearrange("p q (a c) -> p q a c", a=2)[:, :, ::-1, :]
                    pool.tensor_tensor(rotated[:, t % 4, :, :].rearrange("p q (a c) -> p q a c", a=2),
                                       straight[:, t % 2, :, :].rearrange("p q (a c) -> p q a c", a=2),
                                       other, ALU.add).then_inc(tile_rotated, 1)
                pool.wait_ge(wo_in, at(h, 16, 16))
                pool.tensor_tensor(wo_hi[:, :], wo_raw[:, :], zero[:, :].to_broadcast([P, D]), ALU.add).then_inc(wo_hi_done, 1)
                pool.wait_ge(wo_hi_done, at(h, 1, 1))
                pool.tensor_tensor(wo_lo[:, :], wo_raw[:, :], wo_hi[:, :].bitcast(F32),
                                   ALU.subtract).then_inc(wo_split, 1)

        @block.tensor
        def _(pe):
            pe.wait_ge(consts_cast, 2)
            with pe.Fori(0, H0) as h:

                def turn(g):
                    pe.wait_ge(tile_rotated, at(h, TILES, 2 * g + 2))
                    if g >= 3:
                        pe.wait_ge(tp_free, at(h, FREED, g - 2))
                    for q in range(2):
                        for j in range(2):
                            last = pe.transpose(TP[:, g % 3, (2 * q + j) * P:(2 * q + j + 1) * P],
                                                rotated[:, (2 * g + j) % 4, q, :], ident[:, :])
                    last.then_inc(qk_turned, 1)

                pe.wait_ge(w_split, at(h, 1, 1))
                for t in range(TILES):
                    if t >= 4:
                        pe.wait_ge(tile_free, at(h, TILES, t - 3))
                    toks = slice(t * P, (t + 1) * P)
                    parts = [(x, w, k) for k in range(KT) for x, w in ((xT_hi, w_hi), (xT_hi, w_lo), (xT_lo, w_hi))]
                    for n, (x, w, k) in enumerate(parts):
                        last = pe.matmul(S[:, t % 4, 0:QKV], x[:, k, toks], w[:, k, :],
                                         start=(n == 0), stop=(n == len(parts) - 1))
                    last.then_inc(tile_projected, 1)
                    if t % 2 == 1 and t >= 3:
                        turn((t - 3) // 2)
                turn(PAIRS - 1)
                pe.wait_ge(tile_free, at(h, TILES, TILES))
                pe.wait_ge(tp_free, at(h, FREED, TURN))

                def scores(i):
                    n = ROW_GROUPS[i]
                    if n <= 2 and i >= 2:
                        pe.wait_ge(row_exped, at(h, TILES, i - 1))
                    if n > 2:
                        pe.wait_ge(row_exped, at(h, TILES, i))
                    q = slice(i * P, (i + 1) * P)
                    for c in range(n):
                        w = min(BANK, width(i) - c * BANK)
                        out = S[:, base(i) + c, 0:w]
                        keys = slice(c * BANK, c * BANK + w)
                        final = c == n - 1
                        pe.matmul(out, qk_hi[:, 0, q], qk_hi[:, 1, keys], start=True, stop=False)
                        pe.matmul(out, qk_hi[:, 0, q], qk_lo[:, 1, keys], start=False, stop=False)
                        last = pe.matmul(out, qk_lo[:, 0, q], qk_hi[:, 1, keys], start=False, stop=not final)
                        if final:
                            last = pe.matmul(out[:, w - 2 * P:w], ident16[:, :], mask[:, i % 2, :],
                                             start=False, stop=True)
                        last.then_inc(chunk_scored, 1)

                def turn_row(i):
                    pe.wait_ge(row_exped, at(h, TILES, i + 1))
                    blocks = width(i) // P
                    for g in range(ROW_GROUPS[i]):
                        n = number["row", i, g]
                        pe.wait_ge(tp_free, at(h, FREED, n - 2))
                        for b in range(4 * g, min(4 * g + 4, blocks)):
                            last = pe.transpose(TP[:, n % 3, (b % 4) * P:(b % 4 + 1) * P],
                                                probs[:, i % 2, b * P:(b + 1) * P], ident[:, :])
                        last.then_inc(row_turned, 1)

                def mix(j):
                    n = number["row", 2 * j + 1, ROW_GROUPS[2 * j + 1] - 1]
                    pe.wait_ge(tp_free, at(h, FREED, n + 1))
                    if j >= 1:
                        pe.wait_ge(a_lo_done, at(h, PAIRS, j))
                    keys = 2 * j + 2
                    for k in range(keys):
                        pe.matmul(PV[:, 0:2 * P], v_hi[:, k, :], pT_hi[:, k, :], start=(k == 0), stop=False)
                        pe.matmul(PV[:, 0:2 * P], v_hi[:, k, :], pT_lo[:, k, :], start=False, stop=False)
                        last = pe.matmul(PV[:, 0:2 * P], v_lo[:, k, :], pT_hi[:, k, :], start=False, stop=(k == keys - 1))
                    last.then_inc(pair_mixed, 1)

                def project(j):
                    n = number["out", j]
                    pe.wait_ge(tp_free, at(h, FREED, n - 2))
                    pe.wait_ge(a_lo_done, at(h, PAIRS, j + 1))
                    pe.wait_ge(wo_split, at(h, 1, 1))
                    for q in range(2):
                        out = TP[:, n % 3, q * D:(q + 1) * D]
                        toks = slice(q * P, (q + 1) * P)
                        pe.matmul(out, a_hi[:, toks], wo_hi[:, :], start=True, stop=False)
                        pe.matmul(out, a_hi[:, toks], wo_lo[:, :], start=False, stop=False)
                        last = pe.matmul(out, a_lo[:, toks], wo_hi[:, :], start=False, stop=True)
                    last.then_inc(pair_out, 1)

                for s in range(TILES + 3):
                    if s < TILES:
                        scores(s)
                    if s % 2 == 1 and s >= 3:
                        mix((s - 3) // 2)
                    if 1 <= s <= TILES:
                        turn_row(s - 1)
                    if s % 2 == 0 and s >= 4:
                        project((s - 4) // 2)
                pe.wait_ge(tp_free, at(h, FREED, FREED))

        @block.scalar
        def _(act):
            with act.Fori(0, H0) as h:

                def qk_high(g):
                    act.wait_ge(qk_turned, at(h, TURN, g + 1))
                    act.activation(qk_hi[:, :, 2 * P * g:2 * P * (g + 1)],
                                   TP[:, g % 3, :].rearrange("p (q c) -> p q c", q=2), ACT.Copy).then_inc(qk_hi_done, 1)

                for t in range(TILES):
                    act.wait_ge(tile_multiplied, at(h, TILES, t + 1))
                    act.activation(v_hi[:, t, :], S[:, t % 4, 2 * HD:QKV], ACT.Copy).then_inc(v_hi_done, 1)
                    if t % 2 == 1 and t >= 3:
                        qk_high((t - 3) // 2)
                qk_high(PAIRS - 1)

                for s in range(TILES + 3):
                    if s < TILES:
                        act.wait_ge(neg_max_done, at(h, TILES, s + 1))
                        if s >= 2:
                            act.wait_ge(row_turned, at(h, CHUNKS, group_at[s - 2] + ROW_GROUPS[s - 2]))
                        act.activation(probs[:, s % 2, 0:width(s)], row(s), ACT.Exp, bias=neg_max[:, s % 2:s % 2 + 1],
                                       scale=SCALE0, accum_out=row_sum[:, s:s + 1]).then_inc(row_exped, 1)
                    if s % 2 == 1 and s >= 3:
                        j = (s - 3) // 2
                        act.wait_ge(pair_mixed, at(h, PAIRS, j + 1))
                        if j >= 1:
                            act.wait_ge(pair_out, at(h, PAIRS, j))
                        act.activation(a_hi[:, :], PV[:, 0:2 * P], ACT.Copy).then_inc(a_hi_done, 1)
                    if 1 <= s <= TILES:
                        i = s - 1
                        for g in range(ROW_GROUPS[i]):
                            n = number["row", i, g]
                            m = min(4, width(i) // P - 4 * g)
                            act.wait_ge(row_turned, at(h, CHUNKS, group_at[i] + g + 1))
                            act.activation(pT_hi[:, 4 * g:4 * g + m, (i % 2) * P:(i % 2 + 1) * P],
                                           TP[:, n % 3, 0:m * P].rearrange("p (b c) -> p b c", c=P),
                                           ACT.Copy).then_inc(pT_hi_done, 1)

        @block.vector
        def _(dve):
            dve.wait_ge(consts_in, 3 * 16)
            dve.tensor_copy(mask[:, :, :], mask32[:, :].rearrange("p (a c) -> p a c", a=2)).then_inc(consts_cast, 1)
            dve.tensor_copy(ident16[:, :], ident[:, :]).then_inc(consts_cast, 1)
            with dve.Fori(0, H0) as h:

                def v_low(t):
                    dve.wait_ge(v_hi_done, at(h, TILES, t + 1))
                    dve.tensor_tensor(v_lo[:, t, :], S[:, t % 4, 2 * HD:QKV], v_hi[:, t, :].bitcast(F32),
                                      ALU.subtract).then_inc(tile_free, 1)

                def qk_low(g):
                    dve.wait_ge(qk_hi_done, at(h, TURN, g + 1))
                    cols = slice(2 * P * g, 2 * P * (g + 1))
                    dve.tensor_tensor(qk_lo[:, :, cols], TP[:, g % 3, :].rearrange("p (q c) -> p q c", q=2),
                                      qk_hi[:, :, cols].bitcast(F32), ALU.subtract).then_inc(tp_free, 1)

                for t in range(TILES):
                    dve.wait_ge(tile_projected, at(h, TILES, t + 1))
                    if t >= 2:
                        dve.wait_ge(tile_rotated, at(h, TILES, t - 1))
                    qk = S[:, t % 4, 0:2 * HD].rearrange("p (b c) -> p b c", c=HALF)
                    dve.tensor_tensor(straight[:, t % 2, :, :].rearrange("p q (a c) -> p (q a) c", a=2), qk,
                                      cos[:, t, :].unsqueeze(1).to_broadcast([P, 4, HALF]), ALU.mult)
                    qk = S[:, t % 4, 0:2 * HD].rearrange("p (q c) -> p q c", c=HD)
                    dve.tensor_tensor(crossed[:, t % 2, :, :], qk,
                                      sin[:, t, :, :].rearrange("p a c -> p (a c)").unsqueeze(1).to_broadcast([P, 2, HD]),
                                      ALU.mult).then_inc(tile_multiplied, 1)
                    if t >= 1:
                        v_low(t - 1)
                    if t % 2 == 1 and t >= 3:
                        qk_low((t - 3) // 2)
                v_low(TILES - 1)
                qk_low(PAIRS - 1)

                PARTS = sum(1 + (n > 1) for n in ROW_GROUPS)
                parts = 0
                for s in range(TILES + 3):
                    if s < TILES:
                        n, r = ROW_GROUPS[s], row(s)
                        if s >= 2:
                            dve.wait_ge(row_exped, at(h, TILES, s - 1))
                        cut = (n - 1) * BANK
                        if n > 1:
                            dve.wait_ge(chunk_scored, at(h, CHUNKS, chunk_at[s] + n - 1))
                            dve.tensor_reduce(part_max[:, s % 2, 0:1], r[:, 0:cut], AX.X, ALU.max).then_inc(part_max_done, 1)
                            parts += 1
                        dve.wait_ge(chunk_scored, at(h, CHUNKS, chunk_at[s] + n))
                        dve.tensor_reduce(part_max[:, s % 2, 1:2], r[:, cut:width(s)], AX.X, ALU.max).then_inc(part_max_done, 1)
                        parts += 1
                        dve.wait_ge(part_max_done, at(h, PARTS, parts))
                        dve.tensor_scalar(neg_max[:, s % 2:s % 2 + 1], part_max[:, s % 2, 1:2],
                                          part_max[:, s % 2, 0:1] if n > 1 else -3.4e38, -SCALE0,
                                          ALU.max, ALU.mult).then_inc(neg_max_done, 1)
                    if s % 2 == 1 and s >= 3:
                        j = (s - 3) // 2
                        dve.wait_ge(a_hi_done, at(h, PAIRS, j + 1))
                        dve.tensor_tensor(a_lo[:, :], PV[:, 0:2 * P], a_hi[:, :].bitcast(F32),
                                          ALU.subtract).then_inc(a_lo_done, 1)
                        dve.reciprocal(row_inv[:, 2 * j:2 * j + 2], row_sum[:, 2 * j:2 * j + 2]).then_inc(inv_done, 1)
                    if 1 <= s <= TILES:
                        i = s - 1
                        for g in range(ROW_GROUPS[i]):
                            n = number["row", i, g]
                            m = min(4, width(i) // P - 4 * g)
                            dve.wait_ge(pT_hi_done, at(h, CHUNKS, group_at[i] + g + 1))
                            to = (slice(4 * g, 4 * g + m), slice((i % 2) * P, (i % 2 + 1) * P))
                            dve.tensor_tensor(pT_lo[:, to[0], to[1]], TP[:, n % 3, 0:m * P].rearrange("p (b c) -> p b c", c=P),
                                              pT_hi[:, to[0], to[1]].bitcast(F32), ALU.subtract).then_inc(tp_free, 1)
                    if s % 2 == 0 and s >= 4:
                        j = (s - 4) // 2
                        n = number["out", j]
                        dve.wait_ge(pair_out, at(h, PAIRS, j + 1))
                        dve.wait_ge(inv_done, at(h, PAIRS, j + 1))
                        for q in range(2):
                            i = 2 * j + q
                            last = dve.scalar_tensor_tensor(out=Y[:, i, :], in0=TP[:, n % 3, q * D:(q + 1) * D],
                                                            scalar=row_inv[:, i:i + 1], in1=Y[:, i, :],
                                                            op0=ALU.mult, op1=ALU.add)
                        last.then_inc(tp_free, 1)


def ball_projection(nc, core, weight, scale, xT_hi, xT_lo):
    Y, TP = core.Y, core.TP
    with ExitStack() as ctx:
        def sb(n, shape, dt=F32):
            return ctx.enter_context(nc.sbuf_tensor("ball_" + n, shape, dt))

        def sem(n):
            return core.ctx.enter_context(nc.semaphore("ball_" + n))

        w_raw, w_hi, w_lo = sb("w_raw", [P, KT, D]), sb("w_hi", [P, KT, D], F32R), sb("w_lo", [P, KT, D], F32R)
        scale_all = sb("scale_all", [P, D])
        out, squares = sb("out", [P, TILES, D]), sb("squares", [P, 2, D])
        sq_sum, norm, v_norm, tanh, den, inv, factor, o_norm, bound = (sb(n, [P, TILES]) for n in (
            "sq_sum", "norm", "v_norm", "tanh", "den", "inv", "factor", "o_norm", "bound"))
        w_in, scale_in, w_hi_done, w_split, pair_done, out_done, squared, rooted, tanh_done, step = (sem(n) for n in (
            "w_in", "scale_in", "w_hi_done", "w_split", "pair_done", "out_done", "squared", "rooted", "tanh_done", "step"))
        block = ctx.enter_context(nc.Block())

        @block.sync
        def _(sp):
            sp.dma_start(w_raw[:, :, :], weight.rearrange("(k p) n -> p k n", p=P)).then_inc(w_in, 16)
            sp.dma_start(scale_all[:, :], scale.partition_broadcast(P)).then_inc(scale_in, 16)

        @block.tensor
        def _(pe):
            pe.wait_ge(w_split, 1)
            for g in range(PAIRS):
                if g >= 3:
                    pe.wait_ge(out_done, g - 2)
                for j in range(2):
                    t = 2 * g + j
                    toks = slice(t * P, (t + 1) * P)
                    parts = [(x, w, k) for k in range(KT) for x, w in ((xT_hi, w_hi), (xT_hi, w_lo), (xT_lo, w_hi))]
                    for n, (x, w, k) in enumerate(parts):
                        last = pe.matmul(TP[:, g % 3, j * D:(j + 1) * D], x[:, k, toks], w[:, k, :],
                                         start=(n == 0), stop=(n == len(parts) - 1))
                last.then_inc(pair_done, 1)

        @block.scalar
        def _(act):
            for t in range(TILES):
                act.wait_ge(out_done, t // 2 + 1)
                if t >= 2:
                    act.wait_ge(squared, t - 1)
                act.activation(squares[:, t % 2, :], out[:, t, :], ACT.Square, accum_out=sq_sum[:, t:t + 1]).then_inc(squared, 1)
            act.wait_ge(squared, TILES)
            act.activation(norm[:, :], sq_sum[:, :], ACT.Sqrt).then_inc(rooted, 1)
            act.wait_ge(step, 1)
            act.activation(tanh[:, :], v_norm[:, :], ACT.Tanh).then_inc(tanh_done, 1)

        @block.vector
        def _(dve):
            dve.wait_ge(w_in, 16)
            dve.tensor_copy(w_hi[:, :, :], w_raw[:, :, :]).then_inc(w_hi_done, 1)
            dve.wait_ge(w_hi_done, 1)
            dve.tensor_tensor(w_lo[:, :, :], w_raw[:, :, :], w_hi[:, :, :].bitcast(F32), ALU.subtract).then_inc(w_split, 1)
            dve.wait_ge(scale_in, 16)
            for g in range(PAIRS):
                dve.wait_ge(pair_done, g + 1)
                dve.tensor_tensor(out[:, 2 * g:2 * g + 2, :], TP[:, g % 3, :].rearrange("p (j n) -> p j n", j=2),
                                  scale_all[:, :].unsqueeze(1).to_broadcast([P, 2, D]), ALU.mult).then_inc(out_done, 1)
            dve.wait_ge(rooted, 1)
            dve.tensor_scalar(v_norm[:, :], norm[:, :], BALL_EPS, None, ALU.max).then_inc(step, 1)
            dve.wait_ge(step, 1)
            dve.tensor_scalar(den[:, :], v_norm[:, :], BALL_EPS, None, ALU.add).then_inc(step, 1)
            dve.wait_ge(step, 2)
            dve.reciprocal(inv[:, :], den[:, :]).then_inc(step, 1)
            dve.wait_ge(step, 3)
            dve.wait_ge(tanh_done, 1)
            dve.tensor_tensor(factor[:, :], tanh[:, :], inv[:, :], ALU.mult).then_inc(step, 1)
            dve.wait_ge(step, 4)
            dve.tensor_tensor(o_norm[:, :], norm[:, :], factor[:, :], ALU.mult).then_inc(step, 1)
            dve.wait_ge(step, 5)
            dve.tensor_scalar(o_norm[:, :], o_norm[:, :], BALL_EPS, None, ALU.max).then_inc(step, 1)
            dve.wait_ge(step, 6)
            dve.reciprocal(bound[:, :], o_norm[:, :]).then_inc(step, 1)
            dve.wait_ge(step, 7)
            dve.tensor_scalar(bound[:, :], bound[:, :], MAX_NORM, 1.0, ALU.mult, ALU.min).then_inc(step, 1)
            dve.wait_ge(step, 8)
            dve.tensor_tensor(factor[:, :], factor[:, :], bound[:, :], ALU.mult).then_inc(step, 1)
            dve.wait_ge(step, 9)
            for t in range(TILES):
                dve.scalar_tensor_tensor(out=Y[:, t, :], in0=out[:, t, :], scalar=factor[:, t:t + 1], in1=Y[:, t, :],
                                         op0=ALU.mult, op1=ALU.add)


def window_attention(nc, core, consts, wq, wkv, wo, xT_hi, xT_lo):
    Y, ident, S, TP, PV = core.Y, core.ident, core.S, core.TP, core.PV
    CH = 4
    PER = TILES // CH
    KEYS = T + P
    ROUNDS = REP * CH + 3 * TILES
    with ExitStack() as ctx:
        def sb(n, shape, dt=F32):
            return ctx.enter_context(nc.sbuf_tensor("l1_" + n, shape, dt))

        def sem(n):
            return core.ctx.enter_context(nc.semaphore("l1_" + n))

        wq_raw = sb("wq_raw", [P, KT, REP * HD])
        wq_hi, wq_lo = sb("wq_hi", [P, KT, REP * HD], F32R), sb("wq_lo", [P, KT, REP * HD], F32R)
        wkv_raw = sb("wkv_raw", [P, KT, 2 * HD])
        wkv_hi, wkv_lo = sb("wkv_hi", [P, KT, 2 * HD], F32R), sb("wkv_lo", [P, KT, 2 * HD], F32R)
        wo_raw = sb("wo_raw", [P, REP, D])
        wo_hi, wo_lo = sb("wo_hi", [P, REP, D], F32R), sb("wo_lo", [P, REP, D], F32R)
        mask32, mask = sb("mask32", [P, 4 * P]), sb("mask", [P, 2, 2 * P], BF16)
        ident16 = sb("ident16", [P, P], BF16)
        zero = sb("zero", [P, 1])
        k_nat = sb("k_nat", [P, 4, HD])
        kT_hi, kT_lo = sb("kT_hi", [P, KEYS], F32R), sb("kT_lo", [P, KEYS], F32R)
        v_hi, v_lo = sb("v_hi", [P, TILES + 1, HD], F32R), sb("v_lo", [P, TILES + 1, HD], F32R)
        qT_hi, qT_lo = sb("qT_hi", [P, 2, REP, BANK], F32R), sb("qT_lo", [P, 2, REP, BANK], F32R)
        probs = sb("probs", [P, 2, REP, 2 * P])
        pT_hi, pT_lo = sb("pT_hi", [P, 2, REP, P], F32R), sb("pT_lo", [P, 2, REP, P], F32R)
        a_hi, a_lo = sb("a_hi", [P, REP, P], F32R), sb("a_lo", [P, REP, P], F32R)
        row_max, neg_max = sb("row_max", [P, 2, REP]), sb("neg_max", [P, 2, REP])
        row_sum, row_inv = sb("row_sum", [P, 2, REP]), sb("row_inv", [P, 2, REP])

        consts_in, consts_cast, wkv_in, wq_in, wo_in, w_split, padded = (sem(n) for n in (
            "consts_in", "consts_cast", "wkv_in", "wq_in", "wo_in", "w_split", "padded"))
        part = sem("part")
        kv_projected, kv_hi_done, kv_free, k_turned, kT_hi_done, kT_free = (sem(n) for n in (
            "kv_projected", "kv_hi_done", "kv_free", "k_turned", "kT_hi_done", "kT_free"))
        q_projected, qT_hi_done = sem("q_projected"), sem("qT_hi_done")
        scored, max_done, neg_max_done, exped, inv_done, normed, p_turned, pT_hi_done, tp_free = (sem(n) for n in (
            "scored", "max_done", "neg_max_done", "exped", "inv_done", "normed", "p_turned", "pT_hi_done", "tp_free"))
        mixed, a_hi_done, a_lo_done, projected = (sem(n) for n in ("mixed", "a_hi_done", "a_lo_done", "projected"))
        block = ctx.enter_context(nc.Block())

        FREED = CH + ROUNDS

        def order():
            seq = [("q", 0, r) for r in range(REP)]
            for s in range(TILES + 2):
                if s < TILES and s % PER == 2 and s // PER + 1 < CH:
                    seq += [("q", s // PER + 1, r) for r in range(REP)]
                if 1 <= s <= TILES:
                    seq += [("p", s - 1, 0), ("p", s - 1, 1)]
                if s >= 2:
                    seq.append(("out", s - 2))
            return {x: CH + n for n, x in enumerate(seq)}

        number = order()
        assert len(number) == ROUNDS

        @block.sync
        def _(sp):
            sp.dma_start(mask32[:, :], consts[:, CONST["window"][0]:CONST["window"][1]]).then_inc(consts_in, 16)
            sp.dma_start(wkv_raw[:, :, :], wkv[0, :, :, :]).then_inc(wkv_in, 16)
            sp.dma_start(wq_raw[:, :, :], wq[0, :, :, :]).then_inc(wq_in, 16)
            sp.dma_start(wo_raw[:, :, :], wo[0, :, :, :]).then_inc(wo_in, 16)
            with sp.Fori(1, HKV) as h:
                sp.wait_ge(w_split, at(h, 3, -2))
                sp.dma_start(wkv_raw[:, :, :], wkv[h, :, :, :]).then_inc(wkv_in, 16)
                sp.wait_ge(w_split, at(h, 3, -1))
                sp.dma_start(wq_raw[:, :, :], wq[h, :, :, :]).then_inc(wq_in, 16)
                sp.wait_ge(w_split, at(h, 3, 0))
                sp.dma_start(wo_raw[:, :, :], wo[h, :, :, :]).then_inc(wo_in, 16)

        @block.gpsimd
        def _(pool):
            for z in (kT_hi[:, 0:P], kT_lo[:, 0:P], v_hi[:, 0, :], v_lo[:, 0, :]):
                pool.memset(z.bitcast(F32), 0.0).then_inc(padded, 1)
            pool.memset(zero[:, :], 0.0).then_inc(padded, 1)
            pool.wait_ge(padded, 5)
            with pool.Fori(0, HKV) as h:
                for n, (raw, hi, lo, arrived) in enumerate(((wkv_raw, wkv_hi, wkv_lo, wkv_in), (wq_raw, wq_hi, wq_lo, wq_in),
                                                            (wo_raw, wo_hi, wo_lo, wo_in))):
                    if n == 2:
                        pool.wait_ge(kv_projected, at(h, TILES, 1))
                    pool.wait_ge(arrived, at(h, 16, 16))
                    pool.tensor_tensor(hi[:, :, :], raw[:, :, :], zero[:, :].unsqueeze(2).to_broadcast(raw.shape), ALU.add).then_inc(part, 1)
                    pool.wait_ge(part, at(h, 3, n + 1))
                    pool.tensor_tensor(lo[:, :, :], raw[:, :, :], hi[:, :, :].bitcast(F32), ALU.subtract).then_inc(w_split, 1)
                for t in range(TILES):
                    pool.wait_ge(inv_done, at(h, TILES, t + 1))
                    pool.tensor_tensor(probs[:, t % 2, :, :], probs[:, t % 2, :, :],
                                       row_inv[:, t % 2, :].unsqueeze(2).to_broadcast([P, REP, 2 * P]),
                                       ALU.mult).then_inc(normed, 1)

        @block.tensor
        def _(pe):
            pe.wait_ge(consts_cast, 2)
            pe.wait_ge(padded, 4)
            with pe.Fori(0, HKV) as h:

                def turn_keys(c):
                    pe.wait_ge(kv_free, at(h, TILES, 4 * c + 4))
                    if c >= 3:
                        pe.wait_ge(tp_free, at(h, FREED, c - 2))
                    for b in range(4):
                        last = pe.transpose(TP[:, c % 3, b * P:(b + 1) * P], k_nat[:, b, :], ident[:, :])
                    last.then_inc(k_turned, 1)

                pe.wait_ge(w_split, at(h, 3, 1))
                for t in range(TILES):
                    if t >= 4:
                        pe.wait_ge(kv_free, at(h, TILES, t - 3))
                    toks = slice(t * P, (t + 1) * P)
                    parts = [(x, w, k) for k in range(KT) for x, w in ((xT_hi, wkv_hi), (xT_hi, wkv_lo), (xT_lo, wkv_hi))]
                    for n, (x, w, k) in enumerate(parts):
                        last = pe.matmul(S[:, t % 4, 0:2 * HD], x[:, k, toks], w[:, k, :],
                                         start=(n == 0), stop=(n == len(parts) - 1))
                    last.then_inc(kv_projected, 1)
                    if t % 4 == 3:
                        turn_keys(t // 4)
                pe.wait_ge(tp_free, at(h, FREED, CH))

                def project_q(c):
                    if c == 0:
                        pe.wait_ge(w_split, at(h, 3, 2))
                    for r in range(REP):
                        g = number["q", c, r]
                        pe.wait_ge(tp_free, at(h, FREED, g - 2))
                        parts = [(w, x, k) for k in range(KT) for w, x in ((wq_hi, xT_hi), (wq_hi, xT_lo), (wq_lo, xT_hi))]
                        for n, (w, x, k) in enumerate(parts):
                            last = pe.matmul(TP[:, g % 3, :], w[:, k, r * HD:(r + 1) * HD], x[:, k, c * BANK:(c + 1) * BANK],
                                             start=(n == 0), stop=(n == len(parts) - 1))
                        last.then_inc(q_projected, 1)

                def scores(t):
                    pe.wait_ge(tp_free, at(h, FREED, number["q", t // PER, REP - 1] + 1))
                    if t >= 2:
                        pe.wait_ge(exped, at(h, TILES, t - 1))
                    keys = slice(t * P, (t + 2) * P)
                    for r in range(REP):
                        out = S[:, 2 * (t % 2) + r // 2, (r % 2) * 2 * P:(r % 2 + 1) * 2 * P]
                        toks = slice((t % PER) * P, (t % PER + 1) * P)
                        hi, lo = (q[:, (t // PER) % 2, r, toks] for q in (qT_hi, qT_lo))
                        pe.matmul(out, hi, kT_hi[:, keys], start=True, stop=False)
                        pe.matmul(out, hi, kT_lo[:, keys], start=False, stop=False)
                        pe.matmul(out, lo, kT_hi[:, keys], start=False, stop=False)
                        last = pe.matmul(out, ident16[:, :], mask[:, min(t, 1), :], start=False, stop=True)
                    last.then_inc(scored, 1)

                def turn_probs(t):
                    pe.wait_ge(normed, at(h, TILES, t + 1))
                    for b in range(2):
                        n = number["p", t, b]
                        pe.wait_ge(tp_free, at(h, FREED, n - 2))
                        for r in range(REP):
                            last = pe.transpose(TP[:, n % 3, r * P:(r + 1) * P], probs[:, t % 2, r, b * P:(b + 1) * P], ident[:, :])
                        last.then_inc(p_turned, 1)

                def mix(t):
                    pe.wait_ge(tp_free, at(h, FREED, number["p", t, 1] + 1))
                    if t >= 1:
                        pe.wait_ge(a_lo_done, at(h, TILES, t))
                    for b in range(2):
                        hi, lo = (p[:, b, :, :].rearrange("p r c -> p (r c)") for p in (pT_hi, pT_lo))
                        pe.matmul(PV[:, :], v_hi[:, t + b, :], hi, start=(b == 0), stop=False)
                        pe.matmul(PV[:, :], v_hi[:, t + b, :], lo, start=False, stop=False)
                        last = pe.matmul(PV[:, :], v_lo[:, t + b, :], hi, start=False, stop=(b == 1))
                    last.then_inc(mixed, 1)

                def project(t):
                    n = number["out", t]
                    pe.wait_ge(tp_free, at(h, FREED, n - 2))
                    pe.wait_ge(a_lo_done, at(h, TILES, t + 1))
                    pe.wait_ge(w_split, at(h, 3, 3))
                    out = TP[:, n % 3, 0:D]
                    for r in range(REP):
                        pe.matmul(out, a_hi[:, r, :], wo_hi[:, r, :], start=(r == 0), stop=False)
                        pe.matmul(out, a_hi[:, r, :], wo_lo[:, r, :], start=False, stop=False)
                        last = pe.matmul(out, a_lo[:, r, :], wo_hi[:, r, :], start=False, stop=(r == REP - 1))
                    last.then_inc(projected, 1)

                project_q(0)
                for s in range(TILES + 2):
                    if s < TILES:
                        if s % PER == 2 and s // PER + 1 < CH:
                            project_q(s // PER + 1)
                        scores(s)
                    if s >= 2:
                        mix(s - 2)
                    if 1 <= s <= TILES:
                        turn_probs(s - 1)
                    if s >= 2:
                        project(s - 2)
                pe.wait_ge(tp_free, at(h, FREED, FREED))

        @block.scalar
        def _(act):
            with act.Fori(0, HKV) as h:
                for t in range(TILES):
                    act.wait_ge(kv_projected, at(h, TILES, t + 1))
                    if t >= 4:
                        act.wait_ge(k_turned, at(h, CH, t // 4))
                    act.activation(k_nat[:, t % 4, :], S[:, t % 4, 0:HD], ACT.Copy)
                    act.activation(v_hi[:, t + 1, :], S[:, t % 4, HD:2 * HD], ACT.Copy).then_inc(kv_hi_done, 1)
                    if t % 4 == 3:
                        c = t // 4
                        act.wait_ge(k_turned, at(h, CH, c + 1))
                        act.activation(kT_hi[:, P + c * BANK:P + (c + 1) * BANK], TP[:, c % 3, :], ACT.Copy).then_inc(kT_hi_done, 1)

                def queries(c):
                    for r in range(REP):
                        m = REP * c + r
                        act.wait_ge(q_projected, at(h, REP * CH, m + 1))
                        act.activation(qT_hi[:, c % 2, r, :], TP[:, number["q", c, r] % 3, :], ACT.Copy).then_inc(qT_hi_done, 1)

                queries(0)
                for s in range(TILES + 2):
                    if s < TILES:
                        if s % PER == 2 and s // PER + 1 < CH:
                            queries(s // PER + 1)
                        act.wait_ge(neg_max_done, at(h, TILES, s + 1))
                        if s >= 2:
                            act.wait_ge(p_turned, at(h, 2 * TILES, 2 * s - 2))
                        for r in range(REP):
                            last = act.activation(probs[:, s % 2, r, :], S[:, 2 * (s % 2) + r // 2, (r % 2) * 2 * P:(r % 2 + 1) * 2 * P],
                                                  ACT.Exp, bias=neg_max[:, s % 2, r:r + 1], scale=SCALE1,
                                                  accum_out=row_sum[:, s % 2, r:r + 1])
                        last.then_inc(exped, 1)
                    if s >= 2:
                        t = s - 2
                        act.wait_ge(mixed, at(h, TILES, t + 1))
                        if t >= 1:
                            act.wait_ge(projected, at(h, TILES, t))
                        act.activation(a_hi[:, :, :], PV[:, :].rearrange("p (r c) -> p r c", r=REP), ACT.Copy).then_inc(a_hi_done, 1)
                    if 1 <= s <= TILES:
                        t = s - 1
                        for b in range(2):
                            n = number["p", t, b]
                            act.wait_ge(p_turned, at(h, 2 * TILES, 2 * t + b + 1))
                            act.activation(pT_hi[:, b, :, :], TP[:, n % 3, :].rearrange("p (r c) -> p r c", r=REP), ACT.Copy).then_inc(pT_hi_done, 1)

        @block.vector
        def _(dve):
            dve.wait_ge(consts_in, 16)
            dve.tensor_copy(mask[:, :, :], mask32[:, :].rearrange("p (a c) -> p a c", a=2)).then_inc(consts_cast, 1)
            dve.tensor_copy(ident16[:, :], ident[:, :]).then_inc(consts_cast, 1)
            with dve.Fori(0, HKV) as h:
                for t in range(TILES):
                    dve.wait_ge(kv_hi_done, at(h, TILES, t + 1))
                    dve.tensor_tensor(v_lo[:, t + 1, :], S[:, t % 4, HD:2 * HD], v_hi[:, t + 1, :].bitcast(F32),
                                      ALU.subtract).then_inc(kv_free, 1)
                    if t % 4 == 3:
                        c = t // 4
                        cols = slice(P + c * BANK, P + (c + 1) * BANK)
                        dve.wait_ge(kT_hi_done, at(h, CH, c + 1))
                        dve.tensor_tensor(kT_lo[:, cols], TP[:, c % 3, :], kT_hi[:, cols].bitcast(F32), ALU.subtract).then_inc(tp_free, 1)

                def queries(c):
                    for r in range(REP):
                        m = REP * c + r
                        dve.wait_ge(qT_hi_done, at(h, REP * CH, m + 1))
                        dve.tensor_tensor(qT_lo[:, c % 2, r, :], TP[:, number["q", c, r] % 3, :], qT_hi[:, c % 2, r, :].bitcast(F32),
                                          ALU.subtract).then_inc(tp_free, 1)

                queries(0)
                for s in range(TILES + 2):
                    if s < TILES:
                        if s % PER == 2 and s // PER + 1 < CH:
                            queries(s // PER + 1)
                        dve.wait_ge(scored, at(h, TILES, s + 1))
                        if s >= 2:
                            dve.wait_ge(exped, at(h, TILES, s - 1))
                        dve.tensor_reduce(row_max[:, s % 2, :], S[:, 2 * (s % 2):2 * (s % 2) + 2, :].rearrange("p b (r c) -> p (b r) c", r=2),
                                          AX.X, ALU.max).then_inc(max_done, 1)
                        dve.wait_ge(max_done, at(h, TILES, s + 1))
                        dve.tensor_scalar(neg_max[:, s % 2, :], row_max[:, s % 2, :], -SCALE1, None, ALU.mult).then_inc(neg_max_done, 1)
                    if s >= 2:
                        t = s - 2
                        dve.wait_ge(a_hi_done, at(h, TILES, t + 1))
                        dve.tensor_tensor(a_lo[:, :, :], PV[:, :].rearrange("p (r c) -> p r c", r=REP), a_hi[:, :, :].bitcast(F32),
                                          ALU.subtract).then_inc(a_lo_done, 1)
                    if s < TILES:
                        dve.wait_ge(exped, at(h, TILES, s + 1))
                        if s >= 2:
                            dve.wait_ge(normed, at(h, TILES, s - 1))
                        dve.reciprocal(row_inv[:, s % 2, :], row_sum[:, s % 2, :]).then_inc(inv_done, 1)
                    if 1 <= s <= TILES:
                        t = s - 1
                        for b in range(2):
                            n = number["p", t, b]
                            dve.wait_ge(pT_hi_done, at(h, 2 * TILES, 2 * t + b + 1))
                            dve.tensor_tensor(pT_lo[:, b, :, :], TP[:, n % 3, :].rearrange("p (r c) -> p r c", r=REP),
                                              pT_hi[:, b, :, :].bitcast(F32), ALU.subtract).then_inc(tp_free, 1)
                    if s >= 2:
                        t = s - 2
                        n = number["out", t]
                        dve.wait_ge(projected, at(h, TILES, t + 1))
                        dve.tensor_tensor(Y[:, t, :], TP[:, n % 3, 0:D], Y[:, t, :], ALU.add).then_inc(tp_free, 1)


def expert_mix(nc, core, consts, gate_w, sw_gu, sw_down, w_gu, w_down, xT, x_rows, routed):
    Y, ident, S, TP, PV = core.Y, core.ident, core.S, core.TP, core.PV
    HALF_I = INNER // 2
    PIECES = INNER_S // HALF_I
    RING = 4
    NOWHERE = 4096.0
    INFO = 6

    def first(i):
        return isinstance(i, int) and i == 0

    def in_range(i, u, back):
        return not isinstance(i, int) or 0 <= RING * i + u - back < E

    with ExitStack() as ctx:
        def sb(n, shape, dt=F32):
            return ctx.enter_context(nc.sbuf_tensor("moe_" + n, shape, dt))

        def sem(n):
            return core.ctx.enter_context(nc.semaphore("moe_" + n))

        iota, before, lower, where = sb("iota", [P, P]), sb("before", [P, P]), sb("lower", [P, E * E]), sb("where", [P, 2, TILES])
        before16, ones16, lower16 = sb("before16", [P, P], BF16), sb("ones16", [P, P], BF16), sb("lower16", [P, E, E], BF16)
        gw = sb("gw", [P, KT, E])
        sgu, sdown = sb("sgu", [P, KT, 2 * INNER_S]), sb("sdown", [HALF_I, PIECES, D])
        wgu, wdown = sb("wgu", [P, RING, KT, 2 * INNER]), sb("wdown", [HALF_I, RING, 2, D])
        zeros = sb("zeros", [P, TILES // 2 * D])
        top, total, total_inv, gain_sum, gain_inv = (sb(n, [P, TILES]) for n in ("top", "total", "total_inv", "gain_sum", "gain_inv"))
        shifted, exps, score, above, chosen, gain, rest, slot = (sb(n, [P, TILES, E]) for n in (
            "shifted", "exps", "score", "above", "chosen", "gain", "rest", "slot"))
        greater, equal = sb("greater", [P, TILES, E, E], BF16), sb("equal", [P, TILES, E, E], BF16)
        chosen16, info = sb("chosen16", [P, TILES, E], BF16), sb("info", [P, TILES, E, INFO], BF16)
        onehot = sb("onehot", [P, 2, TILES, P], BF16)
        slots = sb("slots", [P, E, INFO])
        token_a, token_b, token = sb("token_a", [P, E]), sb("token_b", [P, E]), sb("token", [P, E], mybir.dt.uint32)
        slot_gain_a, slot_gain = sb("slot_gain_a", [P, E]), sb("slot_gain", [P, E])
        s_act, s_mid = sb("s_act", [P, 2, INNER_S]), sb("s_mid", [P, 2, INNER_S])
        s_midT = sb("s_midT", [HALF_I, 2, PIECES, P])
        xg, xgT = sb("xg", [P, RING, D]), sb("xgT", [P, 2, KT, P])
        e_act, e_mid = sb("e_act", [P, 2, INNER]), sb("e_mid", [P, 2, INNER])
        e_midT, e_out = sb("e_midT", [HALF_I, 2, 2, P]), sb("e_out", [P, 2, D])
        y_routed = sb("y_routed", [P, TILES, D])

        consts_in, gw_in, shared_in, consts_cast, zeroed, cleared, out_free, ring_set = (sem(n) for n in (
            "consts_in", "gw_in", "shared_in", "consts_cast", "zeroed", "cleared", "out_free", "ring_set"))
        weights_in = [sem(f"weights_in{n}") for n in range(RING)]
        gathered = [sem(f"gathered{n}") for n in range(RING)]
        logits_done, shift_done, exps_done, route, rank_done, onehot_done, info_done = (sem(n) for n in (
            "logits_done", "shift_done", "exps_done", "route", "rank_done", "onehot_done", "info_done"))
        s_up_done, s_act_done, s_mixed, s_turned, s_midT_done, s_down_done, s_added = (sem("s_" + n) for n in (
            "up_done", "act_done", "mixed", "turned", "midT_done", "down_done", "added"))
        x_turned, xgT_done, up_done, act_done, mixed, turned, midT_done, down_done, out_done = (sem("e_" + n) for n in (
            "x_turned", "xgT_done", "up_done", "act_done", "mixed", "turned", "midT_done", "down_done", "out_done"))
        added = [sem(f"added{n}") for n in range(2)]
        y_in = sem("y_in")
        block = ctx.enter_context(nc.Block())

        ROUTE = {n: k + 1 for k, n in enumerate((
            "top", "total", "total_inv", "score", "greater", "equal", "equal_lower", "greater_equal", "above", "chosen", "chosen16",
            "gain_raw", "gain_sum", "gain_eps", "gain_inv", "gain", "high", "high_rest", "middle", "middle_rest", "low",
            "numbers", "tiles", "ones", "away", "slot",
            "slots", "token_a", "token_b", "token", "gain_a", "slot_gain"))}

        @block.sync
        def _(sp):
            for n, to in (("iota", iota[:, :]), ("before", before[:, :]), ("lower", lower[:, :]),
                          ("where", where[:, :, :].rearrange("p a t -> p (a t)"))):
                sp.dma_start(to, consts[:, CONST[n][0]:CONST[n][1]]).then_inc(consts_in, 16)
            sp.dma_start(gw[:, :, :], gate_w).then_inc(gw_in, 16)
            sp.dma_start(sgu[:, :, :], sw_gu).then_inc(shared_in, 16)
            sp.dma_start(sdown[:, :, :], sw_down).then_inc(shared_in, 16)
            sp.wait_ge(zeroed, 1)
            for n in range(2):
                sp.dma_start(rows(routed)[:, n * TILES // 2:(n + 1) * TILES // 2, :],
                             zeros[:, :].rearrange("p (t d) -> p t d", d=D)).then_inc(cleared, 16)

            for u in range(RING):
                sp.dma_start(wgu[:, u, :, :], w_gu[u, :, :, :]).then_inc(weights_in[u], 16)
                sp.dma_start(wdown[:, u, :, :], w_down[u, :, :, :]).then_inc(weights_in[u], 16)
            with sp.Fori(1, E // RING) as i:
                for u in range(RING):
                    sp.wait_ge(up_done, at(i, RING, u - RING + 1))
                    sp.dma_start(wgu[:, u, :, :], w_gu[RING * i + u, :, :, :]).then_inc(weights_in[u], 16)
                    sp.wait_ge(down_done, at(i, RING, u - RING + 1))
                    sp.dma_start(wdown[:, u, :, :], w_down[RING * i + u, :, :, :]).then_inc(weights_in[u], 16)
            for n in range(2):
                sp.wait_ge(added[n], 16 * E // 2)
            sp.dma_start(y_routed[:, :, :], rows(routed)).then_inc(y_in, 16)

        @block.gpsimd
        def _(pool):
            pool.memset(zeros[:, :], 0.0).then_inc(zeroed, 1)
            pool.memset(xg[:, :, :], 0.0).then_inc(ring_set, 1)
            pool.sem_inc(out_free, 1)
            pool.wait_ge(ring_set, 1)
            pool.wait_ge(cleared, 32)

            def gather(e):
                if e >= RING:
                    pool.wait_ge(x_turned, e - RING + 1)
                pool.indirect_dma_start(xg[:, e % RING, :], None, x_rows, bass.IndirectOffsetOnAxis(ap=token[:, e:e + 1], axis=0),
                                        bounds_check=T - 1, oob_is_err=False).then_inc(gathered[e % RING], 16)

            def scatter(e):
                pool.wait_ge(out_done, e + 1)
                if e >= 1:
                    pool.wait_ge(added[(e - 1) % 2], 16 * ((e - 1) // 2 + 1))
                    pool.sem_inc(out_free, 1)
                pool.indirect_dma_start(routed, bass.IndirectOffsetOnAxis(ap=token[:, e:e + 1], axis=0), e_out[:, e % 2, :], None,
                                        bounds_check=T - 1, oob_is_err=False, compute_op=ALU.add).then_inc(added[e % 2], 16)

            pool.wait_ge(route, ROUTE["token"])
            for e in range(RING):
                gather(e)
            for e in range(E):
                scatter(e)
                if e + RING < E:
                    gather(e + RING)

        @block.tensor
        def _(pe):
            pe.wait_ge(gw_in, 16)
            for t in range(TILES):
                for k in range(KT):
                    last = pe.matmul(PV[:, t * E:(t + 1) * E], xT[:, k, t * P:(t + 1) * P], gw[:, k, :], start=(k == 0), stop=(k == KT - 1))
            last.then_inc(logits_done, 1)
            pe.wait_ge(shared_in, 32)

            def s_up(t):
                if t >= 2:
                    pe.wait_ge(s_mixed, t - 1)
                for half in range(2):
                    for k in range(KT):
                        last = pe.matmul(S[:, (2 * t + half) % 4, 0:INNER_S], xT[:, k, t * P:(t + 1) * P],
                                         sgu[:, k, half * INNER_S:(half + 1) * INNER_S], start=(k == 0), stop=(k == KT - 1))
                last.then_inc(s_up_done, 1)

            def s_turn(t):
                pe.wait_ge(s_mixed, t + 1)
                if t >= 1:
                    pe.wait_ge(s_midT_done, t)
                for c in range(PIECES):
                    last = pe.transpose(TP[0:HALF_I, 0, c * P:(c + 1) * P], s_mid[:, t % 2, c * HALF_I:(c + 1) * HALF_I], ident[:, :])
                last.then_inc(s_turned, 1)

            def s_down(t):
                pe.wait_ge(s_midT_done, t + 1)
                if t >= 2:
                    pe.wait_ge(s_added, t - 1)
                for c in range(PIECES):
                    last = pe.matmul(TP[:, 1 + t % 2, 0:D], s_midT[:, t % 2, c, :], sdown[:, c, :], start=(c == 0), stop=(c == PIECES - 1))
                last.then_inc(s_down_done, 1)

            def ranks():
                pe.wait_ge(route, ROUTE["chosen16"])
                pe.wait_ge(consts_cast, 3)
                pe.matmul(PV[:, 0:TILES * E], before16[:, :], chosen16[:, :, :].rearrange("p t e -> p (t e)"), start=True, stop=False)
                for d in range(1, TILES):
                    last = pe.matmul(PV[:, d * E:TILES * E], ones16[:, :], chosen16[:, 0:TILES - d, :].rearrange("p t e -> p (t e)"),
                                     start=False, stop=(d == TILES - 1))
                last.then_inc(rank_done, 1)

            def slot_info(e):
                pe.wait_ge(onehot_done, e + 1)
                pe.wait_ge(route, ROUTE["slot"])
                for t in range(TILES):
                    last = pe.matmul(PV[:, e * INFO:(e + 1) * INFO], onehot[:, e % 2, t, :], info[:, t, e, :], start=(t == 0), stop=(t == TILES - 1))
                last.then_inc(info_done, 1)

            for s in range(TILES + 2):
                if s < TILES:
                    s_up(s)
                if 1 <= s <= TILES:
                    s_turn(s - 1)
                if s >= 2:
                    s_down(s - 2)
                if s == 4:
                    ranks()
                if 6 <= s < 6 + E // 2:
                    slot_info(2 * (s - 6))
                    slot_info(2 * (s - 6) + 1)

            def x_turn(i, u):
                pe.wait_ge(gathered[u], at(i, 16, 16))
                if not (first(i) and u == 0):
                    pe.wait_ge(xgT_done, at(i, RING, u))
                for k in range(KT):
                    last = pe.transpose(TP[:, 0, k * P:(k + 1) * P], xg[:, u, k * P:(k + 1) * P], ident[:, :])
                last.then_inc(x_turned, 1)

            def up(i, u, ring):
                pe.wait_ge(xgT_done, at(i, RING, u + 1))
                pe.wait_ge(weights_in[ring], at(i, 32, 32) if u == ring else at(i, 32, 0))
                for k in range(KT):
                    last = pe.matmul(S[:, ring, 0:2 * INNER], xgT[:, ring % 2, k, :], wgu[:, ring, k, :], start=(k == 0), stop=(k == KT - 1))
                last.then_inc(up_done, 1)

            def turn(i, u, ring):
                pe.wait_ge(mixed, at(i, RING, u + 1))
                if not (first(i) and u == 0):
                    pe.wait_ge(midT_done, at(i, RING, u))
                for c in range(2):
                    last = pe.transpose(TP[0:HALF_I, 1, c * P:(c + 1) * P], e_mid[:, ring % 2, c * HALF_I:(c + 1) * HALF_I], ident[:, :])
                last.then_inc(turned, 1)

            def down(i, u, ring):
                pe.wait_ge(midT_done, at(i, RING, u + 1))
                if not (first(i) and u == 0):
                    pe.wait_ge(out_done, at(i, RING, u))
                for c in range(2):
                    last = pe.matmul(TP[:, 2, 0:D], e_midT[:, ring % 2, c, :], wdown[:, ring, c, :], start=(c == 0), stop=(c == 1))
                last.then_inc(down_done, 1)

            pe.wait_ge(s_added, TILES)
            pe.wait_ge(route, ROUTE["slots"])

            def steps(i, us):
                for u in us:
                    if in_range(i, u, 0):
                        x_turn(i, u)
                    for back, stage in ((1, up), (2, turn), (3, down)):
                        if in_range(i, u, back):
                            stage(i, u - back, (u - back) % RING)

            steps(0, range(RING))
            with pe.Fori(1, E // RING) as i:
                steps(i, range(RING))
            steps(E // RING, range(3))

        @block.scalar
        def _(act):
            act.wait_ge(shift_done, 1)
            act.activation(exps[:, :, :], shifted[:, :, :], ACT.Exp).then_inc(exps_done, 1)
            for s in range(TILES + 1):
                if s < TILES:
                    act.wait_ge(s_up_done, s + 1)
                    if s >= 2:
                        act.wait_ge(s_mixed, s - 1)
                    act.activation(s_act[:, s % 2, :], S[:, (2 * s) % 4, 0:INNER_S], ACT.Silu).then_inc(s_act_done, 1)
                if s >= 1:
                    t = s - 1
                    act.wait_ge(s_turned, t + 1)
                    if t >= 2:
                        act.wait_ge(s_down_done, t - 1)
                    act.activation(s_midT[:, t % 2, :, :], TP[0:HALF_I, 0, :].rearrange("p (c n) -> p c n", c=PIECES), ACT.Copy).then_inc(s_midT_done, 1)

            def x_turn(i, u):
                act.wait_ge(x_turned, at(i, RING, u + 1))
                if not (first(i) and u < 2):
                    act.wait_ge(up_done, at(i, RING, u - 1))
                act.activation(xgT[:, u % 2, :, :], TP[:, 0, 0:KT * P].rearrange("p (k c) -> p k c", k=KT), ACT.Copy).then_inc(xgT_done, 1)

            def up(i, u, ring):
                act.wait_ge(up_done, at(i, RING, u + 1))
                if not (first(i) and u < 2):
                    act.wait_ge(mixed, at(i, RING, u - 1))
                act.activation(e_act[:, ring % 2, :], S[:, ring, 0:INNER], ACT.Silu).then_inc(act_done, 1)

            def turn(i, u, ring):
                act.wait_ge(turned, at(i, RING, u + 1))
                if not (first(i) and u < 2):
                    act.wait_ge(down_done, at(i, RING, u - 1))
                act.activation(e_midT[:, ring % 2, :, :], TP[0:HALF_I, 1, 0:2 * P].rearrange("p (c n) -> p c n", c=2), ACT.Copy).then_inc(midT_done, 1)

            def steps(i, us):
                for u in us:
                    if in_range(i, u, 0):
                        x_turn(i, u)
                    for back, stage in ((1, up), (2, turn)):
                        if in_range(i, u, back):
                            stage(i, u - back, (u - back) % RING)

            steps(0, range(RING))
            with act.Fori(1, E // RING) as i:
                steps(i, range(RING))
            steps(E // RING, range(3))

        @block.vector
        def _(dve):
            done = [0]

            def routed_step(name, instruction):
                instruction.then_inc(route, 1)
                done[0] += 1
                assert ROUTE[name] == done[0]
                dve.wait_ge(route, done[0])

            dve.wait_ge(consts_in, 4 * 16)
            dve.tensor_copy(before16[:, :], before[:, :]).then_inc(consts_cast, 1)
            dve.memset(ones16[:, :], 1.0).then_inc(consts_cast, 1)
            dve.tensor_copy(lower16[:, :, :], lower[:, :].rearrange("p (a b) -> p a b", a=E)).then_inc(consts_cast, 1)
            logits = PV[:, 0:TILES * E].rearrange("p (t e) -> p t e", e=E)
            wide = [P, TILES, E]
            dve.wait_ge(logits_done, 1)
            routed_step("top", dve.tensor_reduce(top[:, :], logits, AX.X, ALU.max))
            dve.tensor_tensor(shifted[:, :, :], logits, top[:, :].unsqueeze(2).to_broadcast(wide), ALU.subtract).then_inc(shift_done, 1)
            dve.wait_ge(exps_done, 1)
            routed_step("total", dve.tensor_reduce(total[:, :], exps[:, :, :], AX.X, ALU.add))
            routed_step("total_inv", dve.reciprocal(total_inv[:, :], total[:, :]))
            routed_step("score", dve.tensor_tensor(score[:, :, :], exps[:, :, :], total_inv[:, :].unsqueeze(2).to_broadcast(wide), ALU.mult))

            def choose_a():
                others = score[:, :, :].unsqueeze(2).to_broadcast([P, TILES, E, E])
                mine = score[:, :, :].unsqueeze(3).to_broadcast([P, TILES, E, E])
                routed_step("greater", dve.tensor_tensor(greater[:, :, :, :], others, mine, ALU.is_gt))
                routed_step("equal", dve.tensor_tensor(equal[:, :, :, :], others, mine, ALU.is_equal))

            def choose_b():
                dve.wait_ge(consts_cast, 3)
                flat = [P, TILES, E * E]
                g, q = (x[:, :, :, :].rearrange("p t a b -> p t (a b)") for x in (greater, equal))
                routed_step("equal_lower", dve.tensor_tensor(q, q, lower16[:, :, :].rearrange("p a b -> p (a b)").unsqueeze(1).to_broadcast(flat), ALU.mult))
                routed_step("greater_equal", dve.tensor_tensor(g, g, q, ALU.add))
                routed_step("above", dve.tensor_reduce(above[:, :, :], greater[:, :, :, :], AX.X, ALU.add))
                routed_step("chosen", dve.tensor_scalar(chosen[:, :, :], above[:, :, :], float(TOPK), None, ALU.is_lt))
                routed_step("chosen16", dve.tensor_copy(chosen16[:, :, :], chosen[:, :, :]))

            def weigh():
                routed_step("gain_raw", dve.tensor_tensor(gain[:, :, :], score[:, :, :], chosen[:, :, :], ALU.mult))
                routed_step("gain_sum", dve.tensor_reduce(gain_sum[:, :], gain[:, :, :], AX.X, ALU.add))
                routed_step("gain_eps", dve.tensor_scalar(gain_sum[:, :], gain_sum[:, :], 1e-20, None, ALU.add))
                routed_step("gain_inv", dve.reciprocal(gain_inv[:, :], gain_sum[:, :]))
                routed_step("gain", dve.tensor_tensor(gain[:, :, :], gain[:, :, :], gain_inv[:, :].unsqueeze(2).to_broadcast(wide), ALU.mult))
                routed_step("high", dve.tensor_copy(info[:, :, :, 3], gain[:, :, :]))
                routed_step("high_rest", dve.tensor_tensor(rest[:, :, :], gain[:, :, :], info[:, :, :, 3], ALU.subtract))
                routed_step("middle", dve.tensor_copy(info[:, :, :, 4], rest[:, :, :]))
                routed_step("middle_rest", dve.tensor_tensor(rest[:, :, :], rest[:, :, :], info[:, :, :, 4], ALU.subtract))
                routed_step("low", dve.tensor_copy(info[:, :, :, 5], rest[:, :, :]))

            def place():
                routed_step("numbers", dve.tensor_copy(info[:, :, :, 0], where[:, 0, :].unsqueeze(2).to_broadcast(wide)))
                routed_step("tiles", dve.tensor_copy(info[:, :, :, 1], where[:, 1, :].unsqueeze(2).to_broadcast(wide)))
                routed_step("ones", dve.memset(info[:, :, :, 2], 1.0))
                routed_step("away", dve.tensor_scalar(rest[:, :, :], chosen[:, :, :], -NOWHERE, NOWHERE, ALU.mult, ALU.add))
                dve.wait_ge(rank_done, 1)
                routed_step("slot", dve.tensor_tensor(slot[:, :, :], logits, rest[:, :, :], ALU.add))

            def one_hot(e):
                if e >= 2:
                    dve.wait_ge(info_done, e - 1)
                dve.tensor_tensor(onehot[:, e % 2, :, :], iota[:, :].unsqueeze(1).to_broadcast([P, TILES, P]),
                                  slot[:, :, e].unsqueeze(2).to_broadcast([P, TILES, P]), ALU.is_equal).then_inc(onehot_done, 1)

            def s_silu_mul(t):
                u, b = S[:, (2 * t + 1) % 4, 0:INNER_S], t % 2
                dve.wait_ge(s_act_done, t + 1)
                if t >= 2:
                    dve.wait_ge(s_turned, t - 1)
                dve.tensor_tensor(s_mid[:, b, :], u, s_act[:, b, :], ALU.mult).then_inc(s_mixed, 1)

            def s_add(t):
                dve.wait_ge(s_down_done, t + 1)
                dve.tensor_tensor(Y[:, t, :], TP[:, 1 + t % 2, 0:D], Y[:, t, :], ALU.add).then_inc(s_added, 1)

            for s in range(TILES + 2):
                if s < TILES:
                    s_silu_mul(s)
                if s == 0:
                    choose_a()
                if s == 1:
                    choose_b()
                if s == 2:
                    weigh()
                if s == 4:
                    place()
                if 5 <= s < 5 + E // 2:
                    one_hot(2 * (s - 5))
                    one_hot(2 * (s - 5) + 1)
                if s >= 2:
                    s_add(s - 2)
            dve.wait_ge(info_done, E)
            routed_step("slots", dve.tensor_copy(slots[:, :, :], PV[:, 0:E * INFO].rearrange("p (e c) -> p e c", c=INFO)))
            routed_step("token_a", dve.scalar_tensor_tensor(out=token_a[:, :], in0=slots[:, :, 1], scalar=float(P), in1=slots[:, :, 0], op0=ALU.mult, op1=ALU.add))
            routed_step("token_b", dve.tensor_scalar(token_b[:, :], slots[:, :, 2], -NOWHERE, NOWHERE, ALU.mult, ALU.add))
            routed_step("token", dve.tensor_tensor(token[:, :], token_a[:, :], token_b[:, :], ALU.add))
            routed_step("gain_a", dve.tensor_tensor(slot_gain_a[:, :], slots[:, :, 5], slots[:, :, 4], ALU.add))
            routed_step("slot_gain", dve.tensor_tensor(slot_gain[:, :], slot_gain_a[:, :], slots[:, :, 3], ALU.add))

            def up(i, u, ring):
                up_, b = S[:, ring, INNER:2 * INNER], ring % 2
                dve.wait_ge(act_done, at(i, RING, u + 1))
                if not (first(i) and u < 2):
                    dve.wait_ge(turned, at(i, RING, u - 1))
                dve.tensor_tensor(e_mid[:, b, :], up_, e_act[:, b, :], ALU.mult).then_inc(mixed, 1)

            def down(i, u, ring):
                dve.wait_ge(down_done, at(i, RING, u + 1))
                if not (first(i) and u == 0):
                    dve.wait_ge(out_free, at(i, RING, u))
                dve.tensor_scalar(e_out[:, ring % 2, :], TP[:, 2, 0:D], slot_gain[:, bass.ds(RING * i + u, 1)], None, ALU.mult).then_inc(out_done, 1)

            def steps(i, us):
                for u in us:
                    for back, stage in ((1, up), (3, down)):
                        if in_range(i, u, back):
                            stage(i, u - back, (u - back) % RING)

            steps(0, range(RING))
            with dve.Fori(1, E // RING) as i:
                steps(i, range(RING))
            steps(E // RING, range(3))
            dve.wait_ge(y_in, 16)
            for t in range(TILES):
                dve.tensor_tensor(Y[:, t, :], Y[:, t, :], y_routed[:, t, :], ALU.add)



def load_ident(nc, core, consts):
    with ExitStack() as ctx:
        loaded = ctx.enter_context(nc.semaphore("ident_loaded"))
        block = ctx.enter_context(nc.Block())

        @block.sync
        def _(sp):
            sp.dma_start(core.ident[:, :], consts[:, CONST["ident"][0]:CONST["ident"][1]]).then_inc(loaded, 16)
            sp.wait_ge(loaded, 16)


def build(nc, x, consts, wqkv0, wo0, ball_w, ball_scale, wq1, wkv1, wo1, gate_w, sw_gu, sw_down, w_gu, w_down, out):
    x_rows = nc.dram_tensor("x_rows", (T, D), F32).ap()
    routed = nc.dram_tensor("routed", (T, D), F32).ap()
    with ExitStack() as ctx:
        core = Core(nc, ctx)
        load_ident(nc, core, consts)
        with ExitStack() as split:
            xT_hi = split.enter_context(nc.sbuf_tensor("xT_hi", [P, KT, T], F32R))
            xT_lo = split.enter_context(nc.sbuf_tensor("xT_lo", [P, KT, T], F32R))
            norm_stage(nc, core, "load", xT_hi=xT_hi, xT_lo=xT_lo, source=x, normalize=False)
            rotary_attention(nc, core, consts, wqkv0, wo0, xT_hi, xT_lo)
            norm_stage(nc, core, "norm0", xT_hi=xT_hi, xT_lo=xT_lo)
            ball_projection(nc, core, ball_w, ball_scale, xT_hi, xT_lo)
            norm_stage(nc, core, "norm1", xT_hi=xT_hi, xT_lo=xT_lo)
            window_attention(nc, core, consts, wq1, wkv1, wo1, xT_hi, xT_lo)
        xT = ctx.enter_context(nc.sbuf_tensor("xT", [P, KT, T], F32))
        norm_stage(nc, core, "norm2", xT=xT, store=x_rows)
        expert_mix(nc, core, consts, gate_w, sw_gu, sw_down, w_gu, w_down, xT, x_rows, routed)
        norm_stage(nc, core, "norm3", store=out)



def _constants(np):
    p, e = np.arange(P), np.arange(E)
    c = np.zeros((P, CONSTS), np.float32)

    def put(name, a):
        c[:, CONST[name][0]:CONST[name][1]] = np.asarray(a, np.float32).reshape(P, -1)

    put("ident", np.eye(P))
    later = np.where(p[None, :] > p[:, None], MASKED, 0.0)
    put("causal", np.concatenate([later, np.full((P, P), MASKED), np.zeros((P, P)), later], 1))
    back = np.arange(2 * P)[None, :] - P - p[:, None]
    window = np.where((back <= 0) & (back > -WIN), 0.0, MASKED)
    put("window", np.concatenate([np.where(np.arange(2 * P)[None, :] >= P, window, MASKED), window], 1))
    fraction = np.float32(2.0) * np.arange(HALF, dtype=np.float32) / np.float32(HD)
    timescale = np.power(np.float32(10000.0), fraction).astype(np.float32)
    phase = (np.arange(T, dtype=np.float32)[:, None] / timescale[None, :]).astype(np.float32)
    cos, sin = np.cos(phase), np.sin(phase)
    put("cos", cos.reshape(TILES, P, HALF).transpose(1, 0, 2))
    put("sin", np.stack([sin, -sin], 1).reshape(TILES, P, HD).transpose(1, 0, 2))
    put("iota", np.broadcast_to(p[None, :], (P, P)))
    put("before", p[:, None] < p[None, :])
    put("lower", np.broadcast_to((e[None, :] < e[:, None]).reshape(1, E * E), (P, E * E)))
    put("where", np.concatenate([np.broadcast_to(p[:, None], (P, TILES)), np.broadcast_to(np.arange(TILES)[None, :], (P, TILES))], 1))
    return c


def kernel(**inputs):
    import numpy as np
    import concourse.bacc as bacc
    from concourse.bass_utils import run_bass_kernel_spmd

    i = {k: np.asarray(v) for k, v in inputs.items()}
    turned = np.concatenate([np.arange(0, HD, 2), np.arange(1, HD, 2)])
    qkv0 = np.stack([i["L0_attn_wq"][:, :, turned], i["L0_attn_wk"][:, :, turned], i["L0_attn_wv"]], 2)
    kv1 = np.stack([i["L1_attn_Wk"].reshape(KT, P, HKV, HD), i["L1_attn_Wv"].reshape(KT, P, HKV, HD)], 3)
    arrays = {
        "x": i["L0_attn_x"].reshape(T, D),
        "consts": _constants(np),
        "wqkv0": qkv0.reshape(KT, P, H0, QKV).transpose(2, 1, 0, 3),
        "wo0": i["L0_attn_wo"],
        "ball_w": i["L0_ffn_weight"],
        "ball_scale": i["L0_ffn_scale"],
        "wq1": i["L1_attn_Wq"].reshape(KT, P, HKV, REP * HD).transpose(2, 1, 0, 3),
        "wkv1": kv1.transpose(2, 1, 0, 3, 4).reshape(HKV, P, KT, 2 * HD),
        "wo1": i["L1_attn_Wo"].reshape(HKV, REP, HD, D).transpose(0, 2, 1, 3),
        "gate_w": i["L1_ffn_gate_w"].T.reshape(KT, P, E).transpose(1, 0, 2),
        "sw_gu": np.concatenate([i["L1_ffn_sw_gate"], i["L1_ffn_sw_up"]], 1).reshape(KT, P, 2 * INNER_S).transpose(1, 0, 2),
        "sw_down": i["L1_ffn_sw_down"].reshape(2 * INNER_S // INNER, INNER // 2, D).transpose(1, 0, 2),
        "w_gu": np.concatenate([i["L1_ffn_w_gate"], i["L1_ffn_w_up"]], 2).reshape(E, KT, P, 2 * INNER).transpose(0, 2, 1, 3),
        "w_down": i["L1_ffn_w_down"].reshape(E, 2, INNER // 2, D).transpose(0, 2, 1, 3),
    }
    arrays = {f"in_{k}": np.ascontiguousarray(v) for k, v in arrays.items()}
    nc = bacc.Bacc("TRN2", target_bir_lowering=False, num_devices=1)
    args = [nc.dram_tensor(k, v.shape, mybir.dt.from_np(v.dtype), kind="ExternalInput").ap() for k, v in arrays.items()]
    out = nc.dram_tensor("out_0", (T, D), F32, kind="ExternalOutput").ap()
    build(nc, *args, out)
    r = run_bass_kernel_spmd(nc, [arrays], core_ids=[0])
    return r.results[0]["out_0"].reshape(1, T, D)
```

```python
from contextlib import ExitStack

import concourse.bass as bass
from concourse import mybir

F32 = mybir.dt.float32
F32R = mybir.dt.float32r
BF16 = mybir.dt.bfloat16
I32 = mybir.dt.int32
ALU = mybir.AluOpType
ACT = mybir.ActivationFunctionType
AX = mybir.AxisListType

P = 128
T = 2048
D = 256
TILES = T // P
KT = D // P
PAIRS = TILES // 2
BANK = 512
LN_EPS = 1e-5

H0 = 16
HD = 128
HALF = HD // 2
QKV = 3 * HD
SCALE0 = float(HD) ** -0.5

BALL_EPS = 1e-7
MAX_NORM = 0.99

HQ, HKV, WIN = 16, 4, 64
REP = HQ // HKV
SCALE1 = 1.0 / HD

E = 16
TOPK = 4
INNER = 176
INNER_S = 352
CAP = 128

MASKED = -1e30

_WIDTHS = [("ident", P), ("causal", 2 * 2 * P), ("window", 2 * 2 * P), ("cos", TILES * HALF),
           ("sin", TILES * HALF), ("iota", P), ("before", P), ("lower", E * E), ("where", 2 * TILES)]
CONST = {}
_at = 0
for _name, _n in _WIDTHS:
    CONST[_name] = (_at, _at + _n)
    _at += _n
CONSTS = _at


def at(loop, per_turn, count):
    return loop * per_turn + count


def rows(ap):
    return ap.rearrange("(t p) d -> p t d", p=P)


def bc(ap, shape):
    return ap.to_broadcast(shape)


class Core:

    def __init__(self, nc, ctx):
        self.ctx = ctx
        self.Y = ctx.enter_context(nc.sbuf_tensor("Y", [P, TILES, D], F32))
        self.ident = ctx.enter_context(nc.sbuf_tensor("ident", [P, P], F32))
        self.S = ctx.enter_context(nc.psum_tensor("S", [P, 4, BANK], F32))
        self.TP = ctx.enter_context(nc.psum_tensor("TP", [P, 3, BANK], F32))
        self.PV = ctx.enter_context(nc.psum_tensor("PV", [P, BANK], F32))


def norm_stage(nc, core, name, xT_hi=None, xT_lo=None, xT=None, source=None, normalize=True, store=None):
    Y, ident, TP = core.Y, core.ident, core.TP
    turn = xT_hi is not None or xT is not None
    with ExitStack() as ctx:
        def sem(n):
            return core.ctx.enter_context(nc.semaphore(f"{name}_{n}"))

        loaded = [sem(f"loaded{c}") for c in range(4)] if source is not None else None
        if normalize:
            statistics, root_done, tile_ready = sem("statistics"), sem("root_done"), sem("tile_ready")
        if turn:
            turned, hi_done = sem("turned"), sem("hi_done")
        if xT_hi is not None:
            group_free = sem("group_free")
        if store is not None:
            stored = sem("stored")
        stats = ctx.enter_context(nc.sbuf_tensor(f"{name}_stats", [P, TILES, 6], F32))
        moments = ctx.enter_context(nc.sbuf_tensor(f"{name}_moments", [P, TILES, 2], F32))
        var_eps = ctx.enter_context(nc.sbuf_tensor(f"{name}_var_eps", [P, TILES], F32))
        std = ctx.enter_context(nc.sbuf_tensor(f"{name}_std", [P, TILES], F32))
        rstd = ctx.enter_context(nc.sbuf_tensor(f"{name}_rstd", [P, TILES], F32))
        block = ctx.enter_context(nc.Block())

        @block.sync
        def _(sp):
            if source is not None:
                for c in range(4):
                    sp.dma_start(Y[:, 4 * c:4 * c + 4, :], rows(source)[:, 4 * c:4 * c + 4, :]).then_inc(loaded[c], 16)
            if store is not None:
                for c in range(4):
                    sp.wait_ge(tile_ready, 4 * c + 4)
                    sp.dma_start(rows(store)[:, 4 * c:4 * c + 4, :], Y[:, 4 * c:4 * c + 4, :]).then_inc(stored, 16)
                sp.wait_ge(stored, 4 * 16)

        @block.vector
        def _(dve):
            if normalize:
                for t in range(TILES):
                    dve.bn_stats(stats[:, t, :], Y[:, t, :]).then_inc(statistics, 1)
                for t in range(TILES):
                    dve.wait_ge(statistics, t + 1)
                    dve.bn_aggr(moments[:, t, :], stats[:, t, :]).then_inc(statistics, 1)
                dve.wait_ge(statistics, 2 * TILES)
                dve.tensor_scalar(var_eps[:, :], moments[:, :, 1], LN_EPS, None, ALU.add).then_inc(statistics, 1)
                dve.wait_ge(root_done, 1)
                dve.reciprocal(rstd[:, :], std[:, :]).then_inc(statistics, 1)
                dve.wait_ge(statistics, 2 * TILES + 2)
                for t in range(TILES):
                    dve.tensor_scalar(Y[:, t, :], Y[:, t, :], moments[:, t, 0:1], rstd[:, t:t + 1],
                                      ALU.subtract, ALU.mult).then_inc(tile_ready, 1)
            if xT_hi is not None:
                for g in range(PAIRS):
                    dve.wait_ge(hi_done, g + 1)
                    cols = slice(2 * P * g, 2 * P * (g + 1))
                    dve.tensor_tensor(xT_lo[:, :, cols], TP[:, g % 3, :].rearrange("p (k c) -> p k c", k=KT),
                                      xT_hi[:, :, cols].bitcast(F32), ALU.subtract).then_inc(group_free, 1)

        @block.scalar
        def _(act):
            if normalize:
                act.wait_ge(statistics, 2 * TILES + 1)
                act.activation(std[:, :], var_eps[:, :], ACT.Sqrt).then_inc(root_done, 1)
            if turn:
                for g in range(PAIRS):
                    act.wait_ge(turned, g + 1)
                    cols = slice(2 * P * g, 2 * P * (g + 1))
                    to = xT_hi if xT_hi is not None else xT
                    act.activation(to[:, :, cols], TP[:, g % 3, :].rearrange("p (k c) -> p k c", k=KT),
                                   ACT.Copy).then_inc(hi_done, 1)

        @block.tensor
        def _(pe):
            if not turn:
                return
            for g in range(PAIRS):
                if source is not None and g % 2 == 0:
                    pe.wait_ge(loaded[g // 2], 16)
                if normalize:
                    pe.wait_ge(tile_ready, 2 * g + 2)
                if g >= 3:
                    pe.wait_ge(group_free if xT_hi is not None else hi_done, g - 2)
                for k in range(KT):
                    for j in range(2):
                        last = pe.transpose(TP[:, g % 3, (2 * k + j) * P:(2 * k + j + 1) * P],
                                            Y[:, 2 * g + j, k * P:(k + 1) * P], ident[:, :])
                last.then_inc(turned, 1)


TENSOR_ORDER = """
    project0 project1 project2 project3 project4 turn0 project5 project6 turn1 project7 turn2 project8 project9
    project10 turn3 project11 turn4 project12 project13 project14 turn5 scores0 project15 turn6 scores1 scores2
    scores3 scores4 row0.0 row1.0 row2.0 scores5 row3.0 mix0.0.2 scores6 row4.0 scores7 row4.1 turn7 row5.0
    mix1.0.4 out0 row5.1 scores8 row6.0 row6.1 mix2.0.4 out1 row7.0 scores9 mix2.4.6 row7.1 row8.0 row8.1
    mix3.0.2 row8.2 mix3.2.3 scores10 row9.0 row9.1 mix3.3.8 row9.2 out2 scores11 mix4.0.5 out3 row10.0 row10.1
    scores12 row10.2 row11.0 mix4.5.10 row11.1 row11.2 scores13 mix5.0.1 row12.0 row12.1 mix5.1.5 row12.2 out4
    scores14 row12.3 row13.0 mix5.5.12 row13.1 row13.2 row13.3 scores15 mix6.0.3 row14.0 row14.1 mix6.3.8
    row14.2 out5 mix6.8.10 row14.3 mix6.10.11 row15.0 mix6.11.14 row15.1 row15.2 row15.3 mix7.0.5 out6 mix7.5.16
    out7"""
SCALAR_ORDER = """
    project0 project1 project2 project3 project4 project5 turn0 turn1 project6 project7 project8 turn2 turn3
    project9 project10 project11 turn4 project12 turn5 project13 project14 turn6 project15 scores0 scores1
    scores2 scores3 row0.0 row1.0 row2.0 scores4 row3.0 mix0 scores5 row4.0 scores6 row4.1 turn7 row5.0 scores7
    mix1 row5.1 row6.0 row6.1 scores8 row7.0 mix2 row7.1 scores9 row8.0 row8.1 row8.2 row9.0 row9.1 scores10
    row9.2 mix3 scores11 row10.0 row10.1 row10.2 row11.0 scores12 row11.1 mix4 row11.2 row12.0 scores13 row12.1
    row12.2 row12.3 row13.0 scores14 row13.1 mix5 row13.2 row13.3 row14.0 row14.1 scores15 row14.2 row14.3
    row15.0 mix6 row15.1 row15.2 row15.3 mix7"""
VECTOR_ORDER = """
    project0 project1 project2 project3 project4 project5 project6 project7 turn0 turn1 project8 project9 turn2
    project10 project11 turn3 project12 project13 turn4 project14 turn5 scores0 project15 scores1 turn6 scores2
    scores3 scores4 row0.0 row1.0 scores5 row2.0 row3.0 scores6 mix0 row4.0 scores7 row4.1 turn7 row5.0 out0
    mix1 scores8 row5.1 row6.0 row6.1 out1 row7.0 scores9 mix2 row7.1 row8.0 row8.1 scores10 row8.2 row9.0
    row9.1 mix3 scores11 row9.2 out2 out3 row10.0 scores12 row10.1 row10.2 row11.0 row11.1 mix4 scores13 row11.2
    row12.0 row12.1 row12.2 scores14 out4 row12.3 row13.0 row13.1 mix5 row13.2 scores15 row13.3 row14.0 row14.1
    row14.2 out5 row14.3 row15.0 mix6 row15.1 row15.2 row15.3 out6 mix7 out7"""


def steps_of(order):
    steps = []
    for word in order.split():
        name = word.rstrip("0123456789.")
        steps.append((name, *(int(n) for n in word[len(name):].split("."))))
    return steps


def row_groups(i):
    return (2 * (i // 2) + 2 + 3) // 4


def rotary_attention(nc, core, consts, wqkv, wo, xT_hi, xT_lo):
    Y, ident, S, TP, PV = core.Y, core.ident, core.S, core.TP, core.PV
    TENSOR, SCALAR, VECTOR = (steps_of(order) for order in (TENSOR_ORDER, SCALAR_ORDER, VECTOR_ORDER))
    number = {}
    for what in TENSOR:
        if what[0] in ("turn", "row", "out"):
            number[what] = len(number)
    FREED = len(number)
    ROW_GROUPS = [row_groups(i) for i in range(TILES)]
    CHUNKS = sum(ROW_GROUPS)
    chunk_at = [sum(ROW_GROUPS[:i]) for i in range(TILES)]
    TURN = PAIRS
    SMALL = PAIRS

    def width(i):
        return 2 * P * (i // 2 + 1)

    def base(i):
        return i if i < 4 else (2 * (i % 2) if i < SMALL else 0)

    def row(i):
        return S[:, :, :].rearrange("p b c -> p (b c)")[:, base(i) * BANK:base(i) * BANK + width(i)]

    def probs_at(i):
        return (i % 4) * (T // 2) if i < SMALL else (i % 2) * T

    def pair_at(j):
        return 0 if j % 2 == 0 else TILES - 2

    with ExitStack() as ctx:
        def sb(n, shape, dt=F32):
            return ctx.enter_context(nc.sbuf_tensor("l0_" + n, shape, dt))

        def sem(n):
            return core.ctx.enter_context(nc.semaphore("l0_" + n))

        zero = sb("zero", [P, 1])
        w_raw = sb("w_raw", [P, KT, QKV])
        w_hi, w_lo = sb("w_hi", [P, KT, QKV], F32R), sb("w_lo", [P, KT, QKV], F32R)
        wo_raw = sb("wo_raw", [P, D])
        wo_hi, wo_lo = sb("wo_hi", [P, D], F32R), sb("wo_lo", [P, D], F32R)
        cos, sin = sb("cos", [P, TILES, HALF]), sb("sin", [P, TILES, HALF])
        mask = sb("mask", [P, 2, 2 * P], BF16)
        ident16 = sb("ident16", [P, P], BF16)
        rotated, crossed = sb("rotated", [P, 4, 2, 2, HALF]), sb("crossed", [P, 4, 2, 2, HALF])
        qk_hi, qk_lo = sb("qk_hi", [P, 2, T], F32R), sb("qk_lo", [P, 2, T], F32R)
        v_raw = sb("v_raw", [P, 4, HD])
        v_hi, v_lo = sb("v_hi", [P, TILES, HD], F32R), sb("v_lo", [P, TILES, HD], F32R)
        probs = sb("probs", [P, 2 * T])
        pT_hi, pT_lo = (sb(n, [P, 2 * TILES - 2, 2 * P], F32R) for n in ("pT_hi", "pT_lo"))
        a_hi, a_lo = sb("a_hi", [P, 2 * P], F32R), sb("a_lo", [P, 2 * P], F32R)
        part_max, neg_max = sb("part_max", [P, TILES, 2]), sb("neg_max", [P, TILES])
        row_sum, row_inv = sb("row_sum", [P, TILES]), sb("row_inv", [P, TILES])
        mask32 = probs[:, 0:4 * P]

        consts_in, consts_cast, w_in, wo_in, w_split, wo_split, w_hi_done, wo_hi_done = (sem(n) for n in (
            "consts_in", "consts_cast", "w_in", "wo_in", "w_split", "wo_split", "w_hi_done", "wo_hi_done"))
        zeroed = sem("zeroed")
        tile_projected, tile_multiplied, tile_rotated, qk_turned, v_out, v_low_done, qk_hi_done = (sem(n) for n in (
            "tile_projected", "tile_multiplied", "tile_rotated", "qk_turned", "v_out", "v_low_done", "qk_hi_done"))
        chunk_scored, part_max_done, neg_max_done, row_exped, row_turned, pT_hi_done, tp_free = (sem(n) for n in (
            "chunk_scored", "part_max_done", "neg_max_done", "row_exped", "row_turned", "pT_hi_done", "tp_free"))
        pair_mixed, a_hi_done, a_lo_done, pair_out, inv_done = (sem(n) for n in (
            "pair_mixed", "a_hi_done", "a_lo_done", "pair_out", "inv_done"))
        block = ctx.enter_context(nc.Block())

        @block.sync
        def _(sp):
            sp.dma_start(w_raw[:, :, :], wqkv[0, :, :, :]).then_inc(w_in, 16)
            for n, to in (("cos", cos[:, :, :].rearrange("p t c -> p (t c)")),
                          ("sin", sin[:, :, :].rearrange("p t c -> p (t c)")), ("causal", mask32)):
                sp.dma_start(to, consts[:, CONST[n][0]:CONST[n][1]]).then_inc(consts_in, 16)
            sp.dma_start(wo_raw[:, :], wo[0, :, :]).then_inc(wo_in, 16)
            with sp.Fori(1, H0) as h:
                sp.wait_ge(w_split, at(h, 1, 0))
                sp.dma_start(w_raw[:, :, :], wqkv[h, :, :, :]).then_inc(w_in, 16)
                sp.wait_ge(wo_split, at(h, 1, 0))
                sp.dma_start(wo_raw[:, :], wo[h, :, :]).then_inc(wo_in, 16)

        @block.gpsimd
        def _(pool):
            pool.memset(zero[:, :], 0.0).then_inc(zeroed, 1)
            pool.wait_ge(zeroed, 1)
            with pool.Fori(0, H0) as h:

                def v_low(u):
                    pool.wait_ge(v_out, at(h, TILES, 2 * u + 2))
                    two, raw = slice(2 * u, 2 * u + 2), slice(2 * u % 4, 2 * u % 4 + 2)
                    pool.tensor_tensor(v_lo[:, two, :], v_raw[:, raw, :], v_hi[:, two, :].bitcast(F32),
                                       ALU.subtract).then_inc(v_low_done, 1)

                pool.wait_ge(w_in, at(h, 16, 16))
                pool.tensor_tensor(w_hi[:, :, :], w_raw[:, :, :], zero[:, :].unsqueeze(2).to_broadcast([P, KT, QKV]), ALU.add).then_inc(w_hi_done, 1)
                pool.wait_ge(w_hi_done, at(h, 1, 1))
                pool.tensor_tensor(w_lo[:, :, :], w_raw[:, :, :], w_hi[:, :, :].bitcast(F32),
                                   ALU.subtract).then_inc(w_split, 1)
                for t in range(TILES):
                    pool.wait_ge(tile_multiplied, at(h, TILES, t + 1))
                    for a, sign in ((0, ALU.subtract), (1, ALU.add)):
                        last = pool.tensor_tensor(rotated[:, t % 4, :, a, :], rotated[:, t % 4, :, a, :],
                                                  crossed[:, t % 4, :, 1 - a, :], sign)
                    last.then_inc(tile_rotated, 1)
                    if t % 2 == 1 and t >= 3:
                        v_low(t // 2 - 1)
                v_low(PAIRS - 1)
                pool.wait_ge(wo_in, at(h, 16, 16))
                pool.tensor_tensor(wo_hi[:, :], wo_raw[:, :], zero[:, :].to_broadcast([P, D]), ALU.add).then_inc(wo_hi_done, 1)
                pool.wait_ge(wo_hi_done, at(h, 1, 1))
                pool.tensor_tensor(wo_lo[:, :], wo_raw[:, :], wo_hi[:, :].bitcast(F32),
                                   ALU.subtract).then_inc(wo_split, 1)

        @block.tensor
        def _(pe):
            pe.wait_ge(consts_cast, 2)
            with pe.Fori(0, H0) as h:

                def project(t):
                    if t >= 4:
                        pe.wait_ge(v_out, at(h, TILES, t - 3))
                    toks = slice(t * P, (t + 1) * P)
                    parts = [(x, w, k) for k in range(KT) for x, w in ((xT_hi, w_hi), (xT_hi, w_lo), (xT_lo, w_hi))]
                    for n, (x, w, k) in enumerate(parts):
                        last = pe.matmul(S[:, t % 4, 0:QKV], x[:, k, toks], w[:, k, :],
                                         start=(n == 0), stop=(n == len(parts) - 1))
                    last.then_inc(tile_projected, 1)

                def turn(g):
                    n = number["turn", g]
                    pe.wait_ge(tile_rotated, at(h, TILES, 2 * g + 2))
                    if n >= 3:
                        pe.wait_ge(tp_free, at(h, FREED, n - 2))
                    for q in range(2):
                        for j in range(2):
                            last = pe.transpose(TP[:, n % 3, (2 * q + j) * P:(2 * q + j + 1) * P],
                                                rotated[:, (2 * g + j) % 4, q, :, :].rearrange("p a c -> p (a c)"), ident[:, :])
                    last.then_inc(qk_turned, 1)

                def scores(i):
                    n = ROW_GROUPS[i]
                    if i < 4:
                        pe.wait_ge(v_out, at(h, TILES, TILES - 3 + i))
                    elif i < SMALL:
                        pe.wait_ge(row_exped, at(h, TILES, 2 * (i - 3) if i < 6 else i - 1))
                    else:
                        pe.wait_ge(row_exped, at(h, TILES, i))
                    if i % 2 == 0:
                        pe.wait_ge(tp_free, at(h, FREED, number["turn", i // 2] + 1))
                    q = slice(i * P, (i + 1) * P)
                    for c in range(n):
                        w = min(BANK, width(i) - c * BANK)
                        out = S[:, base(i) + c, 0:w]
                        keys = slice(c * BANK, c * BANK + w)
                        final = c == n - 1
                        pe.matmul(out, qk_hi[:, 0, q], qk_hi[:, 1, keys], start=True, stop=False)
                        pe.matmul(out, qk_hi[:, 0, q], qk_lo[:, 1, keys], start=False, stop=False)
                        last = pe.matmul(out, qk_lo[:, 0, q], qk_hi[:, 1, keys], start=False, stop=not final)
                        if final:
                            last = pe.matmul(out[:, w - 2 * P:w], ident16[:, :], mask[:, i % 2, :],
                                             start=False, stop=True)
                        last.then_inc(chunk_scored, 1)

                def turn_row(i, g):
                    n = number["row", i, g]
                    if g == 0:
                        pe.wait_ge(row_exped, at(h, TILES, i + 1))
                    pe.wait_ge(tp_free, at(h, FREED, n - 2))
                    for b in range(4 * g, min(4 * g + 4, width(i) // P)):
                        last = pe.transpose(TP[:, n % 3, (b % 4) * P:(b % 4 + 1) * P],
                                            probs[:, probs_at(i) + b * P:probs_at(i) + (b + 1) * P], ident[:, :])
                    last.then_inc(row_turned, 1)

                def mix(j, first, end):
                    pe.wait_ge(tp_free, at(h, FREED, number["row", 2 * j + 1, (end - 1) // 4] + 1))
                    if j == 0:
                        pe.wait_ge(v_low_done, at(h, PAIRS, PAIRS))
                    if first == 0 and j >= 1:
                        pe.wait_ge(a_lo_done, at(h, PAIRS, j))
                    for k in range(first, end):
                        hi, lo = pT_hi[:, pair_at(j) + k, :], pT_lo[:, pair_at(j) + k, :]
                        pe.matmul(PV[:, 0:2 * P], v_hi[:, k, :], hi, start=(k == 0), stop=False)
                        pe.matmul(PV[:, 0:2 * P], v_hi[:, k, :], lo, start=False, stop=False)
                        last = pe.matmul(PV[:, 0:2 * P], v_lo[:, k, :], hi, start=False, stop=(k == 2 * j + 1))
                    if end == 2 * j + 2:
                        last.then_inc(pair_mixed, 1)

                def out_projection(j):
                    n = number["out", j]
                    pe.wait_ge(tp_free, at(h, FREED, n - 2))
                    pe.wait_ge(a_lo_done, at(h, PAIRS, j + 1))
                    pe.wait_ge(wo_split, at(h, 1, 1))
                    for q in range(2):
                        out = TP[:, n % 3, q * D:(q + 1) * D]
                        toks = slice(q * P, (q + 1) * P)
                        pe.matmul(out, a_hi[:, toks], wo_hi[:, :], start=True, stop=False)
                        pe.matmul(out, a_hi[:, toks], wo_lo[:, :], start=False, stop=False)
                        last = pe.matmul(out, a_lo[:, toks], wo_hi[:, :], start=False, stop=True)
                    last.then_inc(pair_out, 1)

                pe.wait_ge(w_split, at(h, 1, 1))
                for what, *which in TENSOR:
                    if what == "project":
                        project(*which)
                    elif what == "turn":
                        turn(*which)
                    elif what == "scores":
                        scores(*which)
                    elif what == "row":
                        turn_row(*which)
                    elif what == "mix":
                        mix(*which)
                    else:
                        out_projection(*which)

        @block.scalar
        def _(act):
            with act.Fori(0, H0) as h:

                def v_leaves(t):
                    act.wait_ge(tile_multiplied, at(h, TILES, t + 1))
                    if t >= 4:
                        act.wait_ge(v_low_done, at(h, PAIRS, t // 2 - 1))
                    act.activation(v_raw[:, t % 4, :], S[:, t % 4, 2 * HD:QKV], ACT.Copy)
                    act.activation(v_hi[:, t, :], S[:, t % 4, 2 * HD:QKV], ACT.Copy).then_inc(v_out, 1)

                def qk_high(g):
                    n = number["turn", g]
                    act.wait_ge(qk_turned, at(h, TURN, g + 1))
                    act.activation(qk_hi[:, :, 2 * P * g:2 * P * (g + 1)],
                                   TP[:, n % 3, :].rearrange("p (q c) -> p q c", q=2), ACT.Copy).then_inc(qk_hi_done, 1)

                def exponentials(i):
                    act.wait_ge(neg_max_done, at(h, TILES, i + 1))
                    if i >= 4:
                        held = i - 4 if i < SMALL else (i - 2 if i >= SMALL + 2 else (5, 7)[i - SMALL])
                        act.wait_ge(row_turned, at(h, CHUNKS, chunk_at[held] + ROW_GROUPS[held]))
                    act.activation(probs[:, probs_at(i):probs_at(i) + width(i)], row(i), ACT.Exp, bias=neg_max[:, i:i + 1],
                                   scale=SCALE0, accum_out=row_sum[:, i:i + 1]).then_inc(row_exped, 1)

                def row_high(i, g):
                    n = number["row", i, g]
                    m = min(4, width(i) // P - 4 * g)
                    act.wait_ge(row_turned, at(h, CHUNKS, chunk_at[i] + g + 1))
                    to = pair_at(i // 2) + 4 * g
                    act.activation(pT_hi[:, to:to + m, (i % 2) * P:(i % 2 + 1) * P],
                                   TP[:, n % 3, 0:m * P].rearrange("p (b c) -> p b c", c=P),
                                   ACT.Copy).then_inc(pT_hi_done, 1)

                def pair_high(j):
                    act.wait_ge(pair_mixed, at(h, PAIRS, j + 1))
                    if j >= 1:
                        act.wait_ge(pair_out, at(h, PAIRS, j))
                    act.activation(a_hi[:, :], PV[:, 0:2 * P], ACT.Copy).then_inc(a_hi_done, 1)

                for what, *which in SCALAR:
                    if what == "project":
                        v_leaves(*which)
                    elif what == "turn":
                        qk_high(*which)
                    elif what == "scores":
                        exponentials(*which)
                    elif what == "row":
                        row_high(*which)
                    else:
                        pair_high(*which)

        @block.vector
        def _(dve):
            dve.wait_ge(consts_in, 3 * 16)
            dve.tensor_copy(mask[:, :, :], mask32.rearrange("p (a c) -> p a c", a=2)).then_inc(consts_cast, 1)
            dve.tensor_copy(ident16[:, :], ident[:, :]).then_inc(consts_cast, 1)
            with dve.Fori(0, H0) as h:

                def multiply(t):
                    dve.wait_ge(tile_projected, at(h, TILES, t + 1))
                    if t >= 4:
                        dve.wait_ge(qk_turned, at(h, TURN, t // 2 - 1))
                    qk = S[:, t % 4, 0:2 * HD].rearrange("p (b c) -> p b c", c=HALF)
                    for to, by in ((rotated, cos), (crossed, sin)):
                        last = dve.tensor_tensor(to[:, t % 4, :, :, :].rearrange("p q a c -> p (q a) c"), qk,
                                                 by[:, t, :].unsqueeze(1).to_broadcast([P, 4, HALF]), ALU.mult)
                    last.then_inc(tile_multiplied, 1)

                def qk_low(g):
                    n = number["turn", g]
                    dve.wait_ge(qk_hi_done, at(h, TURN, g + 1))
                    cols = slice(2 * P * g, 2 * P * (g + 1))
                    dve.tensor_tensor(qk_lo[:, :, cols], TP[:, n % 3, :].rearrange("p (q c) -> p q c", q=2),
                                      qk_hi[:, :, cols].bitcast(F32), ALU.subtract).then_inc(tp_free, 1)

                PARTS = sum(1 + (n > 1) for n in ROW_GROUPS)

                def maximum(i):
                    n, r = ROW_GROUPS[i], row(i)
                    cut = (0, 1, 2, 2)[n - 1]
                    parts = sum(1 + (m > 1) for m in ROW_GROUPS[:i + 1])
                    if n > 1:
                        dve.wait_ge(chunk_scored, at(h, CHUNKS, chunk_at[i] + cut))
                        dve.tensor_reduce(part_max[:, i, 0:1], r[:, 0:cut * BANK], AX.X, ALU.max).then_inc(part_max_done, 1)
                    dve.wait_ge(chunk_scored, at(h, CHUNKS, chunk_at[i] + n))
                    dve.tensor_reduce(part_max[:, i, 1:2], r[:, cut * BANK:width(i)], AX.X, ALU.max).then_inc(part_max_done, 1)
                    dve.wait_ge(part_max_done, at(h, PARTS, parts))
                    dve.tensor_scalar(neg_max[:, i:i + 1], part_max[:, i, 1:2],
                                      part_max[:, i, 0:1] if n > 1 else -3.4e38, -SCALE0,
                                      ALU.max, ALU.mult).then_inc(neg_max_done, 1)

                def row_low(i, g):
                    n = number["row", i, g]
                    m = min(4, width(i) // P - 4 * g)
                    dve.wait_ge(pT_hi_done, at(h, CHUNKS, chunk_at[i] + g + 1))
                    to = (slice(pair_at(i // 2) + 4 * g, pair_at(i // 2) + 4 * g + m), slice((i % 2) * P, (i % 2 + 1) * P))
                    dve.tensor_tensor(pT_lo[:, to[0], to[1]], TP[:, n % 3, 0:m * P].rearrange("p (b c) -> p b c", c=P),
                                      pT_hi[:, to[0], to[1]].bitcast(F32), ALU.subtract).then_inc(tp_free, 1)

                def pair_low(j):
                    dve.wait_ge(a_hi_done, at(h, PAIRS, j + 1))
                    dve.tensor_tensor(a_lo[:, :], PV[:, 0:2 * P], a_hi[:, :].bitcast(F32),
                                      ALU.subtract).then_inc(a_lo_done, 1)
                    dve.reciprocal(row_inv[:, 2 * j:2 * j + 2], row_sum[:, 2 * j:2 * j + 2]).then_inc(inv_done, 1)

                def accumulate(j):
                    n = number["out", j]
                    dve.wait_ge(pair_out, at(h, PAIRS, j + 1))
                    dve.wait_ge(inv_done, at(h, PAIRS, j + 1))
                    for q in range(2):
                        i = 2 * j + q
                        last = dve.scalar_tensor_tensor(out=Y[:, i, :], in0=TP[:, n % 3, q * D:(q + 1) * D],
                                                        scalar=row_inv[:, i:i + 1], in1=Y[:, i, :],
                                                        op0=ALU.mult, op1=ALU.add)
                    last.then_inc(tp_free, 1)

                for what, *which in VECTOR:
                    if what == "project":
                        multiply(*which)
                    elif what == "turn":
                        qk_low(*which)
                    elif what == "scores":
                        maximum(*which)
                    elif what == "row":
                        row_low(*which)
                    elif what == "mix":
                        pair_low(*which)
                    else:
                        accumulate(*which)


def ball_projection(nc, core, weight, scale, xT_hi, xT_lo):
    Y, TP = core.Y, core.TP
    with ExitStack() as ctx:
        def sb(n, shape, dt=F32):
            return ctx.enter_context(nc.sbuf_tensor("ball_" + n, shape, dt))

        def sem(n):
            return core.ctx.enter_context(nc.semaphore("ball_" + n))

        w_raw, w_hi, w_lo = sb("w_raw", [P, KT, D]), sb("w_hi", [P, KT, D], F32R), sb("w_lo", [P, KT, D], F32R)
        scale_all = sb("scale_all", [P, D])
        out, squares = sb("out", [P, TILES, D]), sb("squares", [P, 2, D])
        sq_sum, norm, v_norm, tanh, den, inv, factor, o_norm, bound = (sb(n, [P, TILES]) for n in (
            "sq_sum", "norm", "v_norm", "tanh", "den", "inv", "factor", "o_norm", "bound"))
        w_in, scale_in, w_hi_done, w_split, pair_done, out_done, squared, rooted, tanh_done, step = (sem(n) for n in (
            "w_in", "scale_in", "w_hi_done", "w_split", "pair_done", "out_done", "squared", "rooted", "tanh_done", "step"))
        block = ctx.enter_context(nc.Block())

        @block.sync
        def _(sp):
            sp.dma_start(w_raw[:, :, :], weight.rearrange("(k p) n -> p k n", p=P)).then_inc(w_in, 16)
            sp.dma_start(scale_all[:, :], scale.partition_broadcast(P)).then_inc(scale_in, 16)

        @block.tensor
        def _(pe):
            pe.wait_ge(w_split, 1)
            for g in range(PAIRS):
                if g >= 3:
                    pe.wait_ge(out_done, g - 2)
                for j in range(2):
                    t = 2 * g + j
                    toks = slice(t * P, (t + 1) * P)
                    parts = [(x, w, k) for k in range(KT) for x, w in ((xT_hi, w_hi), (xT_hi, w_lo), (xT_lo, w_hi))]
                    for n, (x, w, k) in enumerate(parts):
                        last = pe.matmul(TP[:, g % 3, j * D:(j + 1) * D], x[:, k, toks], w[:, k, :],
                                         start=(n == 0), stop=(n == len(parts) - 1))
                last.then_inc(pair_done, 1)

        @block.scalar
        def _(act):
            for t in range(TILES):
                act.wait_ge(out_done, t // 2 + 1)
                if t >= 2:
                    act.wait_ge(squared, t - 1)
                act.activation(squares[:, t % 2, :], out[:, t, :], ACT.Square, accum_out=sq_sum[:, t:t + 1]).then_inc(squared, 1)
            act.wait_ge(squared, TILES)
            act.activation(norm[:, :], sq_sum[:, :], ACT.Sqrt).then_inc(rooted, 1)
            act.wait_ge(step, 1)
            act.activation(tanh[:, :], v_norm[:, :], ACT.Tanh).then_inc(tanh_done, 1)

        @block.vector
        def _(dve):
            dve.wait_ge(w_in, 16)
            dve.tensor_copy(w_hi[:, :, :], w_raw[:, :, :]).then_inc(w_hi_done, 1)
            dve.wait_ge(w_hi_done, 1)
            dve.tensor_tensor(w_lo[:, :, :], w_raw[:, :, :], w_hi[:, :, :].bitcast(F32), ALU.subtract).then_inc(w_split, 1)
            dve.wait_ge(scale_in, 16)
            for g in range(PAIRS):
                dve.wait_ge(pair_done, g + 1)
                dve.tensor_tensor(out[:, 2 * g:2 * g + 2, :], TP[:, g % 3, :].rearrange("p (j n) -> p j n", j=2),
                                  scale_all[:, :].unsqueeze(1).to_broadcast([P, 2, D]), ALU.mult).then_inc(out_done, 1)
            dve.wait_ge(rooted, 1)
            dve.tensor_scalar(v_norm[:, :], norm[:, :], BALL_EPS, None, ALU.max).then_inc(step, 1)
            dve.wait_ge(step, 1)
            dve.tensor_scalar(den[:, :], v_norm[:, :], BALL_EPS, None, ALU.add).then_inc(step, 1)
            dve.wait_ge(step, 2)
            dve.reciprocal(inv[:, :], den[:, :]).then_inc(step, 1)
            dve.wait_ge(step, 3)
            dve.wait_ge(tanh_done, 1)
            dve.tensor_tensor(factor[:, :], tanh[:, :], inv[:, :], ALU.mult).then_inc(step, 1)
            dve.wait_ge(step, 4)
            dve.tensor_tensor(o_norm[:, :], norm[:, :], factor[:, :], ALU.mult).then_inc(step, 1)
            dve.wait_ge(step, 5)
            dve.tensor_scalar(o_norm[:, :], o_norm[:, :], BALL_EPS, None, ALU.max).then_inc(step, 1)
            dve.wait_ge(step, 6)
            dve.reciprocal(bound[:, :], o_norm[:, :]).then_inc(step, 1)
            dve.wait_ge(step, 7)
            dve.tensor_scalar(bound[:, :], bound[:, :], MAX_NORM, 1.0, ALU.mult, ALU.min).then_inc(step, 1)
            dve.wait_ge(step, 8)
            dve.tensor_tensor(factor[:, :], factor[:, :], bound[:, :], ALU.mult).then_inc(step, 1)
            dve.wait_ge(step, 9)
            for t in range(TILES):
                dve.scalar_tensor_tensor(out=Y[:, t, :], in0=out[:, t, :], scalar=factor[:, t:t + 1], in1=Y[:, t, :],
                                         op0=ALU.mult, op1=ALU.add)


def window_ring(first, last):
    items = []
    if first:
        items += [("kv", 0), ("kv", 1), ("keys", 0)] + [("queries", 0, r) for r in range(REP)]
    for s in range(TILES + (WINDOW_LAG if last else 0)):
        if has_unit(s - 2, first):
            items += [("probs", s - 2, 0), ("probs", s - 2, 1)]
        items += window_ahead(s, last)
        if has_unit(s - 4, first):
            items.append(("out", s - 4))
    held, ring = [-3, -2, -1], {}
    extra = -len(items) % 3
    skips = {len(items) // 3 * (n + 1) for n in range(extra)} if not last else set()
    bank = 0
    for n, item in enumerate(items):
        if n in skips:
            bank = (bank + 1) % 3
        ring[item] = (n, bank, held[bank])
        held[bank] = n
        bank = (bank + 1) % 3
    return ring


BLOCKS, PER_BLOCK = T // BANK, BANK // P
WINDOW_LAG = 4


def has_unit(t, first):
    return (t >= 0 or not first) and t < TILES


def window_ahead(s, last):
    c, r = s // PER_BLOCK + 1, s % PER_BLOCK
    if s >= TILES or (last and c == BLOCKS):
        return []
    ahead = [[("kv", 2 * c)], [("kv", 2 * c + 1)], [("keys", c)], []][r]
    if c < BLOCKS:
        return ahead + [("queries", c, r)]
    return ahead + [("queries", c, n) for n in ((), (0,), (1,), (2, 3))[r]]


def window_attention(nc, core, consts, wq, wkv, wo, xT_hi, xT_lo):
    Y, ident, S, TP, PV = core.Y, core.ident, core.S, core.TP, core.PV
    QUERIES = BLOCKS * REP
    KEYS = T + P
    PER = 2 * TILES + BLOCKS * REP + PAIRS + BLOCKS + TILES
    RINGS = {(first, last): window_ring(first, last) for first, last in ((True, False), (False, False), (False, True))}
    BEFORE = RINGS[False, False]
    assert len(RINGS[False, False]) == PER and len(RINGS[True, False]) == PER - 1
    with ExitStack() as ctx:
        def sb(n, shape, dt=F32):
            return ctx.enter_context(nc.sbuf_tensor("l1_" + n, shape, dt))

        def sem(n):
            return core.ctx.enter_context(nc.semaphore("l1_" + n))

        wq_raw = sb("wq_raw", [P, KT, REP * HD])
        wq_hi, wq_lo = sb("wq_hi", [P, KT, REP * HD], F32R), sb("wq_lo", [P, KT, REP * HD], F32R)
        wkv_raw = sb("wkv_raw", [P, KT, 2 * HD])
        wkv_hi, wkv_lo = sb("wkv_hi", [P, KT, 2 * HD], F32R), sb("wkv_lo", [P, KT, 2 * HD], F32R)
        wo_raw = sb("wo_raw", [P, REP, D])
        wo_hi, wo_lo = sb("wo_hi", [P, REP, D], F32R), sb("wo_lo", [P, REP, D], F32R)
        mask32, mask = sb("mask32", [P, 4 * P]), sb("mask", [P, 2, 2 * P], BF16)
        ident16 = sb("ident16", [P, P], BF16)
        zero = sb("zero", [P, 1])
        k_nat = sb("k_nat", [P, 4, HD])
        kT_hi, kT_lo = sb("kT_hi", [P, KEYS], F32R), sb("kT_lo", [P, KEYS], F32R)
        v_hi, v_lo = sb("v_hi", [P, TILES + 1, HD], F32R), sb("v_lo", [P, TILES + 1, HD], F32R)
        qT_hi, qT_lo = sb("qT_hi", [P, 2, REP, BANK], F32R), sb("qT_lo", [P, 2, REP, BANK], F32R)
        probs = sb("probs", [P, 4, REP, 2 * P])
        pT_hi, pT_lo = (sb(n, [P, 2, 2, REP, P], F32R) for n in ("pT_hi", "pT_lo"))
        a_hi, a_lo = sb("a_hi", [P, REP, P], F32R), sb("a_lo", [P, REP, P], F32R)
        row_max, neg_max = sb("row_max", [P, TILES, REP]), sb("neg_max", [P, TILES, REP])
        row_sum, row_inv = sb("row_sum", [P, TILES, REP]), sb("row_inv", [P, TILES, REP])

        consts_in, consts_cast, wkv_in, wq_in, wo_in, w_split, padded, part = (sem(n) for n in (
            "consts_in", "consts_cast", "wkv_in", "wq_in", "wo_in", "w_split", "padded", "part"))
        kv_projected, v_hi_done, keys_turned, kT_hi_done, q_projected, qT_hi_done = (sem(n) for n in (
            "kv_projected", "v_hi_done", "keys_turned", "kT_hi_done", "q_projected", "qT_hi_done"))
        scored, max_done, neg_max_done, exped, inv_done, normed, p_turned, pT_hi_done, tp_free = (sem(n) for n in (
            "scored", "max_done", "neg_max_done", "exped", "inv_done", "normed", "p_turned", "pT_hi_done", "tp_free"))
        mixed, a_hi_done, a_lo_done, projected = (sem(n) for n in ("mixed", "a_hi_done", "a_lo_done", "projected"))
        block = ctx.enter_context(nc.Block())

        def freed(h, first, n):
            return n + 1 if first else at(h, PER, n)

        @block.sync
        def _(sp):
            sp.dma_start(wkv_raw[:, :, :], wkv[0, :, :, :]).then_inc(wkv_in, 16)
            sp.dma_start(wq_raw[:, :, :], wq[0, :, :, :]).then_inc(wq_in, 16)
            sp.dma_start(mask32[:, :], consts[:, CONST["window"][0]:CONST["window"][1]]).then_inc(consts_in, 16)
            sp.dma_start(wo_raw[:, :, :], wo[0, :, :, :]).then_inc(wo_in, 16)
            with sp.Fori(1, HKV) as h:
                sp.wait_ge(w_split, at(h, 3, -2))
                sp.dma_start(wkv_raw[:, :, :], wkv[h, :, :, :]).then_inc(wkv_in, 16)
                sp.wait_ge(w_split, at(h, 3, -1))
                sp.dma_start(wq_raw[:, :, :], wq[h, :, :, :]).then_inc(wq_in, 16)
                sp.wait_ge(w_split, at(h, 3, 0))
                sp.dma_start(wo_raw[:, :, :], wo[h, :, :, :]).then_inc(wo_in, 16)

        @block.gpsimd
        def _(pool):
            def split(h, n):
                raw, hi, lo, arrived = ((wkv_raw, wkv_hi, wkv_lo, wkv_in), (wq_raw, wq_hi, wq_lo, wq_in),
                                        (wo_raw, wo_hi, wo_lo, wo_in))[n]
                pool.wait_ge(arrived, at(h, 16, 16))
                pool.tensor_tensor(hi[:, :, :], raw[:, :, :], zero[:, :].unsqueeze(2).to_broadcast(raw.shape), ALU.add).then_inc(part, 1)
                pool.wait_ge(part, at(h, 3, n + 1))
                pool.tensor_tensor(lo[:, :, :], raw[:, :, :], hi[:, :, :].bitcast(F32), ALU.subtract).then_inc(w_split, 1)

            def turn(h, first=False, last=False):
                for t in range(TILES):
                    pool.wait_ge(inv_done, at(h, TILES, t + 1))
                    pool.tensor_tensor(probs[:, t % 4, :, :], probs[:, t % 4, :, :],
                                       row_inv[:, t, :].unsqueeze(2).to_broadcast([P, REP, 2 * P]),
                                       ALU.mult).then_inc(normed, 1)
                    if t == WINDOW_LAG - 1:
                        if not first:
                            pool.wait_ge(projected, at(h, TILES, 0))
                        split(h, 2)
                    if t == 9 and not last:
                        pool.wait_ge(kv_projected, at(h, PAIRS, PAIRS))
                        split(h + 1, 0)
                    if t == 11 and not last:
                        pool.wait_ge(q_projected, at(h, QUERIES, QUERIES))
                        split(h + 1, 1)

            for z in (kT_hi[:, 0:P], kT_lo[:, 0:P], v_hi[:, 0, :], v_lo[:, 0, :]):
                pool.memset(z.bitcast(F32), 0.0).then_inc(padded, 1)
            pool.memset(zero[:, :], 0.0).then_inc(padded, 1)
            pool.wait_ge(padded, 5)
            split(0, 0)
            split(0, 1)
            turn(0, first=True)
            with pool.Fori(1, HKV - 1) as h:
                turn(h)
            turn(HKV - 1, last=True)

        @block.tensor
        def _(pe):
            def turn(h, first=False, last=False):
                ring = RINGS[first, last]

                def bank(item):
                    n, b, held = ring[item]
                    if held >= 0 or not first:
                        pe.wait_ge(tp_free, freed(h, first, held))
                    return TP[:, b, :]

                def project_kv(u):
                    out = bank(("kv", u))
                    pe.wait_ge(w_split, at(h, 3, 4 if u >= PAIRS else 1))
                    for j in range(2):
                        t = (2 * u + j) % TILES
                        toks = slice(t * P, (t + 1) * P)
                        parts = [(x, w, k) for k in range(KT) for x, w in ((xT_hi, wkv_hi), (xT_hi, wkv_lo), (xT_lo, wkv_hi))]
                        for n, (x, w, k) in enumerate(parts):
                            last_product = pe.matmul(out[:, j * 2 * HD:(j + 1) * 2 * HD], x[:, k, toks], w[:, k, :],
                                                     start=(n == 0), stop=(n == len(parts) - 1))
                    last_product.then_inc(kv_projected, 1)

                def turn_keys(c):
                    out = bank(("keys", c))
                    pe.wait_ge(v_hi_done, at(h, PAIRS, 2 * c + 2))
                    for b in range(4):
                        move = pe.transpose(out[:, b * P:(b + 1) * P], k_nat[:, b, :], ident[:, :])
                    move.then_inc(keys_turned, 1)

                def project_q(c, r):
                    out = bank(("queries", c, r))
                    pe.wait_ge(w_split, at(h, 3, 5 if c == BLOCKS else 2))
                    toks = slice((c % BLOCKS) * BANK, (c % BLOCKS + 1) * BANK)
                    parts = [(w, x, k) for k in range(KT) for w, x in ((wq_hi, xT_hi), (wq_hi, xT_lo), (wq_lo, xT_hi))]
                    for n, (w, x, k) in enumerate(parts):
                        last_product = pe.matmul(out, w[:, k, r * HD:(r + 1) * HD], x[:, k, toks],
                                                 start=(n == 0), stop=(n == len(parts) - 1))
                    last_product.then_inc(q_projected, 1)

                def scores(t):
                    if t % PER_BLOCK == 0:
                        if t == 0 and not first:
                            n = BEFORE["queries", BLOCKS, REP - 1][0] - PER
                        else:
                            n = ring["queries", t // PER_BLOCK, REP - 1][0]
                        pe.wait_ge(tp_free, freed(h, first, n))
                    if t >= 2 or not first:
                        pe.wait_ge(exped, at(h, TILES, t - 1))
                    keys = slice(t * P, (t + 2) * P)
                    for r in range(REP):
                        out = S[:, 2 * (t % 2) + r // 2, (r % 2) * 2 * P:(r % 2 + 1) * 2 * P]
                        toks = slice((t % REP) * P, (t % REP + 1) * P)
                        hi, lo = (q[:, (t // PER_BLOCK) % 2, r, toks] for q in (qT_hi, qT_lo))
                        pe.matmul(out, hi, kT_hi[:, keys], start=True, stop=False)
                        pe.matmul(out, hi, kT_lo[:, keys], start=False, stop=False)
                        pe.matmul(out, lo, kT_hi[:, keys], start=False, stop=False)
                        last_product = pe.matmul(out, ident16[:, :], mask[:, min(t, 1), :], start=False, stop=True)
                    last_product.then_inc(scored, 1)

                def turn_probs(t):
                    pe.wait_ge(normed, at(h, TILES, t + 1))
                    for b in range(2):
                        out = bank(("probs", t, b))
                        for r in range(REP):
                            move = pe.transpose(out[:, r * P:(r + 1) * P], probs[:, t % 4, r, b * P:(b + 1) * P], ident[:, :])
                        move.then_inc(p_turned, 1)

                def mix(t):
                    n = ring["probs", t, 1][0] if ("probs", t, 1) in ring else BEFORE["probs", t + TILES, 1][0] - PER
                    pe.wait_ge(tp_free, freed(h, first, n))
                    if t >= 1 or not first:
                        pe.wait_ge(a_lo_done, at(h, TILES, t))
                    for b in range(2):
                        hi, lo = (p[:, t % 2, b, :, :].rearrange("p r c -> p (r c)") for p in (pT_hi, pT_lo))
                        v = t % TILES + b
                        pe.matmul(PV[:, :], v_hi[:, v, :], hi, start=(b == 0), stop=False)
                        pe.matmul(PV[:, :], v_hi[:, v, :], lo, start=False, stop=False)
                        last_product = pe.matmul(PV[:, :], v_lo[:, v, :], hi, start=False, stop=(b == 1))
                    last_product.then_inc(mixed, 1)

                def project(t):
                    out = bank(("out", t))[:, 0:D]
                    pe.wait_ge(a_lo_done, at(h, TILES, t + 1))
                    pe.wait_ge(w_split, at(h, 3, 3 if t >= 0 else 0))
                    for r in range(REP):
                        pe.matmul(out, a_hi[:, r, :], wo_hi[:, r, :], start=(r == 0), stop=False)
                        pe.matmul(out, a_hi[:, r, :], wo_lo[:, r, :], start=False, stop=False)
                        last_product = pe.matmul(out, a_lo[:, r, :], wo_hi[:, r, :], start=False, stop=(r == REP - 1))
                    last_product.then_inc(projected, 1)

                if first:
                    project_kv(0)
                    project_kv(1)
                    turn_keys(0)
                    for r in range(REP):
                        project_q(0, r)
                for s in range(TILES + (WINDOW_LAG if last else 0)):
                    if s < TILES:
                        scores(s)
                    if has_unit(s - 2, first):
                        turn_probs(s - 2)
                    for what, *which in window_ahead(s, last):
                        {"kv": project_kv, "keys": turn_keys, "queries": project_q}[what](*which)
                    if has_unit(s - 3, first):
                        mix(s - 3)
                    if has_unit(s - 4, first):
                        project(s - 4)

            pe.wait_ge(consts_cast, 2)
            pe.wait_ge(padded, 4)
            turn(0, first=True)
            with pe.Fori(1, HKV - 1) as h:
                turn(h)
            turn(HKV - 1, last=True)

        @block.scalar
        def _(act):
            def turn(h, first=False, last=False):
                ring = RINGS[first, last]

                def kv_out(u):
                    pair = TP[:, ring["kv", u][1], :].rearrange("p (j c) -> p j c", j=2)
                    act.wait_ge(kv_projected, at(h, PAIRS, u + 1))
                    if u >= 2:
                        act.wait_ge(keys_turned, at(h, BLOCKS, u // 2))
                    act.activation(k_nat[:, 2 * u % 4:2 * u % 4 + 2, :], pair[:, :, 0:HD], ACT.Copy)
                    t = 2 * u % TILES + 1
                    act.activation(v_hi[:, t:t + 2, :], pair[:, :, HD:2 * HD], ACT.Copy).then_inc(v_hi_done, 1)

                def keys_high(c):
                    act.wait_ge(keys_turned, at(h, BLOCKS, c + 1))
                    to = P + (c % BLOCKS) * BANK
                    act.activation(kT_hi[:, to:to + BANK], TP[:, ring["keys", c][1], :], ACT.Copy).then_inc(kT_hi_done, 1)

                def queries_high(c, r):
                    act.wait_ge(q_projected, at(h, QUERIES, REP * c + r + 1))
                    act.activation(qT_hi[:, c % 2, r, :], TP[:, ring["queries", c, r][1], :], ACT.Copy).then_inc(qT_hi_done, 1)

                if first:
                    kv_out(0)
                    kv_out(1)
                    keys_high(0)
                    for r in range(REP):
                        queries_high(0, r)
                for s in range(TILES + (WINDOW_LAG if last else 0)):
                    if has_unit(s - 2, first):
                        t = s - 2
                        for b in range(2):
                            act.wait_ge(p_turned, at(h, 2 * TILES, 2 * t + b + 1))
                            act.activation(pT_hi[:, t % 2, b, :, :],
                                           TP[:, ring["probs", t, b][1], :].rearrange("p (r c) -> p r c", r=REP),
                                           ACT.Copy).then_inc(pT_hi_done, 1)
                    if s < TILES:
                        act.wait_ge(neg_max_done, at(h, TILES, s + 1))
                        if s >= 4 or not first:
                            act.wait_ge(p_turned, at(h, 2 * TILES, 2 * (s - 4) + 2))
                        for r in range(REP):
                            last_row = act.activation(probs[:, s % 4, r, :], S[:, 2 * (s % 2) + r // 2, (r % 2) * 2 * P:(r % 2 + 1) * 2 * P],
                                                      ACT.Exp, bias=neg_max[:, s, r:r + 1], scale=SCALE1,
                                                      accum_out=row_sum[:, s, r:r + 1])
                        last_row.then_inc(exped, 1)
                    for what, *which in window_ahead(s, last):
                        {"kv": kv_out, "keys": keys_high, "queries": queries_high}[what](*which)
                    if has_unit(s - 3, first):
                        t = s - 3
                        act.wait_ge(mixed, at(h, TILES, t + 1))
                        if t >= 1 or not first:
                            act.wait_ge(projected, at(h, TILES, t))
                        act.activation(a_hi[:, :, :], PV[:, :].rearrange("p (r c) -> p r c", r=REP), ACT.Copy).then_inc(a_hi_done, 1)

            turn(0, first=True)
            with act.Fori(1, HKV - 1) as h:
                turn(h)
            turn(HKV - 1, last=True)

        @block.vector
        def _(dve):
            def turn(h, first=False, last=False):
                ring = RINGS[first, last]

                def values_low(u):
                    pair = TP[:, ring["kv", u][1], :].rearrange("p (j c) -> p j c", j=2)
                    t = 2 * u % TILES + 1
                    dve.wait_ge(v_hi_done, at(h, PAIRS, u + 1))
                    dve.tensor_tensor(v_lo[:, t:t + 2, :], pair[:, :, HD:2 * HD], v_hi[:, t:t + 2, :].bitcast(F32),
                                      ALU.subtract).then_inc(tp_free, 1)

                def keys_low(c):
                    cols = slice(P + (c % BLOCKS) * BANK, P + (c % BLOCKS + 1) * BANK)
                    dve.wait_ge(kT_hi_done, at(h, BLOCKS, c + 1))
                    dve.tensor_tensor(kT_lo[:, cols], TP[:, ring["keys", c][1], :], kT_hi[:, cols].bitcast(F32),
                                      ALU.subtract).then_inc(tp_free, 1)

                def queries_low(c, r):
                    dve.wait_ge(qT_hi_done, at(h, QUERIES, REP * c + r + 1))
                    dve.tensor_tensor(qT_lo[:, c % 2, r, :], TP[:, ring["queries", c, r][1], :], qT_hi[:, c % 2, r, :].bitcast(F32),
                                      ALU.subtract).then_inc(tp_free, 1)

                if first:
                    values_low(0)
                    values_low(1)
                    keys_low(0)
                    for r in range(REP):
                        queries_low(0, r)
                for s in range(TILES + (WINDOW_LAG if last else 0)):
                    if s < TILES:
                        dve.wait_ge(scored, at(h, TILES, s + 1))
                        dve.tensor_reduce(row_max[:, s, :], S[:, 2 * (s % 2):2 * (s % 2) + 2, :].rearrange("p b (r c) -> p (b r) c", r=2),
                                          AX.X, ALU.max).then_inc(max_done, 1)
                        dve.wait_ge(max_done, at(h, TILES, s + 1))
                        dve.tensor_scalar(neg_max[:, s, :], row_max[:, s, :], -SCALE1, None, ALU.mult).then_inc(neg_max_done, 1)
                    if has_unit(s - 2, first):
                        t = s - 2
                        for b in range(2):
                            dve.wait_ge(pT_hi_done, at(h, 2 * TILES, 2 * t + b + 1))
                            low = dve.tensor_tensor(pT_lo[:, t % 2, b, :, :],
                                                    TP[:, ring["probs", t, b][1], :].rearrange("p (r c) -> p r c", r=REP),
                                                    pT_hi[:, t % 2, b, :, :].bitcast(F32), ALU.subtract)
                            low.then_inc(tp_free, 1)
                    for what, *which in window_ahead(s, last):
                        {"kv": values_low, "keys": keys_low, "queries": queries_low}[what](*which)
                    if has_unit(s - 3, first):
                        dve.wait_ge(a_hi_done, at(h, TILES, s - 3 + 1))
                        dve.tensor_tensor(a_lo[:, :, :], PV[:, :].rearrange("p (r c) -> p r c", r=REP), a_hi[:, :, :].bitcast(F32),
                                          ALU.subtract).then_inc(a_lo_done, 1)
                    if has_unit(s - 4, first):
                        t = s - 4
                        dve.wait_ge(projected, at(h, TILES, t + 1))
                        dve.tensor_tensor(Y[:, t % TILES, :], TP[:, ring["out", t][1], 0:D], Y[:, t % TILES, :], ALU.add).then_inc(tp_free, 1)
                    if s < TILES:
                        dve.wait_ge(exped, at(h, TILES, s + 1))
                        dve.reciprocal(row_inv[:, s, :], row_sum[:, s, :]).then_inc(inv_done, 1)

            dve.wait_ge(consts_in, 16)
            dve.tensor_copy(mask[:, :, :], mask32[:, :].rearrange("p (a c) -> p a c", a=2)).then_inc(consts_cast, 1)
            dve.tensor_copy(ident16[:, :], ident[:, :]).then_inc(consts_cast, 1)
            turn(0, first=True)
            with dve.Fori(1, HKV - 1) as h:
                turn(h)
            turn(HKV - 1, last=True)


def expert_mix(nc, core, consts, gate_w, sw_gu, sw_down, w_gu, w_down, xT, x_rows, routed):
    Y, ident, S, TP, PV = core.Y, core.ident, core.S, core.TP, core.PV
    HALF_I = INNER // 2
    PIECES = INNER_S // HALF_I
    RING = 4
    NOWHERE = 4096.0
    INFO = 6

    def first(i):
        return isinstance(i, int) and i == 0

    def in_range(i, u, back):
        return not isinstance(i, int) or 0 <= RING * i + u - back < E

    with ExitStack() as ctx:
        def sb(n, shape, dt=F32):
            return ctx.enter_context(nc.sbuf_tensor("moe_" + n, shape, dt))

        def sem(n):
            return core.ctx.enter_context(nc.semaphore("moe_" + n))

        iota, before, lower, where = sb("iota", [P, P]), sb("before", [P, P]), sb("lower", [P, E * E]), sb("where", [P, 2, TILES])
        before16, ones16, lower16 = sb("before16", [P, P], BF16), sb("ones16", [P, P], BF16), sb("lower16", [P, E, E], BF16)
        gw = sb("gw", [P, KT, E])
        sgu, sdown = sb("sgu", [P, KT, 2 * INNER_S]), sb("sdown", [HALF_I, PIECES, D])
        wgu, wdown = sb("wgu", [P, RING, KT, 2 * INNER]), sb("wdown", [HALF_I, RING, 2, D])
        zeros = sb("zeros", [P, TILES // 2 * D])
        top, total, total_inv, gain_sum, gain_inv = (sb(n, [P, TILES]) for n in ("top", "total", "total_inv", "gain_sum", "gain_inv"))
        shifted, exps, score, above, chosen, gain, rest, slot = (sb(n, [P, TILES, E]) for n in (
            "shifted", "exps", "score", "above", "chosen", "gain", "rest", "slot"))
        greater, equal = sb("greater", [P, TILES, E, E], BF16), sb("equal", [P, TILES, E, E], BF16)
        chosen16, info = sb("chosen16", [P, TILES, E], BF16), sb("info", [P, TILES, E, INFO], BF16)
        onehot = sb("onehot", [P, 2, TILES, P], BF16)
        slots = sb("slots", [P, E, INFO])
        token_a, token_b, token = sb("token_a", [P, E]), sb("token_b", [P, E]), sb("token", [P, E], mybir.dt.uint32)
        slot_gain_a, slot_gain = sb("slot_gain_a", [P, E]), sb("slot_gain", [P, E])
        s_act, s_mid = sb("s_act", [P, 2, INNER_S]), sb("s_mid", [P, 2, INNER_S])
        s_midT = sb("s_midT", [HALF_I, 2, PIECES, P])
        xg, xgT = sb("xg", [P, RING, D]), sb("xgT", [P, 2, KT, P])
        e_act, e_mid = sb("e_act", [P, 2, INNER]), sb("e_mid", [P, 2, INNER])
        e_midT, e_out = sb("e_midT", [HALF_I, 2, 2, P]), sb("e_out", [P, 2, D])
        y_routed = sb("y_routed", [P, TILES, D])

        consts_in, gw_in, shared_in, consts_cast, zeroed, cleared, out_free, ring_set = (sem(n) for n in (
            "consts_in", "gw_in", "shared_in", "consts_cast", "zeroed", "cleared", "out_free", "ring_set"))
        weights_in = [sem(f"weights_in{n}") for n in range(RING)]
        gathered = [sem(f"gathered{n}") for n in range(RING)]
        logits_done, shift_done, exps_done, route, rank_done, onehot_done, info_done = (sem(n) for n in (
            "logits_done", "shift_done", "exps_done", "route", "rank_done", "onehot_done", "info_done"))
        s_up_done, s_act_done, s_mixed, s_turned, s_midT_done, s_down_done, s_added = (sem("s_" + n) for n in (
            "up_done", "act_done", "mixed", "turned", "midT_done", "down_done", "added"))
        x_turned, xgT_done, up_done, act_done, mixed, turned, midT_done, down_done, out_done = (sem("e_" + n) for n in (
            "x_turned", "xgT_done", "up_done", "act_done", "mixed", "turned", "midT_done", "down_done", "out_done"))
        added = [sem(f"added{n}") for n in range(2)]
        y_in = [sem(f"y_in{n}") for n in range(4)]
        block = ctx.enter_context(nc.Block())

        ROUTE = {n: k + 1 for k, n in enumerate((
            "top", "total", "total_inv", "score", "greater", "equal", "equal_lower", "greater_equal", "above", "chosen", "chosen16",
            "gain_raw", "gain_sum", "gain_eps", "gain_inv", "gain", "high", "high_rest", "middle", "middle_rest", "low",
            "numbers", "tiles", "ones", "away", "slot",
            "slots", "token_a", "token_b", "token", "gain_a", "slot_gain"))}

        @block.sync
        def _(sp):
            for n, to in (("iota", iota[:, :]), ("before", before[:, :]), ("lower", lower[:, :]),
                          ("where", where[:, :, :].rearrange("p a t -> p (a t)"))):
                sp.dma_start(to, consts[:, CONST[n][0]:CONST[n][1]]).then_inc(consts_in, 16)
            sp.dma_start(gw[:, :, :], gate_w).then_inc(gw_in, 16)
            sp.dma_start(sgu[:, :, :], sw_gu).then_inc(shared_in, 16)
            sp.dma_start(sdown[:, :, :], sw_down).then_inc(shared_in, 16)
            sp.wait_ge(zeroed, 1)
            for n in range(2):
                sp.dma_start(rows(routed)[:, n * TILES // 2:(n + 1) * TILES // 2, :],
                             zeros[:, :].rearrange("p (t d) -> p t d", d=D)).then_inc(cleared, 16)

            for u in range(RING):
                sp.dma_start(wgu[:, u, :, :], w_gu[u, :, :, :]).then_inc(weights_in[u], 16)
                sp.dma_start(wdown[:, u, :, :], w_down[u, :, :, :]).then_inc(weights_in[u], 16)
            with sp.Fori(1, E // RING) as i:
                for u in range(RING):
                    sp.wait_ge(up_done, at(i, RING, u - RING + 1))
                    sp.dma_start(wgu[:, u, :, :], w_gu[RING * i + u, :, :, :]).then_inc(weights_in[u], 16)
                    sp.wait_ge(down_done, at(i, RING, u - RING + 1))
                    sp.dma_start(wdown[:, u, :, :], w_down[RING * i + u, :, :, :]).then_inc(weights_in[u], 16)
            for n in range(2):
                sp.wait_ge(added[n], 16 * E // 2)
            for n in range(4):
                sp.dma_start(y_routed[:, 4 * n:4 * n + 4, :], rows(routed)[:, 4 * n:4 * n + 4, :]).then_inc(y_in[n], 16)

        @block.gpsimd
        def _(pool):
            pool.memset(zeros[:, :], 0.0).then_inc(zeroed, 1)
            pool.memset(xg[:, :, :], 0.0).then_inc(ring_set, 1)
            pool.sem_inc(out_free, 1)
            pool.wait_ge(ring_set, 1)
            pool.wait_ge(cleared, 32)

            def gather(e):
                if e >= RING:
                    pool.wait_ge(x_turned, e - RING + 1)
                pool.indirect_dma_start(xg[:, e % RING, :], None, x_rows, bass.IndirectOffsetOnAxis(ap=token[:, e:e + 1], axis=0),
                                        bounds_check=T - 1, oob_is_err=False).then_inc(gathered[e % RING], 16)

            def scatter(e):
                pool.wait_ge(out_done, e + 1)
                if e >= 1:
                    pool.wait_ge(added[(e - 1) % 2], 16 * ((e - 1) // 2 + 1))
                    pool.sem_inc(out_free, 1)
                pool.indirect_dma_start(routed, bass.IndirectOffsetOnAxis(ap=token[:, e:e + 1], axis=0), e_out[:, e % 2, :], None,
                                        bounds_check=T - 1, oob_is_err=False, compute_op=ALU.add).then_inc(added[e % 2], 16)

            pool.wait_ge(route, ROUTE["token"])
            for e in range(RING):
                gather(e)
            for e in range(E):
                if e + RING < E:
                    gather(e + RING)
                scatter(e)

        @block.tensor
        def _(pe):
            pe.wait_ge(gw_in, 16)
            for t in range(TILES):
                for k in range(KT):
                    last = pe.matmul(PV[:, t * E:(t + 1) * E], xT[:, k, t * P:(t + 1) * P], gw[:, k, :], start=(k == 0), stop=(k == KT - 1))
            last.then_inc(logits_done, 1)
            pe.wait_ge(shared_in, 32)

            def s_up(t):
                if t >= 2:
                    pe.wait_ge(s_mixed, t - 1)
                for half in range(2):
                    for k in range(KT):
                        last = pe.matmul(S[:, (2 * t + half) % 4, 0:INNER_S], xT[:, k, t * P:(t + 1) * P],
                                         sgu[:, k, half * INNER_S:(half + 1) * INNER_S], start=(k == 0), stop=(k == KT - 1))
                last.then_inc(s_up_done, 1)

            def s_turn(t):
                pe.wait_ge(s_mixed, t + 1)
                if t >= 1:
                    pe.wait_ge(s_midT_done, t)
                for c in range(PIECES):
                    last = pe.transpose(TP[0:HALF_I, 0, c * P:(c + 1) * P], s_mid[:, t % 2, c * HALF_I:(c + 1) * HALF_I], ident[:, :])
                last.then_inc(s_turned, 1)

            def s_down(t):
                pe.wait_ge(s_midT_done, t + 1)
                if t >= 2:
                    pe.wait_ge(s_added, t - 1)
                for c in range(PIECES):
                    last = pe.matmul(TP[:, 1 + t % 2, 0:D], s_midT[:, t % 2, c, :], sdown[:, c, :], start=(c == 0), stop=(c == PIECES - 1))
                last.then_inc(s_down_done, 1)

            def ranks():
                pe.wait_ge(route, ROUTE["chosen16"])
                pe.wait_ge(consts_cast, 3)
                pe.matmul(PV[:, 0:TILES * E], before16[:, :], chosen16[:, :, :].rearrange("p t e -> p (t e)"), start=True, stop=False)
                for d in range(1, TILES):
                    last = pe.matmul(PV[:, d * E:TILES * E], ones16[:, :], chosen16[:, 0:TILES - d, :].rearrange("p t e -> p (t e)"),
                                     start=False, stop=(d == TILES - 1))
                last.then_inc(rank_done, 1)

            def slot_info(e):
                pe.wait_ge(onehot_done, e + 1)
                pe.wait_ge(route, ROUTE["slot"])
                for t in range(TILES):
                    last = pe.matmul(PV[:, e * INFO:(e + 1) * INFO], onehot[:, e % 2, t, :], info[:, t, e, :], start=(t == 0), stop=(t == TILES - 1))
                last.then_inc(info_done, 1)

            for s in range(TILES + 2):
                if s < TILES:
                    s_up(s)
                if 1 <= s <= TILES:
                    s_turn(s - 1)
                if s >= 2:
                    s_down(s - 2)
                if s == 4:
                    ranks()
                if 6 <= s < 6 + E // 2:
                    slot_info(2 * (s - 6))
                    slot_info(2 * (s - 6) + 1)

            def x_turn(i, u):
                pe.wait_ge(gathered[u], at(i, 16, 16))
                if not (first(i) and u == 0):
                    pe.wait_ge(xgT_done, at(i, RING, u))
                for k in range(KT):
                    last = pe.transpose(TP[:, 0, k * P:(k + 1) * P], xg[:, u, k * P:(k + 1) * P], ident[:, :])
                last.then_inc(x_turned, 1)

            def up(i, u, ring):
                pe.wait_ge(xgT_done, at(i, RING, u + 1))
                pe.wait_ge(weights_in[ring], at(i, 32, 32) if u == ring else at(i, 32, 0))
                for k in range(KT):
                    last = pe.matmul(S[:, ring, 0:2 * INNER], xgT[:, ring % 2, k, :], wgu[:, ring, k, :], start=(k == 0), stop=(k == KT - 1))
                last.then_inc(up_done, 1)

            def turn(i, u, ring):
                pe.wait_ge(mixed, at(i, RING, u + 1))
                if not (first(i) and u == 0):
                    pe.wait_ge(midT_done, at(i, RING, u))
                for c in range(2):
                    last = pe.transpose(TP[0:HALF_I, 1, c * P:(c + 1) * P], e_mid[:, ring % 2, c * HALF_I:(c + 1) * HALF_I], ident[:, :])
                last.then_inc(turned, 1)

            def down(i, u, ring):
                pe.wait_ge(midT_done, at(i, RING, u + 1))
                if not (first(i) and u == 0):
                    pe.wait_ge(out_done, at(i, RING, u))
                for c in range(2):
                    last = pe.matmul(TP[:, 2, 0:D], e_midT[:, ring % 2, c, :], wdown[:, ring, c, :], start=(c == 0), stop=(c == 1))
                last.then_inc(down_done, 1)

            pe.wait_ge(s_added, TILES)
            pe.wait_ge(route, ROUTE["slots"])

            def steps(i, us):
                for u in us:
                    if in_range(i, u, 0):
                        x_turn(i, u)
                    for back, stage in ((1, up), (2, turn), (3, down)):
                        if in_range(i, u, back):
                            stage(i, u - back, (u - back) % RING)

            steps(0, range(RING))
            with pe.Fori(1, E // RING) as i:
                steps(i, range(RING))
            steps(E // RING, range(3))

        @block.scalar
        def _(act):
            act.wait_ge(shift_done, 1)
            act.activation(exps[:, :, :], shifted[:, :, :], ACT.Exp).then_inc(exps_done, 1)
            for s in range(TILES + 1):
                if s < TILES:
                    act.wait_ge(s_up_done, s + 1)
                    if s >= 2:
                        act.wait_ge(s_mixed, s - 1)
                    act.activation(s_act[:, s % 2, :], S[:, (2 * s) % 4, 0:INNER_S], ACT.Silu).then_inc(s_act_done, 1)
                if s >= 1:
                    t = s - 1
                    act.wait_ge(s_turned, t + 1)
                    if t >= 2:
                        act.wait_ge(s_down_done, t - 1)
                    act.activation(s_midT[:, t % 2, :, :], TP[0:HALF_I, 0, :].rearrange("p (c n) -> p c n", c=PIECES), ACT.Copy).then_inc(s_midT_done, 1)

            def x_turn(i, u):
                act.wait_ge(x_turned, at(i, RING, u + 1))
                if not (first(i) and u < 2):
                    act.wait_ge(up_done, at(i, RING, u - 1))
                act.activation(xgT[:, u % 2, :, :], TP[:, 0, 0:KT * P].rearrange("p (k c) -> p k c", k=KT), ACT.Copy).then_inc(xgT_done, 1)

            def up(i, u, ring):
                act.wait_ge(up_done, at(i, RING, u + 1))
                if not (first(i) and u < 2):
                    act.wait_ge(mixed, at(i, RING, u - 1))
                act.activation(e_act[:, ring % 2, :], S[:, ring, 0:INNER], ACT.Silu).then_inc(act_done, 1)

            def turn(i, u, ring):
                act.wait_ge(turned, at(i, RING, u + 1))
                if not (first(i) and u < 2):
                    act.wait_ge(down_done, at(i, RING, u - 1))
                act.activation(e_midT[:, ring % 2, :, :], TP[0:HALF_I, 1, 0:2 * P].rearrange("p (c n) -> p c n", c=2), ACT.Copy).then_inc(midT_done, 1)

            def steps(i, us):
                for u in us:
                    if in_range(i, u, 0):
                        x_turn(i, u)
                    for back, stage in ((1, up), (2, turn)):
                        if in_range(i, u, back):
                            stage(i, u - back, (u - back) % RING)

            steps(0, range(RING))
            with act.Fori(1, E // RING) as i:
                steps(i, range(RING))
            steps(E // RING, range(3))

        @block.vector
        def _(dve):
            done = [0]

            def routed_step(name, instruction):
                instruction.then_inc(route, 1)
                done[0] += 1
                assert ROUTE[name] == done[0]
                dve.wait_ge(route, done[0])

            dve.wait_ge(consts_in, 4 * 16)
            dve.tensor_copy(before16[:, :], before[:, :]).then_inc(consts_cast, 1)
            dve.memset(ones16[:, :], 1.0).then_inc(consts_cast, 1)
            dve.tensor_copy(lower16[:, :, :], lower[:, :].rearrange("p (a b) -> p a b", a=E)).then_inc(consts_cast, 1)
            logits = PV[:, 0:TILES * E].rearrange("p (t e) -> p t e", e=E)
            wide = [P, TILES, E]
            dve.wait_ge(logits_done, 1)
            routed_step("top", dve.tensor_reduce(top[:, :], logits, AX.X, ALU.max))
            dve.tensor_tensor(shifted[:, :, :], logits, top[:, :].unsqueeze(2).to_broadcast(wide), ALU.subtract).then_inc(shift_done, 1)
            dve.wait_ge(exps_done, 1)
            routed_step("total", dve.tensor_reduce(total[:, :], exps[:, :, :], AX.X, ALU.add))
            routed_step("total_inv", dve.reciprocal(total_inv[:, :], total[:, :]))
            routed_step("score", dve.tensor_tensor(score[:, :, :], exps[:, :, :], total_inv[:, :].unsqueeze(2).to_broadcast(wide), ALU.mult))

            def choose_a():
                others = score[:, :, :].unsqueeze(2).to_broadcast([P, TILES, E, E])
                mine = score[:, :, :].unsqueeze(3).to_broadcast([P, TILES, E, E])
                routed_step("greater", dve.tensor_tensor(greater[:, :, :, :], others, mine, ALU.is_gt))
                routed_step("equal", dve.tensor_tensor(equal[:, :, :, :], others, mine, ALU.is_equal))

            def choose_b():
                dve.wait_ge(consts_cast, 3)
                flat = [P, TILES, E * E]
                g, q = (x[:, :, :, :].rearrange("p t a b -> p t (a b)") for x in (greater, equal))
                routed_step("equal_lower", dve.tensor_tensor(q, q, lower16[:, :, :].rearrange("p a b -> p (a b)").unsqueeze(1).to_broadcast(flat), ALU.mult))
                routed_step("greater_equal", dve.tensor_tensor(g, g, q, ALU.add))
                routed_step("above", dve.tensor_reduce(above[:, :, :], greater[:, :, :, :], AX.X, ALU.add))
                routed_step("chosen", dve.tensor_scalar(chosen[:, :, :], above[:, :, :], float(TOPK), None, ALU.is_lt))
                routed_step("chosen16", dve.tensor_copy(chosen16[:, :, :], chosen[:, :, :]))

            def weigh():
                routed_step("gain_raw", dve.tensor_tensor(gain[:, :, :], score[:, :, :], chosen[:, :, :], ALU.mult))
                routed_step("gain_sum", dve.tensor_reduce(gain_sum[:, :], gain[:, :, :], AX.X, ALU.add))
                routed_step("gain_eps", dve.tensor_scalar(gain_sum[:, :], gain_sum[:, :], 1e-20, None, ALU.add))
                routed_step("gain_inv", dve.reciprocal(gain_inv[:, :], gain_sum[:, :]))
                routed_step("gain", dve.tensor_tensor(gain[:, :, :], gain[:, :, :], gain_inv[:, :].unsqueeze(2).to_broadcast(wide), ALU.mult))
                routed_step("high", dve.tensor_copy(info[:, :, :, 3], gain[:, :, :]))
                routed_step("high_rest", dve.tensor_tensor(rest[:, :, :], gain[:, :, :], info[:, :, :, 3], ALU.subtract))
                routed_step("middle", dve.tensor_copy(info[:, :, :, 4], rest[:, :, :]))
                routed_step("middle_rest", dve.tensor_tensor(rest[:, :, :], rest[:, :, :], info[:, :, :, 4], ALU.subtract))
                routed_step("low", dve.tensor_copy(info[:, :, :, 5], rest[:, :, :]))

            def place():
                routed_step("numbers", dve.tensor_copy(info[:, :, :, 0], where[:, 0, :].unsqueeze(2).to_broadcast(wide)))
                routed_step("tiles", dve.tensor_copy(info[:, :, :, 1], where[:, 1, :].unsqueeze(2).to_broadcast(wide)))
                routed_step("ones", dve.memset(info[:, :, :, 2], 1.0))
                routed_step("away", dve.tensor_scalar(rest[:, :, :], chosen[:, :, :], -NOWHERE, NOWHERE, ALU.mult, ALU.add))
                dve.wait_ge(rank_done, 1)
                routed_step("slot", dve.tensor_tensor(slot[:, :, :], logits, rest[:, :, :], ALU.add))

            def one_hot(e):
                if e >= 2:
                    dve.wait_ge(info_done, e - 1)
                dve.tensor_tensor(onehot[:, e % 2, :, :], iota[:, :].unsqueeze(1).to_broadcast([P, TILES, P]),
                                  slot[:, :, e].unsqueeze(2).to_broadcast([P, TILES, P]), ALU.is_equal).then_inc(onehot_done, 1)

            def s_silu_mul(t):
                u, b = S[:, (2 * t + 1) % 4, 0:INNER_S], t % 2
                dve.wait_ge(s_act_done, t + 1)
                if t >= 2:
                    dve.wait_ge(s_turned, t - 1)
                dve.tensor_tensor(s_mid[:, b, :], u, s_act[:, b, :], ALU.mult).then_inc(s_mixed, 1)

            def s_add(t):
                dve.wait_ge(s_down_done, t + 1)
                dve.tensor_tensor(Y[:, t, :], TP[:, 1 + t % 2, 0:D], Y[:, t, :], ALU.add).then_inc(s_added, 1)

            for s in range(TILES + 2):
                if s < TILES:
                    s_silu_mul(s)
                if s == 0:
                    choose_a()
                if s == 1:
                    choose_b()
                if s == 2:
                    weigh()
                if s == 4:
                    place()
                if 5 <= s < 5 + E // 2:
                    one_hot(2 * (s - 5))
                    one_hot(2 * (s - 5) + 1)
                if s >= 2:
                    s_add(s - 2)
            dve.wait_ge(info_done, E)
            routed_step("slots", dve.tensor_copy(slots[:, :, :], PV[:, 0:E * INFO].rearrange("p (e c) -> p e c", c=INFO)))
            routed_step("token_a", dve.scalar_tensor_tensor(out=token_a[:, :], in0=slots[:, :, 1], scalar=float(P), in1=slots[:, :, 0], op0=ALU.mult, op1=ALU.add))
            routed_step("token_b", dve.tensor_scalar(token_b[:, :], slots[:, :, 2], -NOWHERE, NOWHERE, ALU.mult, ALU.add))
            routed_step("token", dve.tensor_tensor(token[:, :], token_a[:, :], token_b[:, :], ALU.add))
            routed_step("gain_a", dve.tensor_tensor(slot_gain_a[:, :], slots[:, :, 5], slots[:, :, 4], ALU.add))
            routed_step("slot_gain", dve.tensor_tensor(slot_gain[:, :], slot_gain_a[:, :], slots[:, :, 3], ALU.add))

            def up(i, u, ring):
                up_, b = S[:, ring, INNER:2 * INNER], ring % 2
                dve.wait_ge(act_done, at(i, RING, u + 1))
                if not (first(i) and u < 2):
                    dve.wait_ge(turned, at(i, RING, u - 1))
                dve.tensor_tensor(e_mid[:, b, :], up_, e_act[:, b, :], ALU.mult).then_inc(mixed, 1)

            def down(i, u, ring):
                dve.wait_ge(down_done, at(i, RING, u + 1))
                if not (first(i) and u == 0):
                    dve.wait_ge(out_free, at(i, RING, u))
                dve.tensor_scalar(e_out[:, ring % 2, :], TP[:, 2, 0:D], slot_gain[:, bass.ds(RING * i + u, 1)], None, ALU.mult).then_inc(out_done, 1)

            def steps(i, us):
                for u in us:
                    for back, stage in ((1, up), (3, down)):
                        if in_range(i, u, back):
                            stage(i, u - back, (u - back) % RING)

            steps(0, range(RING))
            with dve.Fori(1, E // RING) as i:
                steps(i, range(RING))
            steps(E // RING, range(3))
            for t in range(TILES):
                if t % 4 == 0:
                    dve.wait_ge(y_in[t // 4], 16)
                dve.tensor_tensor(Y[:, t, :], Y[:, t, :], y_routed[:, t, :], ALU.add)



def load_ident(nc, core, consts):
    with ExitStack() as ctx:
        loaded = ctx.enter_context(nc.semaphore("ident_loaded"))
        block = ctx.enter_context(nc.Block())

        @block.sync
        def _(sp):
            sp.dma_start(core.ident[:, :], consts[:, CONST["ident"][0]:CONST["ident"][1]]).then_inc(loaded, 16)
            sp.wait_ge(loaded, 16)


def build(nc, x, consts, wqkv0, wo0, ball_w, ball_scale, wq1, wkv1, wo1, gate_w, sw_gu, sw_down, w_gu, w_down, out):
    x_rows = nc.dram_tensor("x_rows", (T, D), F32).ap()
    routed = nc.dram_tensor("routed", (T, D), F32).ap()
    with ExitStack() as ctx:
        core = Core(nc, ctx)
        load_ident(nc, core, consts)
        with ExitStack() as split:
            xT_hi = split.enter_context(nc.sbuf_tensor("xT_hi", [P, KT, T], F32R))
            xT_lo = split.enter_context(nc.sbuf_tensor("xT_lo", [P, KT, T], F32R))
            norm_stage(nc, core, "load", xT_hi=xT_hi, xT_lo=xT_lo, source=x, normalize=False)
            rotary_attention(nc, core, consts, wqkv0, wo0, xT_hi, xT_lo)
            norm_stage(nc, core, "norm0", xT_hi=xT_hi, xT_lo=xT_lo)
            ball_projection(nc, core, ball_w, ball_scale, xT_hi, xT_lo)
            norm_stage(nc, core, "norm1", xT_hi=xT_hi, xT_lo=xT_lo)
            window_attention(nc, core, consts, wq1, wkv1, wo1, xT_hi, xT_lo)
        xT = ctx.enter_context(nc.sbuf_tensor("xT", [P, KT, T], F32))
        norm_stage(nc, core, "norm2", xT=xT, store=x_rows)
        expert_mix(nc, core, consts, gate_w, sw_gu, sw_down, w_gu, w_down, xT, x_rows, routed)
        norm_stage(nc, core, "norm3", store=out)



def _constants(np):
    p, e = np.arange(P), np.arange(E)
    c = np.zeros((P, CONSTS), np.float32)

    def put(name, a):
        c[:, CONST[name][0]:CONST[name][1]] = np.asarray(a, np.float32).reshape(P, -1)

    put("ident", np.eye(P))
    later = np.where(p[None, :] > p[:, None], MASKED, 0.0)
    put("causal", np.concatenate([later, np.full((P, P), MASKED), np.zeros((P, P)), later], 1))
    back = np.arange(2 * P)[None, :] - P - p[:, None]
    window = np.where((back <= 0) & (back > -WIN), 0.0, MASKED)
    put("window", np.concatenate([np.where(np.arange(2 * P)[None, :] >= P, window, MASKED), window], 1))
    fraction = np.float32(2.0) * np.arange(HALF, dtype=np.float32) / np.float32(HD)
    timescale = np.power(np.float32(10000.0), fraction).astype(np.float32)
    phase = (np.arange(T, dtype=np.float32)[:, None] / timescale[None, :]).astype(np.float32)
    cos, sin = np.cos(phase), np.sin(phase)
    put("cos", cos.reshape(TILES, P, HALF).transpose(1, 0, 2))
    put("sin", sin.reshape(TILES, P, HALF).transpose(1, 0, 2))
    put("iota", np.broadcast_to(p[None, :], (P, P)))
    put("before", p[:, None] < p[None, :])
    put("lower", np.broadcast_to((e[None, :] < e[:, None]).reshape(1, E * E), (P, E * E)))
    put("where", np.concatenate([np.broadcast_to(p[:, None], (P, TILES)), np.broadcast_to(np.arange(TILES)[None, :], (P, TILES))], 1))
    return c


def kernel(**inputs):
    import numpy as np
    import concourse.bacc as bacc
    from concourse.bass_utils import run_bass_kernel_spmd

    i = {k: np.asarray(v) for k, v in inputs.items()}
    turned = np.concatenate([np.arange(0, HD, 2), np.arange(1, HD, 2)])
    qkv0 = np.stack([i["L0_attn_wq"][:, :, turned], i["L0_attn_wk"][:, :, turned], i["L0_attn_wv"]], 2)
    kv1 = np.stack([i["L1_attn_Wk"].reshape(KT, P, HKV, HD), i["L1_attn_Wv"].reshape(KT, P, HKV, HD)], 3)
    arrays = {
        "x": i["L0_attn_x"].reshape(T, D),
        "consts": _constants(np),
        "wqkv0": qkv0.reshape(KT, P, H0, QKV).transpose(2, 1, 0, 3),
        "wo0": i["L0_attn_wo"],
        "ball_w": i["L0_ffn_weight"],
        "ball_scale": i["L0_ffn_scale"],
        "wq1": i["L1_attn_Wq"].reshape(KT, P, HKV, REP * HD).transpose(2, 1, 0, 3),
        "wkv1": kv1.transpose(2, 1, 0, 3, 4).reshape(HKV, P, KT, 2 * HD),
        "wo1": i["L1_attn_Wo"].reshape(HKV, REP, HD, D).transpose(0, 2, 1, 3),
        "gate_w": i["L1_ffn_gate_w"].T.reshape(KT, P, E).transpose(1, 0, 2),
        "sw_gu": np.concatenate([i["L1_ffn_sw_gate"], i["L1_ffn_sw_up"]], 1).reshape(KT, P, 2 * INNER_S).transpose(1, 0, 2),
        "sw_down": i["L1_ffn_sw_down"].reshape(2 * INNER_S // INNER, INNER // 2, D).transpose(1, 0, 2),
        "w_gu": np.concatenate([i["L1_ffn_w_gate"], i["L1_ffn_w_up"]], 2).reshape(E, KT, P, 2 * INNER).transpose(0, 2, 1, 3),
        "w_down": i["L1_ffn_w_down"].reshape(E, 2, INNER // 2, D).transpose(0, 2, 1, 3),
    }
    arrays = {f"in_{k}": np.ascontiguousarray(v) for k, v in arrays.items()}
    nc = bacc.Bacc("TRN2", target_bir_lowering=False, num_devices=1)
    args = [nc.dram_tensor(k, v.shape, mybir.dt.from_np(v.dtype), kind="ExternalInput").ap() for k, v in arrays.items()]
    out = nc.dram_tensor("out_0", (T, D), F32, kind="ExternalOutput").ap()
    build(nc, *args, out)
    r = run_bass_kernel_spmd(nc, [arrays], core_ids=[0])
    return r.results[0]["out_0"].reshape(1, T, D)
```

```python
from contextlib import ExitStack
from functools import partial

import concourse.bass as bass
from concourse import mybir

F32 = mybir.dt.float32
F32R = mybir.dt.float32r
BF16 = mybir.dt.bfloat16
I32 = mybir.dt.int32
ALU = mybir.AluOpType
ACT = mybir.ActivationFunctionType
AX = mybir.AxisListType

P = 128
T = 2048
D = 256
TILES = T // P
KT = D // P
PAIRS = TILES // 2
BANK = 512
LN_EPS = 1e-5

H0 = 16
HD = 128
HALF = HD // 2
QKV = 3 * HD
SCALE0 = float(HD) ** -0.5

BALL_EPS = 1e-7
MAX_NORM = 0.99

HQ, HKV, WIN = 16, 4, 64
REP = HQ // HKV
SCALE1 = 1.0 / HD

E = 16
TOPK = 4
INNER = 176
INNER_S = 352
CAP = 128

MASKED = -1e30

_WIDTHS = [("ident", P), ("causal", P), ("window", 2 * 2 * P), ("cos", TILES * HALF),
           ("sin", TILES * HALF), ("iota", P), ("before", P), ("lower", E * E), ("where", 2 * TILES)]
CONST = {}
_at = 0
for _name, _n in _WIDTHS:
    CONST[_name] = (_at, _at + _n)
    _at += _n
CONSTS = _at


def at(loop, per_turn, count):
    return loop * per_turn + count


def rows(ap):
    return ap.rearrange("(t p) d -> p t d", p=P)


def bc(ap, shape):
    return ap.to_broadcast(shape)


class Core:

    def __init__(self, nc, ctx, consts):
        self.ctx = ctx
        self.Y = ctx.enter_context(nc.sbuf_tensor("Y", [P, TILES, D], F32))
        self.ident = ctx.enter_context(nc.sbuf_tensor("ident", [P, P], F32))
        self.ident_source = consts[:, CONST["ident"][0]:CONST["ident"][1]]
        self.ident_in = ctx.enter_context(nc.semaphore("ident_in"))
        self.S = ctx.enter_context(nc.psum_tensor("S", [P, 4, BANK], F32))
        self.TP = ctx.enter_context(nc.psum_tensor("TP", [P, 3, BANK], F32))
        self.PV = ctx.enter_context(nc.psum_tensor("PV", [P, BANK], F32))


def norm_stage(nc, core, name, xT_hi=None, xT_lo=None, xT=None, source=None, normalize=True, store=None,
               loads=None, splits=None, addend=None):
    Y, ident, TP = core.Y, core.ident, core.TP
    turn = xT_hi is not None or xT is not None
    GROUPS, PER = 4, TILES // 4
    with ExitStack() as ctx:
        def sem(n):
            return core.ctx.enter_context(nc.semaphore(f"{name}_{n}"))

        loaded = [sem(f"loaded{c}") for c in range(GROUPS)] if source is not None else None
        if normalize:
            statistics, variance_done, root_done, inverse_done, tile_ready = (sem(n) for n in (
                "statistics", "variance_done", "root_done", "inverse_done", "tile_ready"))
        if addend is not None:
            (others, others_in), summed = addend, sem("summed")
        if turn:
            turned, hi_done = sem("turned"), sem("hi_done")
        if xT_hi is not None:
            group_free = sem("group_free")
        if store is not None:
            stored = sem("stored")
        if normalize:
            stats = ctx.enter_context(nc.sbuf_tensor(f"{name}_stats", [P, TILES, 6], F32))
            moments = ctx.enter_context(nc.sbuf_tensor(f"{name}_moments", [P, TILES, 2], F32))
            var_eps = ctx.enter_context(nc.sbuf_tensor(f"{name}_var_eps", [P, TILES], F32))
            std = ctx.enter_context(nc.sbuf_tensor(f"{name}_std", [P, TILES], F32))
            rstd = ctx.enter_context(nc.sbuf_tensor(f"{name}_rstd", [P, TILES], F32))
        block = ctx.enter_context(nc.Block())

        @block.sync
        def _(sp):
            if source is not None:
                sp.dma_start(ident[:, :], core.ident_source).then_inc(core.ident_in, 16)
                for c in range(GROUPS):
                    group = slice(PER * c, PER * (c + 1))
                    sp.dma_start(Y[:, group, :], rows(source)[:, group, :]).then_inc(loaded[c], 16)
            if loads is not None:
                loads(sp)
            if store is not None:
                for c in range(GROUPS):
                    group = slice(PER * c, PER * (c + 1))
                    sp.wait_ge(tile_ready, PER * (c + 1))
                    sp.dma_start(rows(store)[:, group, :], Y[:, group, :]).then_inc(stored, 16)
                sp.wait_ge(stored, GROUPS * 16)

        @block.gpsimd
        def _(pool):
            if splits is not None:
                splits(pool)

        @block.vector
        def _(dve):
            def variance(c):
                tiles = range(PER * c, PER * (c + 1))
                if addend is not None:
                    dve.wait_ge(others_in[c], 32)
                    for n, other in enumerate(others):
                        for k, t in enumerate(tiles):
                            if n == 1:
                                dve.wait_ge(summed, 2 * PER * c + k + 1)
                            dve.tensor_tensor(Y[:, t, :], Y[:, t, :], other[:, t, :], ALU.add).then_inc(summed, 1)
                for k, t in enumerate(tiles):
                    if addend is not None:
                        dve.wait_ge(summed, 2 * PER * c + PER + k + 1)
                    dve.bn_stats(stats[:, t, :], Y[:, t, :]).then_inc(statistics, 1)
                for n, t in enumerate(tiles):
                    dve.wait_ge(statistics, 2 * PER * c + n + 1)
                    dve.bn_aggr(moments[:, t, :], stats[:, t, :]).then_inc(statistics, 1)
                dve.wait_ge(statistics, 2 * PER * (c + 1))
                group = slice(PER * c, PER * (c + 1))
                dve.tensor_scalar(var_eps[:, group], moments[:, group, 1], LN_EPS, None, ALU.add).then_inc(variance_done, 1)

            def normalise(c):
                group = slice(PER * c, PER * (c + 1))
                dve.wait_ge(root_done, c + 1)
                dve.reciprocal(rstd[:, group], std[:, group]).then_inc(inverse_done, 1)
                dve.wait_ge(inverse_done, c + 1)
                for t in range(PER * c, PER * (c + 1)):
                    dve.tensor_scalar(Y[:, t, :], Y[:, t, :], moments[:, t, 0:1], rstd[:, t:t + 1],
                                      ALU.subtract, ALU.mult).then_inc(tile_ready, 1)

            def low(g):
                dve.wait_ge(hi_done, g + 1)
                cols = slice(2 * P * g, 2 * P * (g + 1))
                dve.tensor_tensor(xT_lo[:, :, cols], TP[:, g % 3, :].rearrange("p (k c) -> p k c", k=KT),
                                  xT_hi[:, :, cols].bitcast(F32), ALU.subtract).then_inc(group_free, 1)

            if normalize:
                for c in range(GROUPS):
                    variance(c)
            for c in range(GROUPS + 1):
                if normalize and c < GROUPS:
                    normalise(c)
                if xT_hi is not None and c >= 1:
                    low(2 * (c - 1))
                    low(2 * (c - 1) + 1)

        @block.scalar
        def _(act):
            def high(g):
                act.wait_ge(turned, g + 1)
                cols = slice(2 * P * g, 2 * P * (g + 1))
                to = xT_hi if xT_hi is not None else xT
                act.activation(to[:, :, cols], TP[:, g % 3, :].rearrange("p (k c) -> p k c", k=KT),
                               ACT.Copy).then_inc(hi_done, 1)

            if normalize:
                for c in range(GROUPS):
                    group = slice(PER * c, PER * (c + 1))
                    act.wait_ge(variance_done, c + 1)
                    act.activation(std[:, group], var_eps[:, group], ACT.Sqrt).then_inc(root_done, 1)
            if turn:
                for g in range(PAIRS):
                    high(g)

        @block.tensor
        def _(pe):
            if not turn:
                return
            if source is not None:
                pe.wait_ge(core.ident_in, 16)
            for g in range(PAIRS):
                if source is not None and g % 2 == 0:
                    pe.wait_ge(loaded[g // 2], 16)
                if normalize:
                    pe.wait_ge(tile_ready, 2 * g + 2)
                if g >= 3:
                    pe.wait_ge(group_free if xT_hi is not None else hi_done, g - 2)
                for k in range(KT):
                    for j in range(2):
                        last = pe.transpose(TP[:, g % 3, (2 * k + j) * P:(2 * k + j + 1) * P],
                                            Y[:, 2 * g + j, k * P:(k + 1) * P], ident[:, :])
                last.then_inc(turned, 1)


TENSOR_ORDER = """
    project0 project1 project2 project3 project4 turn0 project5 turn1 project6 project7 turn2 project8 project9
    turn3 project10 project11 project12 turn4 project13 turn5 project14 project15 scores0 scores1 turn6 scores2
    scores3 row0.0 scores4 row1.0 row2.0 row3.0 scores5 mix0.0.2 scores6 row4.0 row4.1 scores7 row5.0 mix1.0.4
    row5.1 turn7 scores8 row6.0 mix2.0.1 row6.1 mix2.1.3 out0 row7.0 row7.1 scores9 mix2.3.6 out1 row8.0 row8.1
    mix3.0.3 scores10 row8.2 row9.0 out2 mix3.3.6 row9.1 mix3.6.8 scores11 mix4.0.1 row9.2 row10.0 row10.1
    mix4.1.7 scores12 row10.2 row11.0 mix4.7.9 out3 row11.1 mix4.9.10 row11.2 scores13 row12.0 mix5.0.1 out4
    mix5.1.5 row12.1 row12.2 scores14 mix5.5.6 row12.3 row13.0 row13.1 mix5.6.9 row13.2 row13.3 mix5.9.12
    scores15 row14.0 row14.1 out5 mix6.0.10 row14.2 row14.3 row15.0 mix6.10.14 row15.1 row15.2 row15.3 mix7.0.16
    out6 out7"""
SCALAR_ORDER = """
    project0 project1 turn0 project2 turn1 project3 project4 project5 project6 project7 turn2 project8 turn3
    project9 project10 project11 turn4 turn5 project12 project13 project14 project15 scores0 scores1 turn6
    row0.0 scores2 scores3 row1.0 row2.0 scores4 row3.0 mix0 scores5 row4.0 row4.1 scores6 row5.0 scores7 mix1
    row5.1 turn7 row6.0 row6.1 scores8 row7.0 row7.1 mix2 scores9 row8.0 row8.1 row8.2 row9.0 scores10 row9.1
    mix3 row9.2 row10.0 scores11 row10.1 row10.2 row11.0 scores12 row11.1 row11.2 mix4 row12.0 scores13 row12.1
    row12.2 row12.3 row13.0 scores14 mix5 row13.1 row13.2 row13.3 row14.0 row14.1 scores15 row14.2 row14.3
    row15.0 mix6 row15.1 row15.2 row15.3 mix7"""
VECTOR_ORDER = """
    project0 project1 project2 project3 project4 project5 turn0 project6 project7 turn1 project8 project9 turn2
    project10 project11 turn3 project12 project13 turn4 turn5 project14 project15 scores0 scores1 scores2
    scores3 turn6 row0.0 scores4 row1.0 row2.0 scores5 mix0 row3.0 scores6 scores7 row4.0 row4.1 row5.0 mix1
    row5.1 turn7 scores8 row6.0 row6.1 out0 row7.0 row7.1 scores9 mix2 out1 row8.0 row8.1 scores10 row8.2 row9.0
    out2 row9.1 mix3 scores11 row9.2 row10.0 row10.1 scores12 row10.2 row11.0 out3 row11.1 mix4 scores13 row11.2
    row12.0 out4 row12.1 row12.2 scores14 row12.3 row13.0 mix5 row13.1 row13.2 row13.3 scores15 row14.0 row14.1
    out5 row14.2 row14.3 row15.0 mix6 row15.1 row15.2 row15.3 mix7 out6 out7"""


def steps_of(order):
    steps = []
    for word in order.split():
        name = word.rstrip("0123456789.")
        steps.append((name, *(int(n) for n in word[len(name):].split("."))))
    return steps


def row_groups(i):
    return (i + 1 + 3) // 4


def rotary_attention(nc, core, consts, wqkv, wo, xT_hi, xT_lo, meanwhile):
    Y, ident, S, TP, PV = core.Y, core.ident, core.S, core.TP, core.PV
    TENSOR, SCALAR, VECTOR = (steps_of(order) for order in (TENSOR_ORDER, SCALAR_ORDER, VECTOR_ORDER))
    number = {}
    for what in TENSOR:
        if what[0] in ("turn", "row", "out"):
            number[what] = len(number)
    FREED = len(number)
    ROW_GROUPS = [row_groups(i) for i in range(TILES)]
    CHUNKS = sum(ROW_GROUPS)
    chunk_at = [sum(ROW_GROUPS[:i]) for i in range(TILES)]
    TURN = PAIRS
    SMALL = PAIRS

    def width(i):
        return P * (i + 1)

    def base(i):
        return i if i < 4 else (2 * (i % 2) if i < SMALL else 0)

    def row(i):
        return S[:, :, :].rearrange("p b c -> p (b c)")[:, base(i) * BANK:base(i) * BANK + width(i)]

    def probs_at(i):
        return (i % 4) * (T // 2) if i < SMALL else (i % 2) * T

    def pair_at(j):
        return 0 if j % 2 == 0 else TILES - 2

    with ExitStack() as ctx:
        def sb(n, shape, dt=F32):
            return ctx.enter_context(nc.sbuf_tensor("l0_" + n, shape, dt))

        def sem(n):
            return core.ctx.enter_context(nc.semaphore("l0_" + n))

        zero = sb("zero", [P, 1])
        w_raw = sb("w_raw", [P, KT, QKV])
        w_hi, w_lo = sb("w_hi", [P, KT, QKV], F32R), sb("w_lo", [P, KT, QKV], F32R)
        wo_raw = sb("wo_raw", [P, D])
        wo_hi, wo_lo = sb("wo_hi", [P, D], F32R), sb("wo_lo", [P, D], F32R)
        cos, sin = sb("cos", [P, TILES, HALF]), sb("sin", [P, TILES, HALF])
        mask = sb("mask", [P, P], BF16)
        ident16 = sb("ident16", [P, P], BF16)
        rotated, crossed = sb("rotated", [P, 4, 2, 2, HALF]), sb("crossed", [P, 4, 2, 2, HALF])
        qk_hi, qk_lo = sb("qk_hi", [P, 2, T], F32R), sb("qk_lo", [P, 2, T], F32R)
        v_raw = sb("v_raw", [P, 4, HD])
        v_hi, v_lo = sb("v_hi", [P, TILES, HD], F32R), sb("v_lo", [P, TILES, HD], F32R)
        probs = sb("probs", [P, 2 * T])
        pT_hi, pT_lo = (sb(n, [P, 2 * TILES - 2, 2 * P], F32R) for n in ("pT_hi", "pT_lo"))
        a_hi, a_lo = sb("a_hi", [P, 2, 2 * P], F32R), sb("a_lo", [P, 2, 2 * P], F32R)
        part_max, neg_max = sb("part_max", [P, TILES, 2]), sb("neg_max", [P, TILES])
        row_sum, row_inv = sb("row_sum", [P, TILES]), sb("row_inv", [P, TILES])
        mask32 = probs[:, 0:P]

        consts_in, consts_cast, w_in, wo_in, w_split, wo_split, w_hi_done, wo_hi_done = (sem(n) for n in (
            "consts_in", "consts_cast", "w_in", "wo_in", "w_split", "wo_split", "w_hi_done", "wo_hi_done"))
        zeroed = sem("zeroed")
        tile_projected, tile_multiplied, tile_rotated, qk_turned, v_out, v_low_done, qk_hi_done = (sem(n) for n in (
            "tile_projected", "tile_multiplied", "tile_rotated", "qk_turned", "v_out", "v_low_done", "qk_hi_done"))
        chunk_scored, part_max_done, neg_max_done, row_exped, row_turned, pT_hi_done, tp_free = (sem(n) for n in (
            "chunk_scored", "part_max_done", "neg_max_done", "row_exped", "row_turned", "pT_hi_done", "tp_free"))
        pair_mixed, a_hi_done, a_lo_done, pair_out, inv_done = (sem(n) for n in (
            "pair_mixed", "a_hi_done", "a_lo_done", "pair_out", "inv_done"))

        def loads(sp):
            sp.dma_start(w_raw[:, :, :], wqkv[0, :, :, :]).then_inc(w_in, 16)
            for n, to in (("cos", cos[:, :, :].rearrange("p t c -> p (t c)")),
                          ("sin", sin[:, :, :].rearrange("p t c -> p (t c)")), ("causal", mask32)):
                sp.dma_start(to, consts[:, CONST[n][0]:CONST[n][1]]).then_inc(consts_in, 16)
            sp.dma_start(wo_raw[:, :], wo[0, :, :]).then_inc(wo_in, 16)

        meanwhile(loads=loads)
        block = ctx.enter_context(nc.Block())

        @block.sync
        def _(sp):
            with sp.Fori(1, H0) as h:
                sp.wait_ge(w_split, at(h, 1, 0))
                sp.dma_start(w_raw[:, :, :], wqkv[h, :, :, :]).then_inc(w_in, 16)
                sp.wait_ge(wo_split, at(h, 1, 0))
                sp.dma_start(wo_raw[:, :], wo[h, :, :]).then_inc(wo_in, 16)

        @block.gpsimd
        def _(pool):
            pool.memset(zero[:, :], 0.0).then_inc(zeroed, 1)
            pool.wait_ge(zeroed, 1)
            with pool.Fori(0, H0) as h:

                def v_low(u):
                    pool.wait_ge(v_out, at(h, TILES, 2 * u + 2))
                    two, raw = slice(2 * u, 2 * u + 2), slice(2 * u % 4, 2 * u % 4 + 2)
                    pool.tensor_tensor(v_lo[:, two, :], v_raw[:, raw, :], v_hi[:, two, :].bitcast(F32),
                                       ALU.subtract).then_inc(v_low_done, 1)

                pool.wait_ge(w_in, at(h, 16, 16))
                pool.tensor_tensor(w_hi[:, :, :], w_raw[:, :, :], zero[:, :].unsqueeze(2).to_broadcast([P, KT, QKV]), ALU.add).then_inc(w_hi_done, 1)
                pool.wait_ge(w_hi_done, at(h, 1, 1))
                pool.tensor_tensor(w_lo[:, :, :], w_raw[:, :, :], w_hi[:, :, :].bitcast(F32),
                                   ALU.subtract).then_inc(w_split, 1)
                for t in range(TILES):
                    pool.wait_ge(tile_multiplied, at(h, TILES, t + 1))
                    for a, sign in ((0, ALU.subtract), (1, ALU.add)):
                        last = pool.tensor_tensor(rotated[:, t % 4, :, a, :], rotated[:, t % 4, :, a, :],
                                                  crossed[:, t % 4, :, 1 - a, :], sign)
                    last.then_inc(tile_rotated, 1)
                    if t % 2 == 1 and t >= 3:
                        v_low(t // 2 - 1)
                v_low(PAIRS - 1)
                pool.wait_ge(wo_in, at(h, 16, 16))
                pool.tensor_tensor(wo_hi[:, :], wo_raw[:, :], zero[:, :].to_broadcast([P, D]), ALU.add).then_inc(wo_hi_done, 1)
                pool.wait_ge(wo_hi_done, at(h, 1, 1))
                pool.tensor_tensor(wo_lo[:, :], wo_raw[:, :], wo_hi[:, :].bitcast(F32),
                                   ALU.subtract).then_inc(wo_split, 1)

        @block.tensor
        def _(pe):
            pe.wait_ge(consts_cast, 2)
            with pe.Fori(0, H0) as h:

                def project(t):
                    if t >= 4:
                        pe.wait_ge(v_out, at(h, TILES, t - 3))
                    toks = slice(t * P, (t + 1) * P)
                    parts = [(x, w, k) for k in range(KT) for x, w in ((xT_hi, w_hi), (xT_hi, w_lo), (xT_lo, w_hi))]
                    for n, (x, w, k) in enumerate(parts):
                        last = pe.matmul(S[:, t % 4, 0:QKV], x[:, k, toks], w[:, k, :],
                                         start=(n == 0), stop=(n == len(parts) - 1))
                    last.then_inc(tile_projected, 1)

                def turn(g):
                    n = number["turn", g]
                    pe.wait_ge(tile_rotated, at(h, TILES, 2 * g + 2))
                    if n >= 3:
                        pe.wait_ge(tp_free, at(h, FREED, n - 2))
                    for q in range(2):
                        for j in range(2):
                            last = pe.transpose(TP[:, n % 3, (2 * q + j) * P:(2 * q + j + 1) * P],
                                                rotated[:, (2 * g + j) % 4, q, :, :].rearrange("p a c -> p (a c)"), ident[:, :])
                    last.then_inc(qk_turned, 1)

                def scores(i):
                    n = ROW_GROUPS[i]
                    if i < 4:
                        pe.wait_ge(v_out, at(h, TILES, TILES - 3 + i))
                    elif i < SMALL:
                        pe.wait_ge(row_exped, at(h, TILES, 2 * (i - 3) if i < 6 else i - 1))
                    else:
                        pe.wait_ge(row_exped, at(h, TILES, i))
                    if i % 2 == 0:
                        pe.wait_ge(tp_free, at(h, FREED, number["turn", i // 2] + 1))
                    q = slice(i * P, (i + 1) * P)
                    for c in range(n):
                        own = min(BANK, width(i) - c * BANK)
                        w = max(own, 2 * P)
                        out = S[:, base(i) + c, 0:w]
                        keys = slice(c * BANK, c * BANK + w)
                        final = c == n - 1
                        pe.matmul(out, qk_hi[:, 0, q], qk_hi[:, 1, keys], start=True, stop=False)
                        pe.matmul(out, qk_hi[:, 0, q], qk_lo[:, 1, keys], start=False, stop=False)
                        last = pe.matmul(out, qk_lo[:, 0, q], qk_hi[:, 1, keys], start=False, stop=not final)
                        if final:
                            last = pe.matmul(out[:, own - P:own], ident16[:, :], mask[:, :], start=False, stop=True)
                        last.then_inc(chunk_scored, 1)

                def turn_row(i, g):
                    n = number["row", i, g]
                    if g == 0:
                        pe.wait_ge(row_exped, at(h, TILES, i + 1))
                    pe.wait_ge(tp_free, at(h, FREED, n - 2))
                    for b in range(4 * g, min(4 * g + 4, width(i) // P)):
                        last = pe.transpose(TP[:, n % 3, (b % 4) * P:(b % 4 + 1) * P],
                                            probs[:, probs_at(i) + b * P:probs_at(i) + (b + 1) * P], ident[:, :])
                    last.then_inc(row_turned, 1)

                def mix(j, first, end):
                    if j == 0:
                        pe.wait_ge(v_low_done, at(h, PAIRS, PAIRS))
                    if first == 0 and j >= 1:
                        pe.wait_ge(a_lo_done, at(h, PAIRS, j))
                    for k in range(first, end):
                        if k == first or k % 4 == 0:
                            pe.wait_ge(tp_free, at(h, FREED, number["row", 2 * j + 1, k // 4] + 1))
                        hi, lo = pT_hi[:, pair_at(j) + k, :], pT_lo[:, pair_at(j) + k, :]
                        pe.matmul(PV[:, 0:2 * P], v_hi[:, k, :], hi, start=(k == 0), stop=False)
                        pe.matmul(PV[:, 0:2 * P], v_hi[:, k, :], lo, start=False, stop=False)
                        last = pe.matmul(PV[:, 0:2 * P], v_lo[:, k, :], hi, start=False, stop=(k == 2 * j + 1))
                    if end == 2 * j + 2:
                        last.then_inc(pair_mixed, 1)

                def out_projection(j):
                    n = number["out", j]
                    pe.wait_ge(tp_free, at(h, FREED, n - 2))
                    pe.wait_ge(a_lo_done, at(h, PAIRS, j + 1))
                    pe.wait_ge(wo_split, at(h, 1, 1))
                    for q in range(2):
                        out = TP[:, n % 3, q * D:(q + 1) * D]
                        toks = slice(q * P, (q + 1) * P)
                        pe.matmul(out, a_hi[:, j % 2, toks], wo_hi[:, :], start=True, stop=False)
                        pe.matmul(out, a_hi[:, j % 2, toks], wo_lo[:, :], start=False, stop=False)
                        last = pe.matmul(out, a_lo[:, j % 2, toks], wo_hi[:, :], start=False, stop=True)
                    last.then_inc(pair_out, 1)

                pe.wait_ge(w_split, at(h, 1, 1))
                for what, *which in TENSOR:
                    if what == "project":
                        project(*which)
                    elif what == "turn":
                        turn(*which)
                    elif what == "scores":
                        scores(*which)
                    elif what == "row":
                        turn_row(*which)
                    elif what == "mix":
                        mix(*which)
                    else:
                        out_projection(*which)

        @block.scalar
        def _(act):
            with act.Fori(0, H0) as h:

                def v_leaves(t):
                    act.wait_ge(tile_multiplied, at(h, TILES, t + 1))
                    if t >= 4:
                        act.wait_ge(v_low_done, at(h, PAIRS, t // 2 - 1))
                    act.activation(v_raw[:, t % 4, :], S[:, t % 4, 2 * HD:QKV], ACT.Copy)
                    act.activation(v_hi[:, t, :], S[:, t % 4, 2 * HD:QKV], ACT.Copy).then_inc(v_out, 1)

                def qk_high(g):
                    n = number["turn", g]
                    act.wait_ge(qk_turned, at(h, TURN, g + 1))
                    act.activation(qk_hi[:, :, 2 * P * g:2 * P * (g + 1)],
                                   TP[:, n % 3, :].rearrange("p (q c) -> p q c", q=2), ACT.Copy).then_inc(qk_hi_done, 1)

                def exponentials(i):
                    act.wait_ge(neg_max_done, at(h, TILES, i + 1))
                    if i >= 4:
                        held = i - 4 if i < SMALL else (i - 2 if i >= SMALL + 2 else (5, 7)[i - SMALL])
                        act.wait_ge(row_turned, at(h, CHUNKS, chunk_at[held] + ROW_GROUPS[held]))
                    act.activation(probs[:, probs_at(i):probs_at(i) + width(i)], row(i), ACT.Exp, bias=neg_max[:, i:i + 1],
                                   scale=SCALE0, accum_out=row_sum[:, i:i + 1]).then_inc(row_exped, 1)

                def row_high(i, g):
                    n = number["row", i, g]
                    m = min(4, width(i) // P - 4 * g)
                    act.wait_ge(row_turned, at(h, CHUNKS, chunk_at[i] + g + 1))
                    to = pair_at(i // 2) + 4 * g
                    act.activation(pT_hi[:, to:to + m, (i % 2) * P:(i % 2 + 1) * P],
                                   TP[:, n % 3, 0:m * P].rearrange("p (b c) -> p b c", c=P),
                                   ACT.Copy).then_inc(pT_hi_done, 1)

                def pair_high(j):
                    act.wait_ge(pair_mixed, at(h, PAIRS, j + 1))
                    if j >= 2:
                        act.wait_ge(pair_out, at(h, PAIRS, j - 1))
                    act.activation(a_hi[:, j % 2, :], PV[:, 0:2 * P], ACT.Copy).then_inc(a_hi_done, 1)

                for what, *which in SCALAR:
                    if what == "project":
                        v_leaves(*which)
                    elif what == "turn":
                        qk_high(*which)
                    elif what == "scores":
                        exponentials(*which)
                    elif what == "row":
                        row_high(*which)
                    else:
                        pair_high(*which)

        @block.vector
        def _(dve):
            dve.wait_ge(consts_in, 3 * 16)
            dve.tensor_copy(mask[:, :], mask32).then_inc(consts_cast, 1)
            dve.tensor_copy(ident16[:, :], ident[:, :]).then_inc(consts_cast, 1)
            with dve.Fori(0, H0) as h:

                def multiply(t):
                    dve.wait_ge(tile_projected, at(h, TILES, t + 1))
                    if t >= 4:
                        dve.wait_ge(qk_turned, at(h, TURN, t // 2 - 1))
                    qk = S[:, t % 4, 0:2 * HD].rearrange("p (b c) -> p b c", c=HALF)
                    for to, by in ((rotated, cos), (crossed, sin)):
                        last = dve.tensor_tensor(to[:, t % 4, :, :, :].rearrange("p q a c -> p (q a) c"), qk,
                                                 by[:, t, :].unsqueeze(1).to_broadcast([P, 4, HALF]), ALU.mult)
                    last.then_inc(tile_multiplied, 1)
                    if t in (4, 6, 8, 10):
                        pT, j = (pT_hi, pT_lo)[t // 4 - 1], t // 2 % 2
                        start = pair_at(j) + 2 * j + 1
                        dve.memset(pT[:, start:start + 13:4, 0:P].bitcast(F32), 0.0)

                def qk_low(g):
                    n = number["turn", g]
                    dve.wait_ge(qk_hi_done, at(h, TURN, g + 1))
                    cols = slice(2 * P * g, 2 * P * (g + 1))
                    dve.tensor_tensor(qk_lo[:, :, cols], TP[:, n % 3, :].rearrange("p (q c) -> p q c", q=2),
                                      qk_hi[:, :, cols].bitcast(F32), ALU.subtract).then_inc(tp_free, 1)

                PARTS = sum(1 + (n > 1) for n in ROW_GROUPS)

                def maximum(i):
                    n, r = ROW_GROUPS[i], row(i)
                    cut = (0, 1, 2, 2)[n - 1]
                    parts = sum(1 + (m > 1) for m in ROW_GROUPS[:i + 1])
                    if n > 1:
                        dve.wait_ge(chunk_scored, at(h, CHUNKS, chunk_at[i] + cut))
                        dve.tensor_reduce(part_max[:, i, 0:1], r[:, 0:cut * BANK], AX.X, ALU.max).then_inc(part_max_done, 1)
                    dve.wait_ge(chunk_scored, at(h, CHUNKS, chunk_at[i] + n))
                    dve.tensor_reduce(part_max[:, i, 1:2], r[:, cut * BANK:width(i)], AX.X, ALU.max).then_inc(part_max_done, 1)
                    dve.wait_ge(part_max_done, at(h, PARTS, parts))
                    dve.tensor_scalar(neg_max[:, i:i + 1], part_max[:, i, 1:2],
                                      part_max[:, i, 0:1] if n > 1 else -3.4e38, -SCALE0,
                                      ALU.max, ALU.mult).then_inc(neg_max_done, 1)

                def row_low(i, g):
                    n = number["row", i, g]
                    m = min(4, width(i) // P - 4 * g)
                    dve.wait_ge(pT_hi_done, at(h, CHUNKS, chunk_at[i] + g + 1))
                    to = (slice(pair_at(i // 2) + 4 * g, pair_at(i // 2) + 4 * g + m), slice((i % 2) * P, (i % 2 + 1) * P))
                    dve.tensor_tensor(pT_lo[:, to[0], to[1]], TP[:, n % 3, 0:m * P].rearrange("p (b c) -> p b c", c=P),
                                      pT_hi[:, to[0], to[1]].bitcast(F32), ALU.subtract).then_inc(tp_free, 1)

                def pair_low(j):
                    dve.wait_ge(a_hi_done, at(h, PAIRS, j + 1))
                    dve.tensor_tensor(a_lo[:, j % 2, :], PV[:, 0:2 * P], a_hi[:, j % 2, :].bitcast(F32),
                                      ALU.subtract).then_inc(a_lo_done, 1)
                    dve.reciprocal(row_inv[:, 2 * j:2 * j + 2], row_sum[:, 2 * j:2 * j + 2]).then_inc(inv_done, 1)

                def accumulate(j):
                    n = number["out", j]
                    dve.wait_ge(pair_out, at(h, PAIRS, j + 1))
                    dve.wait_ge(inv_done, at(h, PAIRS, j + 1))
                    for q in range(2):
                        i = 2 * j + q
                        last = dve.scalar_tensor_tensor(out=Y[:, i, :], in0=TP[:, n % 3, q * D:(q + 1) * D],
                                                        scalar=row_inv[:, i:i + 1], in1=Y[:, i, :],
                                                        op0=ALU.mult, op1=ALU.add)
                    last.then_inc(tp_free, 1)

                for what, *which in VECTOR:
                    if what == "project":
                        multiply(*which)
                    elif what == "turn":
                        qk_low(*which)
                    elif what == "scores":
                        maximum(*which)
                    elif what == "row":
                        row_low(*which)
                    elif what == "mix":
                        pair_low(*which)
                    else:
                        accumulate(*which)


def ball_projection(nc, core, weight, scale, xT_hi, xT_lo, meanwhile):
    Y, TP = core.Y, core.TP
    with ExitStack() as ctx:
        def sb(n, shape, dt=F32):
            return ctx.enter_context(nc.sbuf_tensor("ball_" + n, shape, dt))

        def sem(n):
            return core.ctx.enter_context(nc.semaphore("ball_" + n))

        w_raw, w_hi, w_lo = sb("w_raw", [P, KT, D]), sb("w_hi", [P, KT, D], F32R), sb("w_lo", [P, KT, D], F32R)
        scale_all = sb("scale_all", [P, D])
        out, squares = sb("out", [P, TILES, D]), sb("squares", [P, 2, D])
        sq_sum, norm, v_norm, tanh, den, inv, factor, o_norm, bound = (sb(n, [P, TILES]) for n in (
            "sq_sum", "norm", "v_norm", "tanh", "den", "inv", "factor", "o_norm", "bound"))
        w_in, scale_in, w_hi_done, w_split, pair_done, out_done, squared, rooted, tanh_done, step = (sem(n) for n in (
            "w_in", "scale_in", "w_hi_done", "w_split", "pair_done", "out_done", "squared", "rooted", "tanh_done", "step"))
        zero = sb("zero", [P, 1])
        zeroed = sem("zeroed")

        def loads(sp):
            sp.dma_start(w_raw[:, :, :], weight.rearrange("(k p) n -> p k n", p=P)).then_inc(w_in, 16)
            sp.dma_start(scale_all[:, :], scale.partition_broadcast(P)).then_inc(scale_in, 16)

        def splits(pool):
            pool.memset(zero[:, :], 0.0).then_inc(zeroed, 1)
            pool.wait_ge(zeroed, 1)
            pool.wait_ge(w_in, 16)
            pool.tensor_tensor(w_hi[:, :, :], w_raw[:, :, :], zero[:, :].unsqueeze(2).to_broadcast([P, KT, D]), ALU.add).then_inc(w_hi_done, 1)
            pool.wait_ge(w_hi_done, 1)
            pool.tensor_tensor(w_lo[:, :, :], w_raw[:, :, :], w_hi[:, :, :].bitcast(F32), ALU.subtract).then_inc(w_split, 1)

        meanwhile(loads=loads, splits=splits)
        block = ctx.enter_context(nc.Block())

        @block.tensor
        def _(pe):
            pe.wait_ge(w_split, 1)
            for g in range(PAIRS):
                if g >= 3:
                    pe.wait_ge(out_done, g - 2)
                for j in range(2):
                    t = 2 * g + j
                    toks = slice(t * P, (t + 1) * P)
                    parts = [(x, w, k) for k in range(KT) for x, w in ((xT_hi, w_hi), (xT_hi, w_lo), (xT_lo, w_hi))]
                    for n, (x, w, k) in enumerate(parts):
                        last = pe.matmul(TP[:, g % 3, j * D:(j + 1) * D], x[:, k, toks], w[:, k, :],
                                         start=(n == 0), stop=(n == len(parts) - 1))
                last.then_inc(pair_done, 1)

        @block.scalar
        def _(act):
            for t in range(TILES):
                act.wait_ge(out_done, t // 2 + 1)
                if t >= 2:
                    act.wait_ge(squared, t - 1)
                act.activation(squares[:, t % 2, :], out[:, t, :], ACT.Square, accum_out=sq_sum[:, t:t + 1]).then_inc(squared, 1)
            act.wait_ge(squared, TILES)
            act.activation(norm[:, :], sq_sum[:, :], ACT.Sqrt).then_inc(rooted, 1)
            act.wait_ge(step, 1)
            act.activation(tanh[:, :], v_norm[:, :], ACT.Tanh).then_inc(tanh_done, 1)

        @block.vector
        def _(dve):
            dve.wait_ge(scale_in, 16)
            for g in range(PAIRS):
                dve.wait_ge(pair_done, g + 1)
                dve.tensor_tensor(out[:, 2 * g:2 * g + 2, :], TP[:, g % 3, :].rearrange("p (j n) -> p j n", j=2),
                                  scale_all[:, :].unsqueeze(1).to_broadcast([P, 2, D]), ALU.mult).then_inc(out_done, 1)
            dve.wait_ge(rooted, 1)
            dve.tensor_scalar(v_norm[:, :], norm[:, :], BALL_EPS, None, ALU.max).then_inc(step, 1)
            dve.wait_ge(step, 1)
            dve.tensor_scalar(den[:, :], v_norm[:, :], BALL_EPS, None, ALU.add).then_inc(step, 1)
            dve.wait_ge(step, 2)
            dve.reciprocal(inv[:, :], den[:, :]).then_inc(step, 1)
            dve.wait_ge(step, 3)
            dve.wait_ge(tanh_done, 1)
            dve.tensor_tensor(factor[:, :], tanh[:, :], inv[:, :], ALU.mult).then_inc(step, 1)
            dve.wait_ge(step, 4)
            dve.tensor_tensor(o_norm[:, :], norm[:, :], factor[:, :], ALU.mult).then_inc(step, 1)
            dve.wait_ge(step, 5)
            dve.tensor_scalar(o_norm[:, :], o_norm[:, :], BALL_EPS, None, ALU.max).then_inc(step, 1)
            dve.wait_ge(step, 6)
            dve.reciprocal(bound[:, :], o_norm[:, :]).then_inc(step, 1)
            dve.wait_ge(step, 7)
            dve.tensor_scalar(bound[:, :], bound[:, :], MAX_NORM, 1.0, ALU.mult, ALU.min).then_inc(step, 1)
            dve.wait_ge(step, 8)
            dve.tensor_tensor(factor[:, :], factor[:, :], bound[:, :], ALU.mult).then_inc(step, 1)
            dve.wait_ge(step, 9)
            for t in range(TILES):
                dve.scalar_tensor_tensor(out=Y[:, t, :], in0=out[:, t, :], scalar=factor[:, t:t + 1], in1=Y[:, t, :],
                                         op0=ALU.mult, op1=ALU.add)


def window_ring(first, last):
    items = []
    if first:
        items += [("kv", 0), ("kv", 1), ("queries", 0, 0), ("keys", 0)] + [("queries", 0, r) for r in range(1, REP)]
    for s in range(TILES + (WINDOW_LAG if last else 0)):
        if has_unit(s - 2, first):
            items += [("probs", s - 2, 0), ("probs", s - 2, 1)]
        items += window_ahead(s, last)
        if has_unit(s - 4, first):
            items.append(("out", s - 4))
    held, ring = [-3, -2, -1], {}
    extra = -len(items) % 3
    skips = {len(items) // 3 * (n + 1) for n in range(extra)} if not last else set()
    bank = 0
    for n, item in enumerate(items):
        if n in skips:
            bank = (bank + 1) % 3
        ring[item] = (n, bank, held[bank])
        held[bank] = n
        bank = (bank + 1) % 3
    return ring


BLOCKS, PER_BLOCK = T // BANK, BANK // P
WINDOW_LAG = 4


def has_unit(t, first):
    return (t >= 0 or not first) and t < TILES


def scores_late(s):
    return s % PER_BLOCK == 0


def window_ahead(s, last):
    c, r = s // PER_BLOCK + 1, s % PER_BLOCK
    if s >= TILES or (last and c == BLOCKS):
        return []
    ahead = [[("kv", 2 * c)], [("kv", 2 * c + 1)], [("keys", c)], []][r]
    if c < BLOCKS:
        return ahead + [("queries", c, r)]
    return ahead + [("queries", c, n) for n in ((), (0,), (1,), (2, 3))[r]]


def window_attention(nc, core, consts, wq, wkv, wo, xT_hi, xT_lo, meanwhile):
    Y, ident, S, TP, PV = core.Y, core.ident, core.S, core.TP, core.PV
    QUERIES = BLOCKS * REP
    KEYS = T + P
    PER = 2 * TILES + BLOCKS * REP + PAIRS + BLOCKS + TILES
    RINGS = {(first, last): window_ring(first, last) for first, last in ((True, False), (False, False), (False, True))}
    BEFORE = RINGS[False, False]
    assert len(RINGS[False, False]) == PER and len(RINGS[True, False]) == PER - 1
    with ExitStack() as ctx:
        def sb(n, shape, dt=F32):
            return ctx.enter_context(nc.sbuf_tensor("l1_" + n, shape, dt))

        def sem(n):
            return core.ctx.enter_context(nc.semaphore("l1_" + n))

        wq_raw = sb("wq_raw", [P, KT, REP * HD])
        wq_hi, wq_lo = sb("wq_hi", [P, KT, REP * HD], F32R), sb("wq_lo", [P, KT, REP * HD], F32R)
        wkv_raw = sb("wkv_raw", [P, KT, 2 * HD])
        wkv_hi, wkv_lo = sb("wkv_hi", [P, KT, 2 * HD], F32R), sb("wkv_lo", [P, KT, 2 * HD], F32R)
        wo_raw = sb("wo_raw", [P, REP, D])
        wo_hi, wo_lo = sb("wo_hi", [P, REP, D], F32R), sb("wo_lo", [P, REP, D], F32R)
        mask, masked = sb("mask", [P, 2, 2 * P]), sb("masked", [P, 2, REP, 2 * P])
        zero = sb("zero", [P, 1])
        k_nat = sb("k_nat", [P, 4, HD])
        kT_hi, kT_lo = sb("kT_hi", [P, KEYS], F32R), sb("kT_lo", [P, KEYS], F32R)
        v_hi, v_lo = sb("v_hi", [P, TILES + 1, HD], F32R), sb("v_lo", [P, TILES + 1, HD], F32R)
        qT_hi, qT_lo = sb("qT_hi", [P, 2, REP, BANK], F32R), sb("qT_lo", [P, 2, REP, BANK], F32R)
        probs = sb("probs", [P, 4, REP, 2 * P])
        pT_hi, pT_lo = (sb(n, [P, 2, 2, REP, P], F32R) for n in ("pT_hi", "pT_lo"))
        a_hi, a_lo = sb("a_hi", [P, 2, REP, P], F32R), sb("a_lo", [P, 2, REP, P], F32R)
        row_max, neg_max = sb("row_max", [P, TILES, REP]), sb("neg_max", [P, TILES, REP])
        row_sum, row_inv = sb("row_sum", [P, TILES, REP]), sb("row_inv", [P, TILES, REP])

        consts_in, wkv_in, wq_in, wo_in, w_split, padded, part = (sem(n) for n in (
            "consts_in", "wkv_in", "wq_in", "wo_in", "w_split", "padded", "part"))
        kv_projected, v_hi_done, keys_turned, kT_hi_done, q_projected, qT_hi_done = (sem(n) for n in (
            "kv_projected", "v_hi_done", "keys_turned", "kT_hi_done", "q_projected", "qT_hi_done"))
        scored, max_done, neg_max_done, exped, inv_done, normed, p_turned, pT_hi_done, tp_free = (sem(n) for n in (
            "scored", "max_done", "neg_max_done", "exped", "inv_done", "normed", "p_turned", "pT_hi_done", "tp_free"))
        mixed, a_hi_done, a_lo_done, projected = (sem(n) for n in ("mixed", "a_hi_done", "a_lo_done", "projected"))

        def scores_of(t, r):
            return S[:, 2 * (t % 2) + r // 2, (r % 2) * 2 * P:(r % 2 + 1) * 2 * P]

        def freed(h, first, n):
            return n + 1 if first else at(h, PER, n)

        def loads(sp):
            sp.dma_start(wkv_raw[:, :, :], wkv[0, :, :, :]).then_inc(wkv_in, 16)
            sp.dma_start(wq_raw[:, :, :], wq[0, :, :, :]).then_inc(wq_in, 16)
            sp.dma_start(mask[:, :, :].rearrange("p a c -> p (a c)"), consts[:, CONST["window"][0]:CONST["window"][1]]).then_inc(consts_in, 16)
            sp.dma_start(wo_raw[:, :, :], wo[0, :, :, :]).then_inc(wo_in, 16)

        def split(pool, h, n):
            raw, hi, lo, arrived = ((wkv_raw, wkv_hi, wkv_lo, wkv_in), (wq_raw, wq_hi, wq_lo, wq_in),
                                    (wo_raw, wo_hi, wo_lo, wo_in))[n]
            pool.wait_ge(arrived, at(h, 16, 16))
            pool.tensor_tensor(hi[:, :, :], raw[:, :, :], zero[:, :].unsqueeze(2).to_broadcast(raw.shape), ALU.add).then_inc(part, 1)
            pool.wait_ge(part, at(h, 3, n + 1))
            pool.tensor_tensor(lo[:, :, :], raw[:, :, :], hi[:, :, :].bitcast(F32), ALU.subtract).then_inc(w_split, 1)

        def splits(pool):
            for z in (kT_hi[:, 0:P], kT_lo[:, 0:P], v_hi[:, 0, :], v_lo[:, 0, :]):
                pool.memset(z.bitcast(F32), 0.0).then_inc(padded, 1)
            pool.memset(zero[:, :], 0.0).then_inc(padded, 1)
            pool.wait_ge(padded, 5)
            split(pool, 0, 0)
            split(pool, 0, 1)

        meanwhile(loads=loads, splits=splits)
        block = ctx.enter_context(nc.Block())

        @block.sync
        def _(sp):
            with sp.Fori(1, HKV) as h:
                sp.wait_ge(w_split, at(h, 3, -2))
                sp.dma_start(wkv_raw[:, :, :], wkv[h, :, :, :]).then_inc(wkv_in, 16)
                sp.wait_ge(w_split, at(h, 3, -1))
                sp.dma_start(wq_raw[:, :, :], wq[h, :, :, :]).then_inc(wq_in, 16)
                sp.wait_ge(w_split, at(h, 3, 0))
                sp.dma_start(wo_raw[:, :, :], wo[h, :, :, :]).then_inc(wo_in, 16)

        @block.gpsimd
        def _(pool):
            def turn(h, first=False, last=False):
                for t in range(TILES):
                    if t == WINDOW_LAG - 1:
                        if not first:
                            pool.wait_ge(projected, at(h, TILES, 0))
                        split(pool, h, 2)
                    pool.wait_ge(inv_done, at(h, TILES, t + 1))
                    pool.tensor_tensor(probs[:, t % 4, :, :], probs[:, t % 4, :, :],
                                       row_inv[:, t, :].unsqueeze(2).to_broadcast([P, REP, 2 * P]),
                                       ALU.mult).then_inc(normed, 1)
                    if t == 9 and not last:
                        pool.wait_ge(kv_projected, at(h, PAIRS, PAIRS))
                        split(pool, h + 1, 0)
                    if t == 11 and not last:
                        pool.wait_ge(q_projected, at(h, QUERIES, QUERIES))
                        split(pool, h + 1, 1)

            turn(0, first=True)
            with pool.Fori(1, HKV - 1) as h:
                turn(h)
            turn(HKV - 1, last=True)

        @block.tensor
        def _(pe):
            def turn(h, first=False, last=False):
                ring = RINGS[first, last]

                def bank(item):
                    n, b, held = ring[item]
                    if held >= 0 or not first:
                        pe.wait_ge(tp_free, freed(h, first, held))
                    return TP[:, b, :]

                def project_kv(u):
                    out = bank(("kv", u))
                    pe.wait_ge(w_split, at(h, 3, 4 if u >= PAIRS else 1))
                    for j in range(2):
                        t = (2 * u + j) % TILES
                        toks = slice(t * P, (t + 1) * P)
                        parts = [(x, w, k) for k in range(KT) for x, w in ((xT_hi, wkv_hi), (xT_hi, wkv_lo), (xT_lo, wkv_hi))]
                        for n, (x, w, k) in enumerate(parts):
                            last_product = pe.matmul(out[:, j * 2 * HD:(j + 1) * 2 * HD], x[:, k, toks], w[:, k, :],
                                                     start=(n == 0), stop=(n == len(parts) - 1))
                    last_product.then_inc(kv_projected, 1)

                def turn_keys(c):
                    out = bank(("keys", c))
                    pe.wait_ge(v_hi_done, at(h, PAIRS, 2 * c + 2))
                    for b in range(4):
                        move = pe.transpose(out[:, b * P:(b + 1) * P], k_nat[:, b, :], ident[:, :])
                    move.then_inc(keys_turned, 1)

                def project_q(c, r):
                    out = bank(("queries", c, r))
                    pe.wait_ge(w_split, at(h, 3, 5 if c == BLOCKS else 2))
                    toks = slice((c % BLOCKS) * BANK, (c % BLOCKS + 1) * BANK)
                    parts = [(w, x, k) for k in range(KT) for w, x in ((wq_hi, xT_hi), (wq_hi, xT_lo), (wq_lo, xT_hi))]
                    for n, (w, x, k) in enumerate(parts):
                        last_product = pe.matmul(out, w[:, k, r * HD:(r + 1) * HD], x[:, k, toks],
                                                 start=(n == 0), stop=(n == len(parts) - 1))
                    last_product.then_inc(q_projected, 1)

                def scores(t):
                    if t % PER_BLOCK == 0:
                        if t == 0 and not first:
                            n = BEFORE["queries", BLOCKS, REP - 1][0] - PER
                        else:
                            n = ring["queries", t // PER_BLOCK, REP - 1][0]
                        pe.wait_ge(tp_free, freed(h, first, n))
                    if t >= 2 or not first:
                        pe.wait_ge(max_done, at(h, TILES, t - 1))
                    keys = slice(t * P, (t + 2) * P)
                    for r in range(REP):
                        out = scores_of(t, r)
                        toks = slice((t % REP) * P, (t % REP + 1) * P)
                        hi, lo = (q[:, (t // PER_BLOCK) % 2, r, toks] for q in (qT_hi, qT_lo))
                        pe.matmul(out, hi, kT_hi[:, keys], start=True, stop=False)
                        pe.matmul(out, hi, kT_lo[:, keys], start=False, stop=False)
                        last_product = pe.matmul(out, lo, kT_hi[:, keys], start=False, stop=True)
                    last_product.then_inc(scored, 1)

                def turn_probs(t):
                    pe.wait_ge(normed, at(h, TILES, t + 1))
                    for b in range(2):
                        out = bank(("probs", t, b))
                        for r in range(REP):
                            move = pe.transpose(out[:, r * P:(r + 1) * P], probs[:, t % 4, r, b * P:(b + 1) * P], ident[:, :])
                        move.then_inc(p_turned, 1)

                def mix(t):
                    n = ring["probs", t, 1][0] if ("probs", t, 1) in ring else BEFORE["probs", t + TILES, 1][0] - PER
                    pe.wait_ge(tp_free, freed(h, first, n))
                    if t >= 1 or not first:
                        pe.wait_ge(a_lo_done, at(h, TILES, t))
                    for b in range(2):
                        hi, lo = (p[:, t % 2, b, :, :].rearrange("p r c -> p (r c)") for p in (pT_hi, pT_lo))
                        v = t % TILES + b
                        pe.matmul(PV[:, :], v_hi[:, v, :], hi, start=(b == 0), stop=False)
                        pe.matmul(PV[:, :], v_hi[:, v, :], lo, start=False, stop=False)
                        last_product = pe.matmul(PV[:, :], v_lo[:, v, :], hi, start=False, stop=(b == 1))
                    last_product.then_inc(mixed, 1)

                def project(t):
                    out = bank(("out", t))[:, 0:D]
                    pe.wait_ge(a_lo_done, at(h, TILES, t + 1))
                    pe.wait_ge(w_split, at(h, 3, 3 if t >= 0 else 0))
                    for r in range(REP):
                        hi, lo = a_hi[:, t % 2, r, :], a_lo[:, t % 2, r, :]
                        pe.matmul(out, hi, wo_hi[:, r, :], start=(r == 0), stop=False)
                        pe.matmul(out, hi, wo_lo[:, r, :], start=False, stop=False)
                        last_product = pe.matmul(out, lo, wo_hi[:, r, :], start=False, stop=(r == REP - 1))
                    last_product.then_inc(projected, 1)

                if first:
                    project_kv(0)
                    project_kv(1)
                    project_q(0, 0)
                    turn_keys(0)
                    for r in range(1, REP):
                        project_q(0, r)
                for s in range(TILES + (WINDOW_LAG if last else 0)):
                    late = scores_late(s)
                    if s < TILES and not late:
                        scores(s)
                    if has_unit(s - 2, first):
                        turn_probs(s - 2)
                    if s < TILES and late:
                        scores(s)
                    if has_unit(s - 3, first):
                        mix(s - 3)
                    for what, *which in window_ahead(s, last):
                        {"kv": project_kv, "keys": turn_keys, "queries": project_q}[what](*which)
                    if has_unit(s - 4, first):
                        project(s - 4)

            pe.wait_ge(padded, 4)
            turn(0, first=True)
            with pe.Fori(1, HKV - 1) as h:
                turn(h)
            turn(HKV - 1, last=True)

        @block.scalar
        def _(act):
            def turn(h, first=False, last=False):
                ring = RINGS[first, last]

                def kv_out(u):
                    pair = TP[:, ring["kv", u][1], :].rearrange("p (j c) -> p j c", j=2)
                    act.wait_ge(kv_projected, at(h, PAIRS, u + 1))
                    if u >= 2:
                        act.wait_ge(keys_turned, at(h, BLOCKS, u // 2))
                    act.activation(k_nat[:, 2 * u % 4:2 * u % 4 + 2, :], pair[:, :, 0:HD], ACT.Copy)
                    t = 2 * u % TILES + 1
                    act.activation(v_hi[:, t:t + 2, :], pair[:, :, HD:2 * HD], ACT.Copy).then_inc(v_hi_done, 1)

                def keys_high(c):
                    act.wait_ge(keys_turned, at(h, BLOCKS, c + 1))
                    to = P + (c % BLOCKS) * BANK
                    act.activation(kT_hi[:, to:to + BANK], TP[:, ring["keys", c][1], :], ACT.Copy).then_inc(kT_hi_done, 1)

                def queries_high(c, r):
                    act.wait_ge(q_projected, at(h, QUERIES, REP * c + r + 1))
                    act.activation(qT_hi[:, c % 2, r, :], TP[:, ring["queries", c, r][1], :], ACT.Copy).then_inc(qT_hi_done, 1)

                if first:
                    kv_out(0)
                    kv_out(1)
                    queries_high(0, 0)
                    keys_high(0)
                    for r in range(1, REP):
                        queries_high(0, r)
                for s in range(TILES + (WINDOW_LAG if last else 0)):
                    if has_unit(s - 2, first):
                        t = s - 2
                        for b in range(2):
                            act.wait_ge(p_turned, at(h, 2 * TILES, 2 * t + b + 1))
                            act.activation(pT_hi[:, t % 2, b, :, :],
                                           TP[:, ring["probs", t, b][1], :].rearrange("p (r c) -> p r c", r=REP),
                                           ACT.Copy).then_inc(pT_hi_done, 1)
                    if s < TILES:
                        act.wait_ge(neg_max_done, at(h, TILES, s + 1))
                        if s >= 4 or not first:
                            act.wait_ge(p_turned, at(h, 2 * TILES, 2 * (s - 4) + 2))
                        for r in range(REP):
                            last_row = act.activation(probs[:, s % 4, r, :], masked[:, s % 2, r, :],
                                                      ACT.Exp, bias=neg_max[:, s, r:r + 1], scale=SCALE1,
                                                      accum_out=row_sum[:, s, r:r + 1])
                        last_row.then_inc(exped, 1)
                    for what, *which in window_ahead(s, last):
                        {"kv": kv_out, "keys": keys_high, "queries": queries_high}[what](*which)
                    if has_unit(s - 3, first):
                        t = s - 3
                        act.wait_ge(mixed, at(h, TILES, t + 1))
                        if t >= 2 or not first:
                            act.wait_ge(projected, at(h, TILES, t - 1))
                        act.activation(a_hi[:, t % 2, :, :], PV[:, :].rearrange("p (r c) -> p r c", r=REP), ACT.Copy).then_inc(a_hi_done, 1)

            turn(0, first=True)
            with act.Fori(1, HKV - 1) as h:
                turn(h)
            turn(HKV - 1, last=True)

        @block.vector
        def _(dve):
            def turn(h, first=False, last=False):
                ring = RINGS[first, last]

                def values_low(u):
                    pair = TP[:, ring["kv", u][1], :].rearrange("p (j c) -> p j c", j=2)
                    t = 2 * u % TILES + 1
                    dve.wait_ge(v_hi_done, at(h, PAIRS, u + 1))
                    dve.tensor_tensor(v_lo[:, t:t + 2, :], pair[:, :, HD:2 * HD], v_hi[:, t:t + 2, :].bitcast(F32),
                                      ALU.subtract).then_inc(tp_free, 1)

                def keys_low(c):
                    cols = slice(P + (c % BLOCKS) * BANK, P + (c % BLOCKS + 1) * BANK)
                    dve.wait_ge(kT_hi_done, at(h, BLOCKS, c + 1))
                    dve.tensor_tensor(kT_lo[:, cols], TP[:, ring["keys", c][1], :], kT_hi[:, cols].bitcast(F32),
                                      ALU.subtract).then_inc(tp_free, 1)

                def inverse(t):
                    dve.wait_ge(exped, at(h, TILES, t + 1))
                    dve.reciprocal(row_inv[:, t % TILES, :], row_sum[:, t % TILES, :]).then_inc(inv_done, 1)

                def maximum(t):
                    dve.wait_ge(scored, at(h, TILES, t + 1))
                    if t >= 1 or not first:
                        inverse(t - 1)
                    for r in range(REP):
                        last_row = dve.tensor_tensor_reduce(masked[:, t % 2, r, :], scores_of(t, r), mask[:, min(t, 1), :],
                                                            1.0, -3.4e38, ALU.add, ALU.max, row_max[:, t, r:r + 1])
                    last_row.then_inc(max_done, 1)
                    dve.wait_ge(max_done, at(h, TILES, t + 1))
                    dve.tensor_scalar(neg_max[:, t, :], row_max[:, t, :], -SCALE1, None, ALU.mult).then_inc(neg_max_done, 1)

                def queries_low(c, r):
                    dve.wait_ge(qT_hi_done, at(h, QUERIES, REP * c + r + 1))
                    dve.tensor_tensor(qT_lo[:, c % 2, r, :], TP[:, ring["queries", c, r][1], :], qT_hi[:, c % 2, r, :].bitcast(F32),
                                      ALU.subtract).then_inc(tp_free, 1)

                if first:
                    values_low(0)
                    values_low(1)
                    queries_low(0, 0)
                    keys_low(0)
                    for r in range(1, REP):
                        queries_low(0, r)
                for s in range(TILES + (WINDOW_LAG if last else 0)):
                    late = scores_late(s)
                    if s < TILES and not late:
                        maximum(s)
                    if has_unit(s - 2, first):
                        t = s - 2
                        for b in range(2):
                            dve.wait_ge(pT_hi_done, at(h, 2 * TILES, 2 * t + b + 1))
                            low = dve.tensor_tensor(pT_lo[:, t % 2, b, :, :],
                                                    TP[:, ring["probs", t, b][1], :].rearrange("p (r c) -> p r c", r=REP),
                                                    pT_hi[:, t % 2, b, :, :].bitcast(F32), ALU.subtract)
                            low.then_inc(tp_free, 1)
                    if s < TILES and late:
                        maximum(s)
                    for what, *which in window_ahead(s, last):
                        {"kv": values_low, "keys": keys_low, "queries": queries_low}[what](*which)
                    if has_unit(s - 3, first):
                        t = s - 3
                        dve.wait_ge(a_hi_done, at(h, TILES, t + 1))
                        dve.tensor_tensor(a_lo[:, t % 2, :, :], PV[:, :].rearrange("p (r c) -> p r c", r=REP),
                                          a_hi[:, t % 2, :, :].bitcast(F32), ALU.subtract).then_inc(a_lo_done, 1)
                    if has_unit(s - 4, first):
                        t = s - 4
                        dve.wait_ge(projected, at(h, TILES, t + 1))
                        dve.tensor_tensor(Y[:, t % TILES, :], TP[:, ring["out", t][1], 0:D], Y[:, t % TILES, :], ALU.add).then_inc(tp_free, 1)
                    if s == TILES - 1 and last:
                        inverse(s)

            dve.wait_ge(consts_in, 16)
            turn(0, first=True)
            with dve.Fori(1, HKV - 1) as h:
                turn(h)
            turn(HKV - 1, last=True)


def expert_mix(nc, core, consts, gate_w, sw_gu, sw_down, w_gu, w_down, xT, x_rows, routed, meanwhile, afterwards):
    Y, ident, S, TP, PV = core.Y, core.ident, core.S, core.TP, core.PV
    HALF_I = INNER // 2
    PIECES = INNER_S // HALF_I
    RING = 4
    NOWHERE = 4096.0
    INFO = 6

    def first(i):
        return isinstance(i, int) and i == 0

    def in_range(i, u, back):
        return not isinstance(i, int) or 0 <= RING * i + u - back < E

    with ExitStack() as ctx:
        def sb(n, shape, dt=F32):
            return ctx.enter_context(nc.sbuf_tensor("moe_" + n, shape, dt))

        def sem(n):
            return core.ctx.enter_context(nc.semaphore("moe_" + n))

        iota, before, lower, where = sb("iota", [P, P]), sb("before", [P, P]), sb("lower", [P, E * E]), sb("where", [P, 2, TILES])
        before16, ones16, lower16 = sb("before16", [P, P], BF16), sb("ones16", [P, P], BF16), sb("lower16", [P, E, E], BF16)
        gw, gateT = sb("gw", [P, KT, E]), sb("gateT", [E, T])
        sgu, sdown = sb("sgu", [P, KT, 2 * INNER_S]), sb("sdown", [HALF_I, PIECES, D])
        wgu, wdown = sb("wgu", [P, RING, KT, 2 * INNER]), sb("wdown", [HALF_I, RING, 2, D])
        zeros = sb("zeros", [P, TILES // 2 * D])
        top, total, total_inv, gain_sum, gain_inv = (sb(n, [P, TILES]) for n in ("top", "total", "total_inv", "gain_sum", "gain_inv"))
        shifted, exps, score, above, chosen, gain, rest, slot = (sb(n, [P, TILES, E]) for n in (
            "shifted", "exps", "score", "above", "chosen", "gain", "rest", "slot"))
        greater, equal = sb("greater", [P, TILES, E, E], BF16), sb("equal", [P, TILES, E, E], BF16)
        chosen16, info = sb("chosen16", [P, TILES, E], BF16), sb("info", [P, TILES, E, INFO], BF16)
        onehot = sb("onehot", [P, 2, TILES, P], BF16)
        slots = sb("slots", [P, E, INFO])
        token_a, token_b, token = sb("token_a", [P, E]), sb("token_b", [P, E]), sb("token", [P, E], mybir.dt.uint32)
        slot_gain_a, slot_gain = sb("slot_gain_a", [P, E]), sb("slot_gain", [P, E])
        s_act, s_mid = sb("s_act", [P, 2, INNER_S]), sb("s_mid", [P, 2, INNER_S])
        s_midT = sb("s_midT", [HALF_I, 2, PIECES, P])
        xg, xgT = sb("xg", [P, RING, D]), sb("xgT", [P, 2, KT, P])
        e_act, e_mid = sb("e_act", [P, 2, INNER]), sb("e_mid", [P, 2, INNER])
        e_midT, e_out = sb("e_midT", [HALF_I, 2, 2, P]), sb("e_out", [P, 2, D])
        y_routed = [sb(f"y_routed{n}", [P, TILES, D]) for n in range(2)]

        consts_in, gw_in, shared_in, consts_cast, zeroed, cleared, out_free, ring_set = (sem(n) for n in (
            "consts_in", "gw_in", "shared_in", "consts_cast", "zeroed", "cleared", "out_free", "ring_set"))
        weights_in = [sem(f"weights_in{n}") for n in range(RING)]
        gathered = [sem(f"gathered{n}") for n in range(RING)]
        gate_done, gate_out, logits_done, shift_done, exps_done, route, rank_done, onehot_done, info_done = (sem(n) for n in (
            "gate_done", "gate_out", "logits_done", "shift_done", "exps_done", "route", "rank_done", "onehot_done", "info_done"))
        s_up_done, s_act_done, s_mixed, s_turned, s_midT_done, s_down_done, s_added = (sem("s_" + n) for n in (
            "up_done", "act_done", "mixed", "turned", "midT_done", "down_done", "added"))
        x_turned, xgT_done, up_done, act_done, mixed, turned, midT_done, down_done, out_done = (sem("e_" + n) for n in (
            "x_turned", "xgT_done", "up_done", "act_done", "mixed", "turned", "midT_done", "down_done", "out_done"))
        added = [sem(f"added{n}") for n in range(2)]
        y_in = [sem(f"y_in{n}") for n in range(4)]
        ROUTE = {n: k + 1 for k, n in enumerate((
            "top", "total", "total_inv", "score", "greater", "equal", "equal_lower", "greater_equal", "above", "chosen", "chosen16",
            "gain_raw", "gain_sum", "gain_eps", "gain_inv", "gain", "high", "high_rest", "middle", "middle_rest", "low",
            "numbers", "tiles", "ones", "away", "slot",
            "slots", "token_a", "token_b", "token", "gain_a", "slot_gain"))}

        def loads(sp):
            for n, to in (("iota", iota[:, :]), ("before", before[:, :]), ("lower", lower[:, :]),
                          ("where", where[:, :, :].rearrange("p a t -> p (a t)"))):
                sp.dma_start(to, consts[:, CONST[n][0]:CONST[n][1]]).then_inc(consts_in, 16)
            sp.dma_start(gw[:, :, :], gate_w).then_inc(gw_in, 16)
            sp.dma_start(sgu[:, :, :], sw_gu).then_inc(shared_in, 16)
            sp.dma_start(sdown[:, :, :], sw_down).then_inc(shared_in, 16)

        def splits(pool):
            pool.memset(zeros[:, :], 0.0).then_inc(zeroed, 1)
            pool.memset(xg[:, :, :], 0.0).then_inc(ring_set, 1)

        meanwhile(loads=loads, splits=splits)
        stage = ctx.enter_context(ExitStack())
        block = stage.enter_context(nc.Block())

        @block.sync
        def _(sp):
            sp.wait_ge(zeroed, 1)
            for n in range(2):
                for to in routed:
                    sp.dma_start(rows(to)[:, n * TILES // 2:(n + 1) * TILES // 2, :],
                                 zeros[:, :].rearrange("p (t d) -> p t d", d=D)).then_inc(cleared, 16)
            for u in range(RING):
                sp.dma_start(wgu[:, u, :, :], w_gu[u, :, :, :]).then_inc(weights_in[u], 16)
                sp.dma_start(wdown[:, u, :, :], w_down[u, :, :, :]).then_inc(weights_in[u], 16)
            with sp.Fori(1, E // RING) as i:
                for u in range(RING):
                    sp.wait_ge(up_done, at(i, RING, u - RING + 1))
                    sp.dma_start(wgu[:, u, :, :], w_gu[RING * i + u, :, :, :]).then_inc(weights_in[u], 16)
                    sp.wait_ge(down_done, at(i, RING, u - RING + 1))
                    sp.dma_start(wdown[:, u, :, :], w_down[RING * i + u, :, :, :]).then_inc(weights_in[u], 16)
            for n in range(2):
                sp.wait_ge(added[n], 16 * E // 2)
            for n in range(4):
                for to, y in zip(routed, y_routed):
                    sp.dma_start(y[:, 4 * n:4 * n + 4, :], rows(to)[:, 4 * n:4 * n + 4, :]).then_inc(y_in[n], 16)

        @block.gpsimd
        def _(pool):
            pool.sem_inc(out_free, 1)
            pool.wait_ge(ring_set, 1)
            pool.wait_ge(cleared, 64)

            def gather(e):
                if e >= RING:
                    pool.wait_ge(x_turned, e - RING + 1)
                pool.indirect_dma_start(xg[:, e % RING, :], None, x_rows, bass.IndirectOffsetOnAxis(ap=token[:, e:e + 1], axis=0),
                                        bounds_check=T - 1, oob_is_err=False).then_inc(gathered[e % RING], 16)

            def scatter(e):
                if e >= 2:
                    pool.wait_ge(added[e % 2], 16 * (e // 2))
                    pool.sem_inc(out_free, 1)
                pool.wait_ge(out_done, e + 1)
                pool.indirect_dma_start(routed[e % 2], bass.IndirectOffsetOnAxis(ap=token[:, e:e + 1], axis=0), e_out[:, e % 2, :], None,
                                        bounds_check=T - 1, oob_is_err=False, compute_op=ALU.add).then_inc(added[e % 2], 16)

            pool.wait_ge(route, ROUTE["token"])
            AHEAD = RING + 2
            for e in range(AHEAD):
                gather(e)
            for e in range(E):
                if e + AHEAD < E:
                    gather(e + AHEAD)
                scatter(e)

        @block.tensor
        def _(pe):
            pe.wait_ge(gw_in, 16)
            for c in range(T // BANK):
                for k in range(KT):
                    last = pe.matmul(S[0:E, c, :], gw[:, k, :], xT[:, k, c * BANK:(c + 1) * BANK], start=(k == 0), stop=(k == KT - 1))
                last.then_inc(gate_done, 1)
            for t in range(TILES):
                pe.wait_ge(gate_out, t // PER_BLOCK + 1)
                last = pe.transpose(PV[:, t * E:(t + 1) * E], gateT[:, t * P:(t + 1) * P], ident[0:E, 0:E])
            last.then_inc(logits_done, 1)
            pe.wait_ge(shared_in, 32)

            def s_up(t):
                if t >= 2:
                    pe.wait_ge(s_mixed, t - 1)
                for half in range(2):
                    for k in range(KT):
                        last = pe.matmul(S[:, (2 * t + half) % 4, 0:INNER_S], xT[:, k, t * P:(t + 1) * P],
                                         sgu[:, k, half * INNER_S:(half + 1) * INNER_S], start=(k == 0), stop=(k == KT - 1))
                last.then_inc(s_up_done, 1)

            def s_turn(t):
                pe.wait_ge(s_mixed, t + 1)
                if t >= 1:
                    pe.wait_ge(s_midT_done, t)
                for c in range(PIECES):
                    last = pe.transpose(TP[0:HALF_I, 0, c * P:(c + 1) * P], s_mid[:, t % 2, c * HALF_I:(c + 1) * HALF_I], ident[:, :])
                last.then_inc(s_turned, 1)

            def s_down(t):
                pe.wait_ge(s_midT_done, t + 1)
                if t >= 2:
                    pe.wait_ge(s_added, t - 1)
                for c in range(PIECES):
                    last = pe.matmul(TP[:, 1 + t % 2, 0:D], s_midT[:, t % 2, c, :], sdown[:, c, :], start=(c == 0), stop=(c == PIECES - 1))
                last.then_inc(s_down_done, 1)

            def ranks():
                pe.wait_ge(route, ROUTE["chosen16"])
                pe.wait_ge(consts_cast, 3)
                pe.matmul(PV[:, 0:TILES * E], before16[:, :], chosen16[:, :, :].rearrange("p t e -> p (t e)"), start=True, stop=False)
                for d in range(1, TILES):
                    last = pe.matmul(PV[:, d * E:TILES * E], ones16[:, :], chosen16[:, 0:TILES - d, :].rearrange("p t e -> p (t e)"),
                                     start=False, stop=(d == TILES - 1))
                last.then_inc(rank_done, 1)

            def slot_info(e):
                pe.wait_ge(onehot_done, e + 1)
                pe.wait_ge(route, ROUTE["slot"])
                for t in range(TILES):
                    last = pe.matmul(PV[:, e * INFO:(e + 1) * INFO], onehot[:, e % 2, t, :], info[:, t, e, :], start=(t == 0), stop=(t == TILES - 1))
                last.then_inc(info_done, 1)

            for s in range(TILES + 2):
                if s < TILES:
                    s_up(s)
                if 1 <= s <= TILES:
                    s_turn(s - 1)
                if s >= 2:
                    s_down(s - 2)
                if s == 5:
                    ranks()
                if 7 <= s < 7 + E // 2:
                    slot_info(2 * (s - 7))
                    slot_info(2 * (s - 7) + 1)

            def x_turn(i, u):
                pe.wait_ge(gathered[u], at(i, 16, 16))
                if not (first(i) and u == 0):
                    pe.wait_ge(xgT_done, at(i, RING, u))
                for k in range(KT):
                    last = pe.transpose(TP[:, 0, k * P:(k + 1) * P], xg[:, u, k * P:(k + 1) * P], ident[:, :])
                last.then_inc(x_turned, 1)

            def up(i, u, ring):
                pe.wait_ge(xgT_done, at(i, RING, u + 1))
                pe.wait_ge(weights_in[ring], at(i, 32, 32) if u == ring else at(i, 32, 0))
                for k in range(KT):
                    last = pe.matmul(S[:, ring, 0:2 * INNER], xgT[:, ring % 2, k, :], wgu[:, ring, k, :], start=(k == 0), stop=(k == KT - 1))
                last.then_inc(up_done, 1)

            def turn(i, u, ring):
                pe.wait_ge(mixed, at(i, RING, u + 1))
                if not (first(i) and u == 0):
                    pe.wait_ge(midT_done, at(i, RING, u))
                for c in range(2):
                    last = pe.transpose(TP[0:HALF_I, 1, c * P:(c + 1) * P], e_mid[:, ring % 2, c * HALF_I:(c + 1) * HALF_I], ident[:, :])
                last.then_inc(turned, 1)

            def down(i, u, ring):
                pe.wait_ge(midT_done, at(i, RING, u + 1))
                if not (first(i) and u == 0):
                    pe.wait_ge(out_done, at(i, RING, u))
                for c in range(2):
                    last = pe.matmul(TP[:, 2, 0:D], e_midT[:, ring % 2, c, :], wdown[:, ring, c, :], start=(c == 0), stop=(c == 1))
                last.then_inc(down_done, 1)

            pe.wait_ge(s_added, TILES)
            pe.wait_ge(route, ROUTE["slots"])

            def steps(i, us):
                for u in us:
                    if in_range(i, u, 0):
                        x_turn(i, u)
                    for back, stage in ((1, up), (2, turn), (3, down)):
                        if in_range(i, u, back):
                            stage(i, u - back, (u - back) % RING)

            steps(0, range(RING))
            with pe.Fori(1, E // RING) as i:
                steps(i, range(RING))
            steps(E // RING, range(3))

        @block.scalar
        def _(act):
            for c in range(T // BANK):
                act.wait_ge(gate_done, c + 1)
                act.activation(gateT[:, c * BANK:(c + 1) * BANK], S[0:E, c, :], ACT.Copy).then_inc(gate_out, 1)
            act.wait_ge(shift_done, 1)
            act.activation(exps[:, :, :], shifted[:, :, :], ACT.Exp).then_inc(exps_done, 1)
            for s in range(TILES + 1):
                if s < TILES:
                    act.wait_ge(s_up_done, s + 1)
                    if s >= 2:
                        act.wait_ge(s_mixed, s - 1)
                    act.activation(s_act[:, s % 2, :], S[:, (2 * s) % 4, 0:INNER_S], ACT.Silu).then_inc(s_act_done, 1)
                if s >= 1:
                    t = s - 1
                    act.wait_ge(s_turned, t + 1)
                    if t >= 2:
                        act.wait_ge(s_down_done, t - 1)
                    act.activation(s_midT[:, t % 2, :, :], TP[0:HALF_I, 0, :].rearrange("p (c n) -> p c n", c=PIECES), ACT.Copy).then_inc(s_midT_done, 1)

            def x_turn(i, u):
                act.wait_ge(x_turned, at(i, RING, u + 1))
                if not (first(i) and u < 2):
                    act.wait_ge(up_done, at(i, RING, u - 1))
                act.activation(xgT[:, u % 2, :, :], TP[:, 0, 0:KT * P].rearrange("p (k c) -> p k c", k=KT), ACT.Copy).then_inc(xgT_done, 1)

            def up(i, u, ring):
                act.wait_ge(up_done, at(i, RING, u + 1))
                if not (first(i) and u < 2):
                    act.wait_ge(mixed, at(i, RING, u - 1))
                act.activation(e_act[:, ring % 2, :], S[:, ring, 0:INNER], ACT.Silu).then_inc(act_done, 1)

            def turn(i, u, ring):
                act.wait_ge(turned, at(i, RING, u + 1))
                if not (first(i) and u < 2):
                    act.wait_ge(down_done, at(i, RING, u - 1))
                act.activation(e_midT[:, ring % 2, :, :], TP[0:HALF_I, 1, 0:2 * P].rearrange("p (c n) -> p c n", c=2), ACT.Copy).then_inc(midT_done, 1)

            def steps(i, us):
                for u in us:
                    if in_range(i, u, 0):
                        x_turn(i, u)
                    for back, stage in ((1, up), (2, turn)):
                        if in_range(i, u, back):
                            stage(i, u - back, (u - back) % RING)

            steps(0, range(RING))
            with act.Fori(1, E // RING) as i:
                steps(i, range(RING))
            steps(E // RING, range(3))

        @block.vector
        def _(dve):
            done = [0]

            def routed_step(name, instruction):
                instruction.then_inc(route, 1)
                done[0] += 1
                assert ROUTE[name] == done[0]
                dve.wait_ge(route, done[0])

            dve.wait_ge(consts_in, 4 * 16)
            dve.tensor_copy(before16[:, :], before[:, :]).then_inc(consts_cast, 1)
            dve.memset(ones16[:, :], 1.0).then_inc(consts_cast, 1)
            dve.tensor_copy(lower16[:, :, :], lower[:, :].rearrange("p (a b) -> p a b", a=E)).then_inc(consts_cast, 1)
            logits = PV[:, 0:TILES * E].rearrange("p (t e) -> p t e", e=E)
            wide = [P, TILES, E]
            dve.wait_ge(logits_done, 1)
            routed_step("top", dve.tensor_reduce(top[:, :], logits, AX.X, ALU.max))
            dve.tensor_tensor(shifted[:, :, :], logits, top[:, :].unsqueeze(2).to_broadcast(wide), ALU.subtract).then_inc(shift_done, 1)
            dve.wait_ge(exps_done, 1)
            routed_step("total", dve.tensor_reduce(total[:, :], exps[:, :, :], AX.X, ALU.add))
            routed_step("total_inv", dve.reciprocal(total_inv[:, :], total[:, :]))
            routed_step("score", dve.tensor_tensor(score[:, :, :], exps[:, :, :], total_inv[:, :].unsqueeze(2).to_broadcast(wide), ALU.mult))

            def compare(part):
                others = score[:, :, :].unsqueeze(2).to_broadcast([P, TILES, E, E])
                mine = score[:, :, :].unsqueeze(3).to_broadcast([P, TILES, E, E])
                g, q = (x[:, :, :, :].rearrange("p t a b -> p t (a b)") for x in (greater, equal))
                if part == 0:
                    routed_step("greater", dve.tensor_tensor(greater[:, :, :, :], others, mine, ALU.is_gt))
                elif part == 1:
                    routed_step("equal", dve.tensor_tensor(equal[:, :, :, :], others, mine, ALU.is_equal))
                elif part == 2:
                    dve.wait_ge(consts_cast, 3)
                    routed_step("equal_lower", dve.tensor_tensor(q, q, lower16[:, :, :].rearrange("p a b -> p (a b)").unsqueeze(1).to_broadcast([P, TILES, E * E]), ALU.mult))
                    routed_step("greater_equal", dve.tensor_tensor(g, g, q, ALU.add))
                else:
                    routed_step("above", dve.tensor_reduce(above[:, :, :], greater[:, :, :, :], AX.X, ALU.add))
                    routed_step("chosen", dve.tensor_scalar(chosen[:, :, :], above[:, :, :], float(TOPK), None, ALU.is_lt))
                    routed_step("chosen16", dve.tensor_copy(chosen16[:, :, :], chosen[:, :, :]))

            def weigh():
                routed_step("gain_raw", dve.tensor_tensor(gain[:, :, :], score[:, :, :], chosen[:, :, :], ALU.mult))
                routed_step("gain_sum", dve.tensor_reduce(gain_sum[:, :], gain[:, :, :], AX.X, ALU.add))
                routed_step("gain_eps", dve.tensor_scalar(gain_sum[:, :], gain_sum[:, :], 1e-20, None, ALU.add))
                routed_step("gain_inv", dve.reciprocal(gain_inv[:, :], gain_sum[:, :]))
                routed_step("gain", dve.tensor_tensor(gain[:, :, :], gain[:, :, :], gain_inv[:, :].unsqueeze(2).to_broadcast(wide), ALU.mult))
                routed_step("high", dve.tensor_copy(info[:, :, :, 3], gain[:, :, :]))
                routed_step("high_rest", dve.tensor_tensor(rest[:, :, :], gain[:, :, :], info[:, :, :, 3], ALU.subtract))
                routed_step("middle", dve.tensor_copy(info[:, :, :, 4], rest[:, :, :]))
                routed_step("middle_rest", dve.tensor_tensor(rest[:, :, :], rest[:, :, :], info[:, :, :, 4], ALU.subtract))
                routed_step("low", dve.tensor_copy(info[:, :, :, 5], rest[:, :, :]))

            def place():
                routed_step("numbers", dve.tensor_copy(info[:, :, :, 0], where[:, 0, :].unsqueeze(2).to_broadcast(wide)))
                routed_step("tiles", dve.tensor_copy(info[:, :, :, 1], where[:, 1, :].unsqueeze(2).to_broadcast(wide)))
                routed_step("ones", dve.memset(info[:, :, :, 2], 1.0))
                routed_step("away", dve.tensor_scalar(rest[:, :, :], chosen[:, :, :], -NOWHERE, NOWHERE, ALU.mult, ALU.add))
                dve.wait_ge(rank_done, 1)
                routed_step("slot", dve.tensor_tensor(slot[:, :, :], logits, rest[:, :, :], ALU.add))

            def one_hot(e):
                if e >= 2:
                    dve.wait_ge(info_done, e - 1)
                dve.tensor_tensor(onehot[:, e % 2, :, :], iota[:, :].unsqueeze(1).to_broadcast([P, TILES, P]),
                                  slot[:, :, e].unsqueeze(2).to_broadcast([P, TILES, P]), ALU.is_equal).then_inc(onehot_done, 1)

            def s_silu_mul(t):
                u, b = S[:, (2 * t + 1) % 4, 0:INNER_S], t % 2
                dve.wait_ge(s_act_done, t + 1)
                if t >= 2:
                    dve.wait_ge(s_turned, t - 1)
                dve.tensor_tensor(s_mid[:, b, :], u, s_act[:, b, :], ALU.mult).then_inc(s_mixed, 1)

            def s_add(t):
                dve.wait_ge(s_down_done, t + 1)
                dve.tensor_tensor(Y[:, t, :], TP[:, 1 + t % 2, 0:D], Y[:, t, :], ALU.add).then_inc(s_added, 1)

            for s in range(TILES + 2):
                if s < TILES:
                    s_silu_mul(s)
                if s < 4:
                    compare(s)
                if s == 4:
                    weigh()
                if s == 5:
                    place()
                if 6 <= s < 6 + E // 2:
                    one_hot(2 * (s - 6))
                    one_hot(2 * (s - 6) + 1)
                if s >= 2:
                    s_add(s - 2)
            dve.wait_ge(info_done, E)
            routed_step("slots", dve.tensor_copy(slots[:, :, :], PV[:, 0:E * INFO].rearrange("p (e c) -> p e c", c=INFO)))
            routed_step("token_a", dve.scalar_tensor_tensor(out=token_a[:, :], in0=slots[:, :, 1], scalar=float(P), in1=slots[:, :, 0], op0=ALU.mult, op1=ALU.add))
            routed_step("token_b", dve.tensor_scalar(token_b[:, :], slots[:, :, 2], -NOWHERE, NOWHERE, ALU.mult, ALU.add))
            routed_step("token", dve.tensor_tensor(token[:, :], token_a[:, :], token_b[:, :], ALU.add))
            routed_step("gain_a", dve.tensor_tensor(slot_gain_a[:, :], slots[:, :, 5], slots[:, :, 4], ALU.add))
            routed_step("slot_gain", dve.tensor_tensor(slot_gain[:, :], slot_gain_a[:, :], slots[:, :, 3], ALU.add))

            def up(i, u, ring):
                up_, b = S[:, ring, INNER:2 * INNER], ring % 2
                dve.wait_ge(act_done, at(i, RING, u + 1))
                if not (first(i) and u < 2):
                    dve.wait_ge(turned, at(i, RING, u - 1))
                dve.tensor_tensor(e_mid[:, b, :], up_, e_act[:, b, :], ALU.mult).then_inc(mixed, 1)

            def down(i, u, ring):
                dve.wait_ge(down_done, at(i, RING, u + 1))
                if not (first(i) and u == 0):
                    dve.wait_ge(out_free, at(i, RING, u))
                dve.tensor_scalar(e_out[:, ring % 2, :], TP[:, 2, 0:D], slot_gain[:, bass.ds(RING * i + u, 1)], None, ALU.mult).then_inc(out_done, 1)

            def steps(i, us):
                for u in us:
                    for back, stage in ((1, up), (3, down)):
                        if in_range(i, u, back):
                            stage(i, u - back, (u - back) % RING)

            steps(0, range(RING))
            with dve.Fori(1, E // RING) as i:
                steps(i, range(RING))
            steps(E // RING, range(3))

        stage.close()
        afterwards(addend=(y_routed, y_in))



def build(nc, x, consts, wqkv0, wo0, ball_w, ball_scale, wq1, wkv1, wo1, gate_w, sw_gu, sw_down, w_gu, w_down, out):
    x_rows = nc.dram_tensor("x_rows", (T, D), F32).ap()
    routed = [nc.dram_tensor(f"routed{n}", (T, D), F32).ap() for n in range(2)]
    with ExitStack() as ctx:
        core = Core(nc, ctx, consts)
        with ExitStack() as split:
            xT_hi = split.enter_context(nc.sbuf_tensor("xT_hi", [P, KT, T], F32R))
            xT_lo = split.enter_context(nc.sbuf_tensor("xT_lo", [P, KT, T], F32R))
            rotary_attention(nc, core, consts, wqkv0, wo0, xT_hi, xT_lo,
                             partial(norm_stage, nc, core, "load", xT_hi=xT_hi, xT_lo=xT_lo, source=x, normalize=False))
            ball_projection(nc, core, ball_w, ball_scale, xT_hi, xT_lo,
                            partial(norm_stage, nc, core, "norm0", xT_hi=xT_hi, xT_lo=xT_lo))
            window_attention(nc, core, consts, wq1, wkv1, wo1, xT_hi, xT_lo,
                             partial(norm_stage, nc, core, "norm1", xT_hi=xT_hi, xT_lo=xT_lo))
        xT = ctx.enter_context(nc.sbuf_tensor("xT", [P, KT, T], F32))
        expert_mix(nc, core, consts, gate_w, sw_gu, sw_down, w_gu, w_down, xT, x_rows, routed,
                   partial(norm_stage, nc, core, "norm2", xT=xT, store=x_rows),
                   partial(norm_stage, nc, core, "norm3", store=out))



def _constants(np):
    p, e = np.arange(P), np.arange(E)
    c = np.zeros((P, CONSTS), np.float32)

    def put(name, a):
        c[:, CONST[name][0]:CONST[name][1]] = np.asarray(a, np.float32).reshape(P, -1)

    put("ident", np.eye(P))
    put("causal", np.where(p[None, :] > p[:, None], MASKED, 0.0))
    back = np.arange(2 * P)[None, :] - P - p[:, None]
    window = np.where((back <= 0) & (back > -WIN), 0.0, MASKED)
    put("window", np.concatenate([np.where(np.arange(2 * P)[None, :] >= P, window, MASKED), window], 1))
    fraction = np.float32(2.0) * np.arange(HALF, dtype=np.float32) / np.float32(HD)
    timescale = np.power(np.float32(10000.0), fraction).astype(np.float32)
    phase = (np.arange(T, dtype=np.float32)[:, None] / timescale[None, :]).astype(np.float32)
    cos, sin = np.cos(phase), np.sin(phase)
    put("cos", cos.reshape(TILES, P, HALF).transpose(1, 0, 2))
    put("sin", sin.reshape(TILES, P, HALF).transpose(1, 0, 2))
    put("iota", np.broadcast_to(p[None, :], (P, P)))
    put("before", p[:, None] < p[None, :])
    put("lower", np.broadcast_to((e[None, :] < e[:, None]).reshape(1, E * E), (P, E * E)))
    put("where", np.concatenate([np.broadcast_to(p[:, None], (P, TILES)), np.broadcast_to(np.arange(TILES)[None, :], (P, TILES))], 1))
    return c


def kernel(**inputs):
    import numpy as np
    import concourse.bacc as bacc
    from concourse.bass_utils import run_bass_kernel_spmd

    i = {k: np.asarray(v) for k, v in inputs.items()}
    turned = np.concatenate([np.arange(0, HD, 2), np.arange(1, HD, 2)])
    qkv0 = np.stack([i["L0_attn_wq"][:, :, turned], i["L0_attn_wk"][:, :, turned], i["L0_attn_wv"]], 2)
    kv1 = np.stack([i["L1_attn_Wk"].reshape(KT, P, HKV, HD), i["L1_attn_Wv"].reshape(KT, P, HKV, HD)], 3)
    arrays = {
        "x": i["L0_attn_x"].reshape(T, D),
        "consts": _constants(np),
        "wqkv0": qkv0.reshape(KT, P, H0, QKV).transpose(2, 1, 0, 3),
        "wo0": i["L0_attn_wo"],
        "ball_w": i["L0_ffn_weight"],
        "ball_scale": i["L0_ffn_scale"],
        "wq1": i["L1_attn_Wq"].reshape(KT, P, HKV, REP * HD).transpose(2, 1, 0, 3),
        "wkv1": kv1.transpose(2, 1, 0, 3, 4).reshape(HKV, P, KT, 2 * HD),
        "wo1": i["L1_attn_Wo"].reshape(HKV, REP, HD, D).transpose(0, 2, 1, 3),
        "gate_w": i["L1_ffn_gate_w"].T.reshape(KT, P, E).transpose(1, 0, 2),
        "sw_gu": np.concatenate([i["L1_ffn_sw_gate"], i["L1_ffn_sw_up"]], 1).reshape(KT, P, 2 * INNER_S).transpose(1, 0, 2),
        "sw_down": i["L1_ffn_sw_down"].reshape(2 * INNER_S // INNER, INNER // 2, D).transpose(1, 0, 2),
        "w_gu": np.concatenate([i["L1_ffn_w_gate"], i["L1_ffn_w_up"]], 2).reshape(E, KT, P, 2 * INNER).transpose(0, 2, 1, 3),
        "w_down": i["L1_ffn_w_down"].reshape(E, 2, INNER // 2, D).transpose(0, 2, 1, 3),
    }
    arrays = {f"in_{k}": np.ascontiguousarray(v) for k, v in arrays.items()}
    nc = bacc.Bacc("TRN2", target_bir_lowering=False, num_devices=1)
    args = [nc.dram_tensor(k, v.shape, mybir.dt.from_np(v.dtype), kind="ExternalInput").ap() for k, v in arrays.items()]
    out = nc.dram_tensor("out_0", (T, D), F32, kind="ExternalOutput").ap()
    build(nc, *args, out)
    r = run_bass_kernel_spmd(nc, [arrays], core_ids=[0])
    return r.results[0]["out_0"].reshape(1, T, D)
```
